# Optimizing a Trainium2 kernel written in Bass

```python
import numpy as np
import jax
import jax.numpy as jnp

def _softmax(x, axis=-1):
    return jax.nn.softmax(x, axis=axis)

def _gelu(x):
    return jax.nn.gelu(x, approximate=True)

def _silu(x):
    return jax.nn.silu(x)

def _sigmoid(x):
    return jax.nn.sigmoid(x)

def _layernorm(x, axis=-1, eps=1e-05):
    m = jnp.mean(x, axis=axis, keepdims=True)
    v = jnp.var(x, axis=axis, keepdims=True)
    return (x - m) / jnp.sqrt(v + eps)

def _scatter_add(tgt, idx, src, axis=0):
    return tgt.at[idx].add(src)

def _segment_sum(src, seg, n):
    return jax.ops.segment_sum(src, seg, n)
kernel_name = 'mk_gnn_ffn_d2_gnn_r8_84a425'

def setup_inputs(seed: int=0):
    np.random.seed(seed)
    _w = jnp.asarray

    def _rec_inputs():
        import jax
        import jax.numpy as jnp
        _gk = jax.random.key(seed)
        x = -0.0002117 + 1 * jax.random.normal(jax.random.fold_in(_gk, 1), (12500, 256), jnp.float32)
        src = jax.random.randint(jax.random.fold_in(_gk, 2), (200000,), 0, 12500, jnp.int32)
        dst = jax.random.randint(jax.random.fold_in(_gk, 3), (200000,), 0, 12500, jnp.int32)
        _o = jnp.argsort(dst, stable=True)
        src = src[_o]
        dst = dst[_o]
        edge_weight = jax.random.uniform(jax.random.fold_in(_gk, 13), (200000,), jnp.float32, 0.0, 1)
        return (x, src, dst, edge_weight)
    x, src, dst, edge_weight = _rec_inputs()

    def _L0_gnn_setup():
        import jax, jax.numpy as jnp
        import numpy as np
        N_NODES = 12500
        N_EDGES = 400000
        IN_FEATS = 256
        OUT_FEATS = 256
        key = jax.random.key(seed)
        k1, k2, k3, k4, k5, k6 = jax.random.split(key, 6)
        features = jax.random.normal(k1, (N_NODES, IN_FEATS), dtype=jnp.float32)
        edge_src = jax.random.randint(k2, (N_EDGES,), 0, N_NODES, dtype=jnp.int64)
        edge_dst = jnp.sort(jax.random.randint(k3, (N_EDGES,), 0, N_NODES, dtype=jnp.int64))
        edge_weight = jax.random.uniform(k4, (N_EDGES,), dtype=jnp.float32)
        bound = 1.0 / np.sqrt(IN_FEATS)
        W = jax.random.uniform(k5, (OUT_FEATS, IN_FEATS), dtype=jnp.float32, minval=-bound, maxval=bound)
        b = jax.random.uniform(k6, (OUT_FEATS,), dtype=jnp.float32, minval=-bound, maxval=bound)
        return {'features': features, 'edge_src': edge_src, 'edge_dst': edge_dst, 'edge_weight': edge_weight, 'W': W, 'b': b}
    _L0_gnn_all = _L0_gnn_setup()
    _L0_gnn_in = {k: v for k, v in _L0_gnn_all.items() if k in ('W', 'b')}
    del _L0_gnn_all

    def _L0_ffn_setup():
        import math
        import jax, jax.numpy as jnp
        import numpy as np
        CAPACITY_FACTOR = 1.25
        key = jax.random.key(seed)
        ks = jax.random.split(key, 5)
        B, L, D, F, E = (8, 1024, 256, 1024, 8)
        h = jax.random.normal(ks[0], (B, L, D), dtype=jnp.float32)
        gate_w = jax.random.normal(ks[1], (D, E), dtype=jnp.float32) * 0.02
        gate_b = jnp.zeros((E,), dtype=jnp.float32)
        w1 = jax.random.normal(ks[2], (E, D, F), dtype=jnp.float32) * (1.0 / math.sqrt(D))
        b1 = jnp.zeros((E, F), dtype=jnp.float32)
        w2 = jax.random.normal(ks[3], (E, F, D), dtype=jnp.float32) * (1.0 / math.sqrt(F))
        b2 = jnp.zeros((E, D), dtype=jnp.float32)
        return {'h': h, 'gate_w': gate_w, 'gate_b': gate_b, 'w1': w1, 'b1': b1, 'w2': w2, 'b2': b2}
    _L0_ffn_all = _L0_ffn_setup()
    _L0_ffn_in = {k: v for k, v in _L0_ffn_all.items() if k in ('gate_w', 'gate_b', 'w1', 'b1', 'w2', 'b2')}
    del _L0_ffn_all

    def _L1_gnn_setup():
        import jax, jax.numpy as jnp
        import numpy as np
        N = 12500
        NNZ = 400000
        IN_DIM = 256
        OUT_DIM = 256
        BN_EPS = 1e-05
        key = jax.random.key(seed)
        ks = jax.random.split(key, 6)
        x = jax.random.normal(ks[0], (N, IN_DIM), dtype=jnp.float32)
        A_indices = jax.random.randint(ks[1], (2, NNZ), 0, N, dtype=jnp.int64)
        A_values = jax.random.uniform(ks[2], (NNZ,), dtype=jnp.float32)
        W = jax.random.normal(ks[3], (IN_DIM, OUT_DIM), dtype=jnp.float32) / np.sqrt(IN_DIM)
        bias = jax.random.normal(ks[4], (OUT_DIM,), dtype=jnp.float32) * 0.02
        gamma = jnp.ones((OUT_DIM,), dtype=jnp.float32)
        beta = jnp.zeros((OUT_DIM,), dtype=jnp.float32)
        return {'x': x, 'A_indices': A_indices, 'A_values': A_values, 'A_shape': N, 'W': W, 'bias': bias, 'gamma': gamma, 'beta': beta}
    _L1_gnn_all = _L1_gnn_setup()
    _L1_gnn_in = {k: v for k, v in _L1_gnn_all.items() if k in ('W', 'bias', 'gamma', 'beta')}
    del _L1_gnn_all

    def _L1_ffn_setup():
        import jax, jax.numpy as jnp
        import numpy as np
        B, N, D = (16, 512, 256)
        NUM_EXPERTS, TOP_K, HEADS = (4, 2, 4)
        N_EDGES = 131072
        LN_EPS = 1e-05

        def _layernorm(x, g, b):
            mu = x.mean(-1, keepdims=True)
            var = ((x - mu) ** 2).mean(-1, keepdims=True)
            return (x - mu) * jax.lax.rsqrt(var + LN_EPS) * g + b

        def _forward(x, edge_index, W_gat, att_src, att_dst, b_gat, ln_gamma, ln_beta, W1, b1, W2, b2):
            Bc, Nc, Dc = x.shape
            M = Bc * Nc
            x_flat = x.reshape(M, Dc)
            h = (x_flat @ W_gat).reshape(M, HEADS, NUM_EXPERTS)
            loops = jnp.arange(M, dtype=edge_index.dtype)
            src = jnp.concatenate([edge_index[0], loops])
            dst = jnp.concatenate([edge_index[1], loops])
            a_src = (h * att_src).sum(-1)
            a_dst = (h * att_dst).sum(-1)
            e = jax.nn.leaky_relu(a_src[src] + a_dst[dst], negative_slope=0.2)
            e_max = jax.ops.segment_max(e, dst, num_segments=M)
            ee = jnp.exp(e - e_max[dst])
            denom = jax.ops.segment_sum(ee, dst, num_segments=M)
            alpha = ee / (denom[dst] + 1e-16)
            msg = h[src] * alpha[:, :, None]
            agg = jax.ops.segment_sum(msg, dst, num_segments=M).reshape(M, HEADS * NUM_EXPERTS) + b_gat
            scores = _layernorm(agg, ln_gamma, ln_beta).reshape(M, HEADS, NUM_EXPERTS).mean(1)
            scores = scores.reshape(Bc, Nc, NUM_EXPERTS)
            topk_s, topk_i = jax.lax.top_k(scores, TOP_K)
            w = jax.nn.softmax(topk_s, axis=-1)
            out = jnp.zeros_like(x)
            for ei in range(NUM_EXPERTS):
                g = jnp.where(topk_i == ei, w, 0.0).sum(-1)
                hh = jax.nn.gelu(x @ W1[ei] + b1[ei], approximate=False)
                out = out + g[..., None] * (hh @ W2[ei] + b2[ei])
            return out
        key = jax.random.key(seed)
        ks = jax.random.split(key, 8)
        s = 0.05
        return {'x': jax.random.normal(ks[0], (B, N, D), jnp.float32), 'W_gat': jax.random.normal(ks[1], (D, HEADS * NUM_EXPERTS), jnp.float32) * s, 'att_src': jax.random.normal(ks[2], (HEADS, NUM_EXPERTS), jnp.float32) * s, 'att_dst': jax.random.normal(ks[3], (HEADS, NUM_EXPERTS), jnp.float32) * s, 'b_gat': jnp.zeros((HEADS * NUM_EXPERTS,), jnp.float32), 'ln_gamma': jnp.ones((HEADS * NUM_EXPERTS,), jnp.float32), 'ln_beta': jnp.zeros((HEADS * NUM_EXPERTS,), jnp.float32), 'W1': jax.random.normal(ks[4], (NUM_EXPERTS, D, 2 * D), jnp.float32) * s, 'b1': jnp.zeros((NUM_EXPERTS, 2 * D), jnp.float32), 'W2': jax.random.normal(ks[5], (NUM_EXPERTS, 2 * D, D), jnp.float32) * s, 'b2': jnp.zeros((NUM_EXPERTS, D), jnp.float32), 'edge_index': jax.random.randint(ks[6], (2, N_EDGES), 0, B * N, jnp.int32)}
    _L1_ffn_all = _L1_ffn_setup()
    _L1_ffn_in = {k: v for k, v in _L1_ffn_all.items() if k in ('W_gat', 'att_src', 'att_dst', 'b_gat', 'ln_gamma', 'ln_beta', 'W1', 'b1', 'W2', 'b2', 'edge_index')}
    del _L1_ffn_all
    return {'x': x, 'src': src, 'dst': dst, 'edge_weight': edge_weight, 'L0_gnn_W': _L0_gnn_in['W'], 'L0_gnn_b': _L0_gnn_in['b'], 'L0_ffn_gate_w': _L0_ffn_in['gate_w'], 'L0_ffn_gate_b': _L0_ffn_in['gate_b'], 'L0_ffn_w1': _L0_ffn_in['w1'], 'L0_ffn_b1': _L0_ffn_in['b1'], 'L0_ffn_w2': _L0_ffn_in['w2'], 'L0_ffn_b2': _L0_ffn_in['b2'], 'L1_gnn_W': _L1_gnn_in['W'], 'L1_gnn_bias': _L1_gnn_in['bias'], 'L1_gnn_gamma': _L1_gnn_in['gamma'], 'L1_gnn_beta': _L1_gnn_in['beta'], 'L1_ffn_W_gat': _L1_ffn_in['W_gat'], 'L1_ffn_att_src': _L1_ffn_in['att_src'], 'L1_ffn_att_dst': _L1_ffn_in['att_dst'], 'L1_ffn_b_gat': _L1_ffn_in['b_gat'], 'L1_ffn_ln_gamma': _L1_ffn_in['ln_gamma'], 'L1_ffn_ln_beta': _L1_ffn_in['ln_beta'], 'L1_ffn_W1': _L1_ffn_in['W1'], 'L1_ffn_b1': _L1_ffn_in['b1'], 'L1_ffn_W2': _L1_ffn_in['W2'], 'L1_ffn_b2': _L1_ffn_in['b2'], 'L1_ffn_edge_index': _L1_ffn_in['edge_index']}

def reference(x, src, dst, edge_weight, L0_gnn_W, L0_gnn_b, L0_ffn_gate_w, L0_ffn_gate_b, L0_ffn_w1, L0_ffn_b1, L0_ffn_w2, L0_ffn_b2, L1_gnn_W, L1_gnn_bias, L1_gnn_gamma, L1_gnn_beta, L1_ffn_W_gat, L1_ffn_att_src, L1_ffn_att_dst, L1_ffn_b_gat, L1_ffn_ln_gamma, L1_ffn_ln_beta, L1_ffn_W1, L1_ffn_b1, L1_ffn_W2, L1_ffn_b2, L1_ffn_edge_index):
    import jax
    import jax.numpy as jnp

    def _L0_gnn_ref(features, edge_src, edge_dst, edge_weight, W, b):
        import jax, jax.numpy as jnp
        import numpy as np
        N_NODES = 12500
        N_EDGES = 400000
        IN_FEATS = 256
        OUT_FEATS = 256
        msgs = features[edge_src] * edge_weight[:, None]
        agg = jax.ops.segment_sum(msgs, edge_dst, num_segments=N_NODES, indices_are_sorted=True)
        return jnp.einsum('ni,oi->no', agg, W) + b

    def _L0_ffn_ref(h, gate_w, gate_b, w1, b1, w2, b2):
        import math
        import jax, jax.numpy as jnp
        import numpy as np
        CAPACITY_FACTOR = 1.25
        B, L, D = h.shape
        E = gate_w.shape[1]
        T = B * L
        C = max(1, math.ceil(CAPACITY_FACTOR * T / E))
        x = h.reshape(T, D)
        logits = x @ gate_w + gate_b
        probs = jax.nn.softmax(logits, axis=-1)
        idx = jnp.argmax(probs, axis=-1)
        prb = jnp.take_along_axis(probs, idx[:, None], axis=1)[:, 0]
        one_hot = jax.nn.one_hot(idx, E, dtype=jnp.float32)
        pos = (jnp.cumsum(one_hot, axis=0) * one_hot).sum(-1).astype(jnp.int32) - 1
        kept = pos < C
        pos_safe = jnp.where(kept, pos, C)
        buf = jnp.zeros((E, C, D), dtype=h.dtype).at[idx, pos_safe].set(x, mode='drop')
        hmid = jax.nn.relu(jnp.einsum('ecd,edf->ecf', buf, w1) + b1[:, None, :])
        ybuf = jnp.einsum('ecf,efd->ecd', hmid, w2) + b2[:, None, :]
        pos_g = jnp.minimum(pos, C - 1)
        y_tok = ybuf[idx, pos_g] * (prb * kept)[:, None]
        y = y_tok.reshape(B, L, D)
        y = jnp.nan_to_num(y, nan=0.0, posinf=10000.0, neginf=-10000.0)
        return y

    def _L1_gnn_ref(x, A_indices, A_values, A_shape, W, bias, gamma, beta):
        import jax, jax.numpy as jnp
        import numpy as np
        N = 12500
        NNZ = 400000
        IN_DIM = 256
        OUT_DIM = 256
        BN_EPS = 1e-05
        h = jnp.einsum('nd,df->nf', x, W)
        row, col = (A_indices[0], A_indices[1])
        gathered = A_values[:, None] * h[col]
        agg = jax.ops.segment_sum(gathered, row, num_segments=A_shape)
        h = agg + bias
        mean = jnp.mean(h, axis=0)
        var = jnp.mean(jnp.square(h - mean), axis=0)
        h = (h - mean) * jax.lax.rsqrt(var + BN_EPS) * gamma + beta
        return jax.nn.relu(h)

    def _L1_ffn_ref(x, W_gat, att_src, att_dst, b_gat, ln_gamma, ln_beta, W1, b1, W2, b2, edge_index):
        import jax, jax.numpy as jnp
        import numpy as np
        B, N, D = (16, 512, 256)
        NUM_EXPERTS, TOP_K, HEADS = (4, 2, 4)
        N_EDGES = 131072
        LN_EPS = 1e-05

        def _layernorm(x, g, b):
            mu = x.mean(-1, keepdims=True)
            var = ((x - mu) ** 2).mean(-1, keepdims=True)
            return (x - mu) * jax.lax.rsqrt(var + LN_EPS) * g + b

        def _forward(x, edge_index, W_gat, att_src, att_dst, b_gat, ln_gamma, ln_beta, W1, b1, W2, b2):
            Bc, Nc, Dc = x.shape
            M = Bc * Nc
            x_flat = x.reshape(M, Dc)
            h = (x_flat @ W_gat).reshape(M, HEADS, NUM_EXPERTS)
            loops = jnp.arange(M, dtype=edge_index.dtype)
            src = jnp.concatenate([edge_index[0], loops])
            dst = jnp.concatenate([edge_index[1], loops])
            a_src = (h * att_src).sum(-1)
            a_dst = (h * att_dst).sum(-1)
            e = jax.nn.leaky_relu(a_src[src] + a_dst[dst], negative_slope=0.2)
            e_max = jax.ops.segment_max(e, dst, num_segments=M)
            ee = jnp.exp(e - e_max[dst])
            denom = jax.ops.segment_sum(ee, dst, num_segments=M)
            alpha = ee / (denom[dst] + 1e-16)
            msg = h[src] * alpha[:, :, None]
            agg = jax.ops.segment_sum(msg, dst, num_segments=M).reshape(M, HEADS * NUM_EXPERTS) + b_gat
            scores = _layernorm(agg, ln_gamma, ln_beta).reshape(M, HEADS, NUM_EXPERTS).mean(1)
            scores = scores.reshape(Bc, Nc, NUM_EXPERTS)
            topk_s, topk_i = jax.lax.top_k(scores, TOP_K)
            w = jax.nn.softmax(topk_s, axis=-1)
            out = jnp.zeros_like(x)
            for ei in range(NUM_EXPERTS):
                g = jnp.where(topk_i == ei, w, 0.0).sum(-1)
                hh = jax.nn.gelu(x @ W1[ei] + b1[ei], approximate=False)
                out = out + g[..., None] * (hh @ W2[ei] + b2[ei])
            return out
        return _forward(x, edge_index, W_gat, att_src, att_dst, b_gat, ln_gamma, ln_beta, W1, b1, W2, b2)
    edge_index = jnp.stack([src, dst])
    x = x + _L0_gnn_ref(_layernorm(x, axis=-1), src, dst, edge_weight, L0_gnn_W, L0_gnn_b)
    x = x + _L0_ffn_ref(_layernorm(x, axis=-1)[None], L0_ffn_gate_w, L0_ffn_gate_b, L0_ffn_w1, L0_ffn_b1, L0_ffn_w2, L0_ffn_b2)[0]
    x = x + _L1_gnn_ref(_layernorm(x, axis=-1), edge_index, edge_weight, 12500, L1_gnn_W, L1_gnn_bias, L1_gnn_gamma, L1_gnn_beta)
    x = x + _L1_ffn_ref(_layernorm(x, axis=-1)[None], L1_ffn_W_gat, L1_ffn_att_src, L1_ffn_att_dst, L1_ffn_b_gat, L1_ffn_ln_gamma, L1_ffn_ln_beta, L1_ffn_W1, L1_ffn_b1, L1_ffn_W2, L1_ffn_b2, L1_ffn_edge_index)[0]
    return x

_drawn_inputs = setup_inputs


def setup_inputs(seed=0):
    import zlib

    import numpy as np

    out = dict(_drawn_inputs(seed))
    spreads = {'L0_ffn_gate_b': (0.0, 0.1),
     'L0_ffn_b1': (0.0, 0.508),
     'L0_ffn_b2': (0.0, 0.421),
     'L1_gnn_gamma': (1.0, 0.2),
     'L1_gnn_beta': (0.0, 0.1),
     'L1_ffn_b_gat': (0.0, 0.1),
     'L1_ffn_ln_gamma': (1.0, 0.2),
     'L1_ffn_ln_beta': (0.0, 0.1),
     'L1_ffn_b1': (0.0, 0.1),
     'L1_ffn_b2': (0.0, 0.1)}
    factors = {'L1_gnn_bias': 64.0, 'L1_ffn_att_dst': 9.001}
    for name, (base, spread) in spreads.items():
        noise = np.random.default_rng([zlib.crc32(name.encode()), seed]).standard_normal(out[name].shape)
        drawn = base * np.exp(spread * noise) if base else spread * noise
        out[name] = jnp.asarray(drawn.astype(out[name].dtype))
    for name, factor in factors.items():
        out[name] = (out[name] * factor).astype(out[name].dtype)
    return out
```

```python
import concourse.bass as bass
from concourse import mybir
from contextlib import ExitStack
from collections import namedtuple

F32, I32, BF16, U16 = mybir.dt.float32, mybir.dt.int32, mybir.dt.bfloat16, mybir.dt.uint16
ALU, ACT, AX = mybir.AluOpType, mybir.ActivationFunctionType, mybir.AxisListType

P = 128
N, D = 12500, 256
TILES = -(-N // P)
NPAD = TILES * P
BUCKETS = TILES + 1
GROUP = 7
GROUPS = TILES // GROUP
EDGES, GEDGES = 200000, 131072
LANES = 16
HALF = LANES // 2
BANKS, RING = 8, 4
ECH = -(-(-(-EDGES // P)) // LANES) * LANES
GCH = GEDGES // P
EROWS = -(-ECH // P) * P
EPAIRS = -(-(-(-EDGES // P) + TILES) // LANES) * LANES
GPAIRS = -(-(GCH + TILES) // LANES) * LANES
EBLK, GBLK = -(-EPAIRS // P), -(-GPAIRS // P)
EXPERTS, CAP, HID = 8, -(-5 * N // (4 * 8)), 1024
SLOTS = 2048
GEXP, GHID, HEADS = 4, 512, 4
LN_EPS = BN_EPS = 1e-5


Plan = namedtuple("Plan", "pairs blocks chunks tiles chunk shift")
Fields = namedtuple("Fields", "rows fields")
Pairs = namedtuple("Pairs", "row place weight tile")
Product = namedtuple("Product", "kind sums w bias")
Routed = namedtuple("Routed", "kind table rows scale")
Normed = namedtuple("Normed", "kind sums gain offset")


class Kept:
    pass


class Stage:

    def __init__(self, nc):
        self.nc, self.ctx, self.sems = nc, ExitStack(), []

    def sb(self, name, shape, dt):
        return self.ctx.enter_context(self.nc.sbuf_tensor(f"{name}_{self.nc.next_id()}", shape, dt))

    def ps(self, name, shape, dt=F32):
        return self.ctx.enter_context(self.nc.psum_tensor(f"{name}_{self.nc.next_id()}", shape, dt))

    def sem(self, name):
        s = self.nc.alloc_semaphore(f"{name}_{self.nc.next_id()}")
        self.sems.append(s)
        return s

    def __enter__(self):
        return self

    def __exit__(self, *exc):
        if exc[0] is None:
            self.nc.clear_and_free_semaphores(self.sems)
            self.nc.all_engine_barrier()
        self.ctx.close()


class Chain:

    def __init__(self, eng, sem, base=0, once=None):
        self.eng, self.sem, self.base, self.n, self.once = eng, sem, base, 0, once

    def __call__(self, *instructions):
        for ins in instructions:
            ins.then_inc(self.sem, 1)
        self.n += len(instructions)
        if self.once is None:
            self.eng.wait_ge(self.sem, self.base + self.n)
        else:
            hold(self.eng, self.once, self.sem, self.base + self.n)


def hold(eng, once, sem, value):
    reg = eng.to_reg(value)
    eng.wait_ge(once, 1)
    eng.wait_ge(sem, reg)


def load_tiles(nc, eng, q, first, regs):
    eng.reg_load(regs, q.tile[0:1, bass.ds(first, len(regs))])
    return [nc.s_assert_within(eng.snap(r), 0, BUCKETS - 1, skip_runtime_bounds_check_because="a tile counts buckets begun before a pair, of which the first is left out")
            for r in regs]


def bc(ap, n, axis=2):
    a = ap.unsqueeze(axis)
    shape = list(a.shape)
    shape[axis] = n
    return a.to_broadcast(shape)


def constants(nc, k):
    with Stage(nc) as s, nc.Block() as block:
        done = s.sem("constants_done")

        @block.gpsimd
        def _(pool):
            n = [0]

            def link(ins):
                n[0] += 1
                ins.then_inc(done, 1)
                pool.wait_ge(done, n[0])

            link(nc.gpsimd.iota(k.iota_i[:, :], pattern=[[1, P]], base=0, channel_multiplier=0))
            link(nc.gpsimd.tensor_copy(k.iota[:, :], k.iota_i[:, :]))
            link(nc.gpsimd.memset(k.ones[:, :], 1.0))
            link(nc.gpsimd.memset(k.ident[:, :], 0.0))
            link(nc.gpsimd.affine_select(out=k.ident[:, :], in_=k.ident[:, :], compare_op=ALU.not_equal, fill=1.0,
                                         base=0, pattern=[[-1, P]], channel_multiplier=1))
            link(nc.gpsimd.affine_select(out=k.before[:, :], in_=k.ones[:, :], compare_op=ALU.is_gt, fill=0.0,
                                         base=0, pattern=[[1, P]], channel_multiplier=-1))
            link(nc.gpsimd.iota(k.qcol_i[:, :], pattern=[[P, EBLK]], base=0, channel_multiplier=1))
            link(nc.gpsimd.tensor_copy(k.qcol[:, :], k.qcol_i[:, :]))
            link(nc.gpsimd.tensor_copy(k.ident_bf[:, :], k.ident[:, :]))
            link(nc.gpsimd.memset(k.eps[:, :], LN_EPS))
            nc.gpsimd.memset(k.zero[:, :], 0.0).then_inc(done, 1)


def layer_norm_in(nc, k, x, f):
    xv = x.rearrange("(g j p) d -> g p j d", j=GROUP, p=P)
    fv = f[0:NPAD, :].rearrange("(g j p) d -> g p j d", j=GROUP, p=P)
    with Stage(nc) as s:
        xin = [s.sb(f"xin{h}", [P, GROUP, D], F32) for h in range(2)]
        fout = [s.sb(f"fout{h}", [P, GROUP, D], F32) for h in range(2)]
        stats, mv = s.sb("stats", [P, GROUP, 6], F32), s.sb("mv", [P, GROUP, 2], F32)
        std, rstd = s.sb("std", [P, GROUP], F32), s.sb("rstd", [P, GROUP], F32)
        loaded = [s.sem(f"loaded{h}") for h in range(2)]
        stored = [s.sem(f"stored{h}") for h in range(2)]
        normed, chain, var_done, std_done, zeros = (s.sem(n) for n in ("normed", "chain", "var_done", "std_done", "zeros"))
        PER = 2 * (3 * GROUP + 1)
        with nc.Block() as block:
            @block.sync
            def _(sp):
                sp.dma_start(f[NPAD:NPAD + P, :], k.zero[:, :]).then_inc(zeros, 16)
                sp.sem_inc(normed, 2)
                with sp.Fori(0, GROUPS // 2) as i:
                    for h in range(2):
                        hold(sp, normed, normed, i * 2 + h + 1)
                        sp.dma_start(xin[h][:, :, :], xv[bass.ds(i * 2 + h, 1), :, :, :].rearrange("o p j d -> (o p) j d")).then_inc(loaded[h], 16)

            @block.vector
            def _(dve):
                def turn(i, again):
                    link = Chain(dve, chain, i * PER, normed)
                    for h in range(2):
                        hold(dve, normed, loaded[h], i * 16 + 16)
                        for j in range(GROUP):
                            link(nc.vector.bn_stats(stats[:, j, :], xin[h][:, j, :]))
                            link(nc.vector.bn_aggr(mv[:, j, :], stats[:, j, :]))
                        dve.sem_inc(var_done, 1)
                        dve.wait_ge(std_done, i * 2 + h + 1)
                        link(nc.vector.reciprocal(rstd[:, :], std[:, :]))
                        if again:
                            hold(dve, normed, stored[h], i * 16)
                        for j in range(GROUP):
                            link(nc.vector.tensor_scalar(fout[h][:, j, :], xin[h][:, j, :], mv[:, j, 0:1], rstd[:, j:j + 1], ALU.subtract, ALU.mult))
                        dve.sem_inc(normed, 1)
                    assert link.n == PER

                turn(0, False)
                with dve.Fori(1, GROUPS // 2) as i:
                    turn(i, True)

            @block.scalar
            def _(act):
                act.wait_ge(zeros, 16)
                with act.Fori(0, GROUPS // 2) as i:
                    for h in range(2):
                        act.wait_ge(var_done, i * 2 + h + 1)
                        nc.scalar.activation(std[:, :], mv[:, :, 1], ACT.Sqrt, bias=k.eps[:, :]).then_inc(std_done, 1)
                        hold(act, normed, normed, i * 2 + h + 3)
                        act.dma_start(fv[bass.ds(i * 2 + h, 1), :, :, :].rearrange("o p j d -> (o p) j d"), fout[h][:, :, :]).then_inc(stored[h], 16)
                for h in range(2):
                    act.wait_ge(stored[h], GROUPS // 2 * 16)


def edge_tables(nc, k, a, plans, sorted_e, sorted_g):
    with Stage(nc) as s:
        rec_e, rec_g = s.sb("rec_e", [P, ECH, 4], F32), s.sb("rec_g", [P, GCH, 2], F32)
        pos_e, pos_g = s.sb("pos_e", [P, ECH], I32), s.sb("pos_g", [P, GCH], I32)
        edge_ranks(nc, k, a, plans, rec_e, rec_g, pos_e, pos_g)
        scatter_records(nc, rec_e, pos_e, sorted_e, ECH, 4)
        scatter_records(nc, rec_g, pos_g, sorted_g, GCH, 2)


def edge_ranks(nc, k, a, plans, rec_e, rec_g, pos_e, pos_g):
    B = BUCKETS
    with Stage(nc) as s:
        fields = [(a["dst"], rec_e, 0, ECH), (a["src"], rec_e, 1, ECH), (a["w"], rec_e, 2, ECH),
                  (a["gsrc"], rec_g, 0, GCH), (a["gdst"], rec_g, 1, GCH)]
        raw = [s.sb(f"raw{n}", [P, -(-c // P), P], src.tensor.dtype if n == 2 else I32) for n, (src, _, _, c) in enumerate(fields)]
        asf = s.sb("asf", [P, EROWS], F32)
        key_i = s.sb("key_i", [P, ECH], I32)
        keys = [s.sb("key_a", [P, ECH], BF16), s.sb("key_e", [P, ECH], BF16), s.sb("key_g", [P, GCH], BF16)]
        hit = s.sb("hit", [P, ECH], BF16)
        mask = s.sb("mask", [P, ECH], U16)
        posf = s.sb("posf", [P, ECH], F32)
        cnt = s.sb("cnt", [P, 3, B], F32)
        prior = s.sb("prior", [P, 3, B], F32)
        tot, start, first, last, pairs, begin, rel, drel = (s.sb(n, [P, 3, B], F32) for n in ("tot", "start", "first", "last", "pairs", "begin", "rel", "drel"))
        whole = s.sb("whole", [P, 3, B], I32)
        sel = s.sb("sel", [P, B], F32)
        tcol, ccol = s.sb("tcol", [P, 3, EBLK], F32), s.sb("ccol", [P, 3, EBLK], F32)
        tint = s.sb("tint", [P, 3, EBLK], I32)
        turned = [s.ps(f"turned{n}", [P, P]) for n in range(2)]
        ranks = s.ps("ranks", [P, 4 * 512])
        sums = s.ps("sums", [P, 3 * B])
        loaded = [s.sem(f"loaded{n}") for n in range(len(fields))]
        converted, transposed, copied, chain, counted, summed, stored = (s.sem(n) for n in (
            "converted", "transposed", "copied", "chain", "counted", "summed", "stored"))
        steps = [(n, b) for n, (_, _, _, c) in enumerate(fields) for b in range(-(-c // P))]
        with nc.Block() as block:
            @block.sync
            def _(sp):
                for n, (src, _, _, c) in enumerate(fields):
                    nb = -(-c // P)
                    sp.dma_start(raw[n][:, :, :], src[0:nb * P, :].rearrange("(b p) e -> p b e", p=P)).then_inc(loaded[n], 16)
                sp.wait_ge(chain, 1)
                sp.wait_ge(stored, 1)
                for n in range(3):
                    sp.dma_start(plans[n].tiles.rearrange("(b p) -> p b", p=P), tint[:, n, 0:plans[n].blocks],
                                 allow_slow_non_contiguous=True).then_inc(stored, 16)
                sp.wait_ge(stored, 49)

            @block.tensor
            def _(pe):
                for i, (n, b) in enumerate(steps):
                    c = min(P, fields[n][3] - b * P)
                    pe.wait_ge(converted, n + 1)
                    if i >= 2:
                        pe.wait_ge(copied, i - 1)
                    nc.tensor.transpose(turned[i % 2][:, 0:c], asf[0:c, b * P:(b + 1) * P], k.ident[0:c, 0:c]).then_inc(transposed, 1)
                pe.wait_ge(counted, 1)
                flat = cnt[:, :, :].rearrange("p n b -> p (n b)")
                nc.tensor.matmul(sums[:, :], k.ones[:, :], flat, start=True, stop=True).then_inc(summed, 1)
                pe.wait_ge(counted, 2)
                nc.tensor.matmul(sums[:, :], k.before[:, :], flat, start=True, stop=True).then_inc(summed, 1)

            @block.vector
            def _(dve):
                link = Chain(dve, chain)
                i = 0
                for n, (_, rec, f, c) in enumerate(fields):
                    nb = -(-c // P)
                    dve.wait_ge(loaded[n], 16)
                    if i:
                        dve.wait_ge(transposed, i)
                    nc.vector.tensor_copy(asf[:, 0:nb * P], raw[n][:, :, :].rearrange("p b e -> p (b e)")).then_inc(converted, 1)
                    for b in range(nb):
                        m = min(P, c - b * P)
                        dve.wait_ge(transposed, i + 1)
                        nc.vector.tensor_copy(rec[:, b * P:b * P + m, f], turned[i % 2][:, 0:m]).then_inc(copied, 1)
                        i += 1
                dve.wait_ge(copied, i)
                link(nc.vector.memset(rec_e[:, :, 3], 0.0))
                for key, src, c in ((keys[0], rec_e[:, :, 0], ECH), (keys[1], rec_e[:, :, 1], ECH), (keys[2], rec_g[:, :, 1], GCH)):
                    link(nc.vector.tensor_copy(key_i[:, 0:c], src))
                    link(nc.vector.tensor_scalar(key_i[:, 0:c], key_i[:, 0:c], 7, None, ALU.arith_shift_right))
                    link(nc.vector.tensor_copy(key[:, :], key_i[:, 0:c]))
                at = link.n
                with dve.Fori(0, B) as b:
                    turn = Chain(dve, chain, b * 3 + at, converted)
                    for n, key in enumerate(keys):
                        c = (ECH, ECH, GCH)[n]
                        turn(nc.vector.tensor_scalar(hit[:, 0:c], key[:, :], k.iota[:, bass.ds(b, 1)], None, ALU.is_equal, ALU.add,
                                                     accum_out=cnt[:, n, bass.ds(b, 1)]))
                link.n = at + 3 * B
                dve.sem_inc(counted, 1)
                dve.wait_ge(summed, 1)
                link(nc.vector.tensor_copy(tot[:, :, :].rearrange("p n b -> p (n b)"), sums[:, :]))
                dve.sem_inc(counted, 1)
                dve.wait_ge(summed, 2)
                link(nc.vector.tensor_copy(prior[:, :, :].rearrange("p n b -> p (n b)"), sums[:, :]))
                for n in range(3):
                    link(nc.vector.tensor_tensor_scan(start[:, n, :], tot[:, n, :], tot[:, n, :], 0.0, ALU.add, ALU.bypass))
                link(nc.vector.tensor_tensor(start[:, :, :], start[:, :, :], tot[:, :, :], ALU.subtract))
                link(nc.vector.tensor_copy(whole[:, :, :], start[:, :, :]))
                link(nc.vector.tensor_scalar(whole[:, :, :], whole[:, :, :], 7, None, ALU.arith_shift_right))
                link(nc.vector.tensor_copy(first[:, :, :], whole[:, :, :]))
                link(nc.vector.tensor_tensor(last[:, :, :], start[:, :, :], tot[:, :, :], ALU.add))
                link(nc.vector.tensor_scalar(whole[:, :, :], last[:, :, :], -1.0, None, ALU.add))
                link(nc.vector.tensor_scalar(whole[:, :, :], whole[:, :, :], 7, None, ALU.arith_shift_right))
                link(nc.vector.tensor_copy(last[:, :, :], whole[:, :, :]))
                link(nc.vector.tensor_tensor(last[:, :, :], last[:, :, :], first[:, :, :], ALU.subtract))
                link(nc.vector.tensor_scalar(pairs[:, :, :], tot[:, :, :], 0.0, None, ALU.is_gt))
                link(nc.vector.scalar_tensor_tensor(pairs[:, :, :], last[:, :, :], 1.0, pairs[:, :, :], ALU.add, ALU.mult))
                for n in range(3):
                    link(nc.vector.tensor_tensor_scan(begin[:, n, :], pairs[:, n, :], pairs[:, n, :], 0.0, ALU.add, ALU.bypass))
                link(nc.vector.tensor_tensor(begin[:, :, :], begin[:, :, :], pairs[:, :, :], ALU.subtract))
                link(nc.vector.tensor_tensor(rel[:, :, :], first[:, :, :], begin[:, :, :], ALU.subtract))
                link(nc.vector.tensor_copy(drel[:, :, 0:1], rel[:, :, 0:1]))
                link(nc.vector.tensor_tensor(drel[:, :, 1:B], rel[:, :, 1:B], rel[:, :, 0:B - 1], ALU.subtract))
                for n in range(3):
                    for q in range(plans[n].blocks):
                        link(nc.vector.tensor_scalar(sel[:, 1:B], begin[:, n, 1:B], k.qcol[:, q:q + 1], None, ALU.is_le, ALU.add,
                                                     accum_out=tcol[:, n, q:q + 1]))
                        link(nc.vector.scalar_tensor_tensor(sel[:, :], begin[:, n, :], k.qcol[:, q:q + 1], drel[:, n, :], ALU.is_le, ALU.mult,
                                                            accum_out=ccol[:, n, q:q + 1]))
                    m = plans[n].blocks
                    link(nc.vector.tensor_tensor(ccol[:, n, 0:m], ccol[:, n, 0:m], k.qcol[:, 0:m], ALU.add))
                    link(nc.vector.tensor_scalar(plans[n].chunk[:, 0:m], ccol[:, n, 0:m], float(plans[n].chunks - 1), None, ALU.min))
                    link(nc.vector.tensor_scalar(plans[n].shift[:, 0:m], tcol[:, n, 0:m], float(P), None, ALU.mult))
                    link(nc.vector.tensor_copy(tint[:, n, 0:m], tcol[:, n, 0:m]))
                dve.sem_inc(stored, 1)
                link(nc.vector.scalar_tensor_tensor(prior[:, :, :], start[:, :, :], -1.0, prior[:, :, :], ALU.add, ALU.add))
                for n, pos, c in ((1, pos_e, ECH), (2, pos_g, GCH)):
                    at = link.n
                    with dve.Fori(0, B) as b:
                        turn = Chain(dve, chain, b * 3 + at, converted)
                        turn(nc.vector.tensor_scalar(mask[:, 0:c], keys[n][:, :], k.iota[:, bass.ds(b, 1)], None, ALU.is_equal))
                        turn(nc.vector.tensor_tensor_scan(ranks[:, 0:c], mask[:, 0:c], mask[:, 0:c], prior[:, n, bass.ds(b, 1)], ALU.add, ALU.bypass))
                        turn(nc.vector.copy_predicated(posf[:, 0:c], mask[:, 0:c], ranks[:, 0:c]))
                    link.n = at + 3 * B
                    link(nc.vector.tensor_copy(pos[:, :], posf[:, 0:c]))


def scatter_records(nc, rec, pos, dest, chunks, width):
    turns = chunks // LANES
    with Stage(nc) as s:
        idx = s.sb("idx", [P, LANES], I32)
        pay = s.sb("pay", [P, LANES, width], F32)
        staged, ready = s.sem("staged"), s.sem("ready")
        landed = [s.sem(f"landed{h}") for h in range(2)]
        with nc.Block() as block:
            @block.gpsimd
            def _(pool):
                pool.sem_inc(ready, 1)

                def turn(i, again):
                    for h in range(2):
                        lo = slice(h * HALF, (h + 1) * HALF)
                        if again:
                            hold(pool, ready, landed[h], i * (16 * HALF))
                        nc.gpsimd.tensor_copy(idx[:, lo], pos[:, bass.ds(i * LANES + h * HALF, HALF)]).then_inc(staged, 1)
                        nc.gpsimd.tensor_copy(pay[:, lo, :], rec[:, bass.ds(i * LANES + h * HALF, HALF), :]).then_inc(staged, 1)
                        hold(pool, ready, staged, i * 4 + 2 * h + 2)
                        for u in range(h * HALF, (h + 1) * HALF):
                            pool.indirect_dma_start(out=dest, out_offset=bass.IndirectOffsetOnAxis(ap=idx[:, u:u + 1], axis=0),
                                                    in_=pay[:, u, :], in_offset=None).then_inc(landed[h], 16)

                turn(0, False)
                with pool.Fori(1, turns) as i:
                    turn(i, True)
                for h in range(2):
                    pool.wait_ge(landed[h], 16 * HALF * turns)


def pair_arrays(nc, k, plan, q, sources):
    with Stage(nc) as s:
        nb = plan.blocks
        got = [s.sb(f"got{n}", [P, nb, r.shape[1]], r.tensor.dtype) for n, r in enumerate(sources.rows)]
        asf = s.sb("asf", [P, 2, 3, P], F32)
        turned = [s.ps(f"turned{n}", [P, 3, P]) for n in range(2)]
        gathered, made, transposed, copied, tiles = (s.sem(n) for n in ("gathered", "made", "transposed", "copied", "tiles"))
        nf = len(sources.fields)
        with nc.Block() as block:
            @block.gpsimd
            def _(pool):
                for b in range(nb):
                    for n, r in enumerate(sources.rows):
                        pool.indirect_dma_start(out=got[n][:, b, :], out_offset=None, in_=r,
                                                in_offset=bass.IndirectOffsetOnAxis(ap=plan.chunk[:, b:b + 1], axis=0)).then_inc(gathered, 16)

            @block.sync
            def _(sp):
                sp.dma_start(q.tile[0:1, 0:nb * P], plan.tiles.unsqueeze(0)).then_inc(tiles, 16)
                sp.wait_ge(tiles, 16)

            @block.vector
            def _(dve):
                dve.wait_ge(gathered, 16 * nb * len(sources.rows))
                for b in range(nb):
                    if b >= 2:
                        dve.wait_ge(transposed, nf * (b - 1))
                    for f, (n, first, step) in enumerate(sources.fields):
                        src = got[n][:, b, first:first + (P - 1) * step + 1:step]
                        if f == 0:
                            ins = nc.vector.tensor_scalar(asf[:, b % 2, f, :], src, plan.shift[:, b:b + 1], None, ALU.subtract)
                        else:
                            ins = nc.vector.tensor_copy(asf[:, b % 2, f, :], src)
                        ins.then_inc(made, 1)
                    dve.wait_ge(transposed, nf * (b + 1))
                    for f, dest in enumerate((q.place, q.row, q.weight)[:nf]):
                        nc.vector.tensor_copy(dest[:, b * P:(b + 1) * P], turned[b % 2][:, f, :]).then_inc(copied, 1)

            @block.tensor
            def _(pe):
                for b in range(nb):
                    if b >= 2:
                        pe.wait_ge(copied, nf * (b - 1))
                    for f in range(nf):
                        pe.wait_ge(made, nf * b + f + 1)
                        nc.tensor.transpose(turned[b % 2][:, f, :], asf[:, b % 2, f, :], k.ident[:, :]).then_inc(transposed, 1)


def aggregate_edges(nc, k, table, q, agg):
    turns = EPAIRS // (RING * BANKS)
    SPAN = RING * BANKS
    with Stage(nc) as s:
        idx = s.sb("idx", [P, SPAN], I32)
        rows = s.sb("rows", [P, SPAN, D], F32)
        spread = s.sb("spread", [P, 2 * BANKS, P], F32)
        part = s.ps("part", [P, BANKS, 512])
        gathered = [s.sem(f"gathered{u}") for u in range(SPAN)]
        ready, staged, spread_done, multiplied, added = (s.sem(n) for n in ("ready", "staged", "spread_done", "multiplied", "added"))
        with nc.Block() as block:
            @block.gpsimd
            def _(pool):
                pool.wait_ge(ready, 1)
                with pool.Fori(0, turns) as i:
                    for r in range(RING):
                        hold(pool, ready, multiplied, (i * RING + r + 1) * BANKS)
                        nc.gpsimd.tensor_copy(idx[:, r * BANKS:(r + 1) * BANKS], q.row[:, bass.ds((i * RING + r) * BANKS, BANKS)]).then_inc(staged, 1)
                        hold(pool, ready, staged, i * RING + r + 1)
                        for u in range(r * BANKS, (r + 1) * BANKS):
                            pool.indirect_dma_start(out=rows[:, u, :], out_offset=None, in_=table,
                                                    in_offset=bass.IndirectOffsetOnAxis(ap=idx[:, u:u + 1], axis=0)).then_inc(gathered[u], 16)

            @block.vector
            def _(dve):
                def spread_weights(g, h):
                    for u in range(BANKS):
                        nc.vector.tensor_scalar(spread[:, h * BANKS + u, :], k.iota[:, :], q.place[:, bass.ds(g * BANKS + u, 1)],
                                                q.weight[:, bass.ds(g * BANKS + u, 1)], ALU.is_equal, ALU.mult).then_inc(spread_done, 1)

                regs = [dve.alloc_register(f"tile{n}_{nc.next_id()}") for n in range(4)]

                def add(g):
                    for u in range(BANKS):
                        if u % 4 == 0:
                            tiles = load_tiles(nc, dve, q, g * BANKS + u, regs)
                            hold(dve, ready, multiplied, (g + RING) * BANKS + u + 4)
                        sum_t = agg[:, bass.ds(tiles[u % 4], 1), :].rearrange("p o d -> p (o d)")
                        dve.wait_ge(added, (g + 1) * BANKS + u)
                        nc.vector.tensor_tensor(sum_t, sum_t, part[:, u, 0:D], ALU.add).then_inc(added, 1)

                nc.vector.memset(agg[:, :, :], 0.0).then_inc(ready, 1)
                dve.wait_ge(ready, 1)
                dve.sem_inc(added, BANKS)
                spread_weights(0, 0)
                with dve.Fori(0, EPAIRS // (2 * BANKS) - 1) as i:
                    for h in range(2):
                        spread_weights(i * 2 + h + 1, 1 - h)
                        add(i * 2 + h)
                last = EPAIRS // BANKS - 1
                spread_weights(last, 1)
                add(last - 1)
                add(last)

            @block.tensor
            def _(pe):
                pe.wait_ge(ready, 1)
                pe.sem_inc(multiplied, RING * BANKS)
                with pe.Fori(0, turns) as i:
                    for u in range(SPAN):
                        pe.wait_ge(spread_done, i * SPAN + u + 1)
                        pe.wait_ge(added, i * SPAN + u + 1)
                        pe.wait_ge(gathered[u], i * 16 + 16)
                        nc.tensor.matmul(part[:, u % BANKS, 0:D], spread[:, u % (2 * BANKS), :], rows[:, u, :], start=True, stop=True).then_inc(multiplied, 1)


def turn_weights(nc, k, pairs):
    with Stage(nc) as s:
        nat = s.sb("nat", [P, 2, D], F32)
        turned = [s.ps(f"turned{n}", [P, P]) for n in range(2)]
        loaded, transposed, copied = s.sem("loaded"), s.sem("transposed"), s.sem("copied")
        with nc.Block() as block:
            @block.sync
            def _(sp):
                for n, (w, _) in enumerate(pairs):
                    if n:
                        sp.wait_ge(transposed, 4 * n)
                    sp.dma_start(nat[:, :, :], w.rearrange("(c p) i -> p c i", p=P)).then_inc(loaded, 16)

            @block.tensor
            def _(pe):
                for m in range(4 * len(pairs)):
                    c, i = m % 4 // 2, m % 2
                    pe.wait_ge(loaded, 16 * (m // 4 + 1))
                    if m >= 2:
                        pe.wait_ge(copied, m - 1)
                    nc.tensor.transpose(turned[m % 2][:, :], nat[:, c, i * P:(i + 1) * P], k.ident[:, :]).then_inc(transposed, 1)

            @block.vector
            def _(dve):
                for m in range(4 * len(pairs)):
                    c, i = m % 4 // 2, m % 2
                    dve.wait_ge(transposed, m + 1)
                    nc.vector.tensor_copy(pairs[m // 4][1][:, i, c * P:(c + 1) * P], turned[m % 2][:, :]).then_inc(copied, 1)


def load_small(nc, k, loads):
    with Stage(nc) as s, nc.Block() as block:
        loaded = s.sem("loaded")

        @block.sync
        def _(sp):
            for sbuf, dram in loads:
                sp.dma_start(sbuf, dram).then_inc(loaded, 16)
            sp.wait_ge(loaded, 16 * len(loads))


def update_nodes(nc, k, head, x_old, x_new, f_new, w, width, bias, result):
    rows = lambda v: v[0:NPAD, :].rearrange("(g j p) d -> g p j d", j=GROUP, p=P)
    at = lambda v, g: v[bass.ds(g, 1), :, :, :].rearrange("o p j d -> (o p) j d")
    xo, xn = rows(x_old), rows(x_new)
    fn = rows(f_new) if f_new is not None else None
    res_dram = rows(result) if width == D else None
    product = head.kind == "product"
    PT = 2 * GROUP * (2 if product else 1)
    NH = {"product": GROUP, "experts": 8, "batch_norm": 3}[head.kind]
    PER = 2 * (NH + 3 * GROUP + 1)
    with Stage(nc) as s:
        x = [s.sb(f"x{h}", [P, GROUP, D], F32) for h in range(2)]
        f = [s.sb(f"f{h}", [P, GROUP, D], F32) for h in range(2)]
        part = s.sb("part", [P, GROUP, D], F32) if head.kind != "experts" else None
        xt = [s.sb(f"xt{n}", [P, 2, P], F32) for n in range(2)]
        res = s.sb("res", [P, 2, GROUP, D], F32) if width == D else None
        stats, mv = s.sb("stats", [P, GROUP, 6], F32), s.sb("mv", [P, GROUP, 2], F32)
        std, rstd = s.sb("std", [P, GROUP], F32), s.sb("rstd", [P, GROUP], F32)
        if head.kind == "experts":
            y = [s.sb(f"y{h}", [P, GROUP, D], F32) for h in range(2)]
            idx = s.sb("idx", [P, 2, GROUP], I32)
            clean, odd = s.sb("clean", [P, GROUP, D], F32), s.sb("odd", [P, GROUP, D], U16)
        xt_ps = [s.ps(f"xt_ps{n}", [P, 2, P]) for n in range(2)]
        head_ps = [s.ps(f"head_ps{n}", [P, D]) for n in range(2)]
        tail_ps = [s.ps(f"tail_ps{n}", [P, D]) for n in range(2)]
        (go, x_done, f_done, chain, var_done, std_done, part_done, transposed, turned, head_done, head_used, tail_done,
         tail_used, staged, odd_go) = (s.sem(n) for n in (
             "go", "x_done", "f_done", "chain", "var_done", "std_done", "part_done", "transposed", "turned", "head_done",
             "head_used", "tail_done", "tail_used", "staged", "odd_go"))
        loaded, x_stored, f_stored, r_stored, fetched = ([s.sem(f"{n}{h}") for h in range(2)] for n in (
            "loaded", "x_stored", "f_stored", "r_stored", "fetched"))
        turns = GROUPS // 2
        with nc.Block() as block:
            @block.sync
            def _(sp):
                sp.wait_ge(go, 1)

                def turn(i, again):
                    for h in range(2):
                        if again:
                            hold(sp, go, x_stored[h], i * 16)
                            hold(sp, go, f_done, (i * 2 + h - 1) * GROUP)
                        sp.dma_start(x[h][:, :, :], at(xo, i * 2 + h)).then_inc(loaded[h], 16)
                    for h in range(2):
                        hold(sp, go, x_done, i * 2 + h + 1)
                        sp.dma_start(at(xn, i * 2 + h), x[h][:, :, :]).then_inc(x_stored[h], 16)
                        if fn is not None:
                            hold(sp, go, f_done, (i * 2 + h + 1) * GROUP)
                            sp.dma_start(at(fn, i * 2 + h), f[h][:, :, :]).then_inc(f_stored[h], 16)
                        if res is not None:
                            hold(sp, go, tail_used, (i * 2 + h + 1) * GROUP + 2)
                            sp.dma_start(at(res_dram, i * 2 + h), res[:, h, :, :]).then_inc(r_stored[h], 16)

                turn(0, False)
                with sp.Fori(1, turns) as i:
                    turn(i, True)
                for h in range(2):
                    sp.wait_ge(x_stored[h], 16 * turns)
                    if fn is not None:
                        sp.wait_ge(f_stored[h], 16 * turns)
                    if res is not None:
                        sp.wait_ge(r_stored[h], 16 * turns)

            if head.kind == "experts":
                @block.gpsimd
                def _(pool):
                    pool.wait_ge(go, 1)

                    def turn(i, again):
                        for h in range(2):
                            if again:
                                hold(pool, go, x_done, i * 2 + h - 1)
                            nc.gpsimd.tensor_copy(idx[:, h, :], head.rows[:, bass.ds((i * 2 + h) * GROUP, GROUP)]).then_inc(staged, 1)
                            hold(pool, go, staged, i * 2 + h + 1)
                            for j in range(GROUP):
                                pool.indirect_dma_start(out=y[h][:, j, :], out_offset=None, in_=head.table,
                                                        in_offset=bass.IndirectOffsetOnAxis(ap=idx[:, h, j:j + 1], axis=0)).then_inc(fetched[h], 16)

                    turn(0, False)
                    with pool.Fori(1, turns) as i:
                        turn(i, True)

            @block.tensor
            def _(pe):
                pe.wait_ge(go, 1)
                with pe.Fori(0, turns) as i:
                    m = 0

                    def multiply(src, src_ready, value, weights, out, done, used, used_value, row):
                        nonlocal m
                        pe.wait_ge(src_ready, value)
                        pe.wait_ge(turned, i * PT + m + 1)
                        for c in range(2):
                            ins = nc.tensor.transpose(xt_ps[m % 2][:, c, :], src[:, c * P:(c + 1) * P], k.ident[:, :])
                        ins.then_inc(transposed, 1)
                        pe.wait_ge(used, used_value)
                        pe.wait_ge(turned, i * PT + m + 3)
                        if row is not None:
                            nc.tensor.matmul(out, k.ones[0:1, :], row, start=True, stop=False)
                        nc.tensor.matmul(out, xt[m % 2][:, 0, :], weights[:, 0, :], start=row is None, stop=False)
                        nc.tensor.matmul(out, xt[m % 2][:, 1, :], weights[:, 1, :], start=False, stop=True).then_inc(done, 1)
                        m += 1

                    for h in range(2):
                        for j in range(GROUP if product else 0):
                            n = h * GROUP + j
                            multiply(part[:, j, :], part_done, i * 2 + h + 1, head.w, head_ps[n % 2][:, :], head_done,
                                     head_used, i * 2 * GROUP + n + 1, head.bias)
                        for j in range(GROUP):
                            n = h * GROUP + j
                            multiply(f[h][:, j, :], f_done, i * 2 * GROUP + n + 1, w, tail_ps[n % 2][:, 0:width], tail_done,
                                     tail_used, i * 2 * GROUP + n + 1, bias)
                    assert m == PT

            @block.scalar
            def _(act):
                act.sem_inc(turned, 2)
                act.sem_inc(tail_used, 2)
                act.sem_inc(go, 1)

                def turn(i, again):
                    m = 0

                    def copy_turned():
                        nonlocal m
                        act.wait_ge(transposed, i * PT + m + 1)
                        nc.scalar.activation(xt[m % 2][:, :, :], xt_ps[m % 2][:, :, :], ACT.Copy).then_inc(turned, 1)
                        m += 1

                    for h in range(2):
                        if product:
                            if again or h:
                                hold(act, go, head_done, (i * 2 + h) * GROUP)
                            nc.scalar.activation(part[:, :, :], head.sums[:, bass.ds((i * 2 + h) * GROUP, GROUP), :], ACT.Copy).then_inc(part_done, 1)
                            for j in range(GROUP):
                                copy_turned()
                        act.wait_ge(var_done, i * 2 + h + 1)
                        nc.scalar.activation(std[:, :], mv[:, :, 1], ACT.Sqrt, bias=k.eps[:, :]).then_inc(std_done, 1)
                        for j in range(GROUP):
                            n = h * GROUP + j
                            copy_turned()
                            if res is not None:
                                if again and j == 0:
                                    hold(act, go, r_stored[h], i * 16)
                                act.wait_ge(tail_done, i * 2 * GROUP + n + 1)
                                nc.scalar.activation(res[:, h, j, :], tail_ps[n % 2][:, :], ACT.Copy).then_inc(tail_used, 1)
                            else:
                                hold(act, go, tail_done, i * 2 * GROUP + n + 1)
                                nc.scalar.activation(result[:, bass.ds(i * 2 * GROUP + n, 1), :].rearrange("p o w -> p (o w)"),
                                                     tail_ps[n % 2][:, 0:width], ACT.Copy).then_inc(tail_used, 1)

                turn(0, False)
                with act.Fori(1, turns) as i:
                    turn(i, True)

            @block.vector
            def _(dve):
                dve.sem_inc(head_used, 2)
                dve.wait_ge(go, 1)
                if head.kind == "experts":
                    nc.vector.memset(k.big[:, :], 1e4).then_inc(odd_go, 1)
                    nc.vector.memset(k.small[:, :], -1e4).then_inc(odd_go, 1)
                    dve.wait_ge(odd_go, 2)

                def turn(i, again):
                    link = Chain(dve, chain, i * PER, go)
                    for h in range(2):
                        hold(dve, go, loaded[h], i * 16 + 16)
                        xh = x[h]
                        if product:
                            for j in range(GROUP):
                                n = h * GROUP + j
                                dve.wait_ge(head_done, i * 2 * GROUP + n + 1)
                                ins = nc.vector.tensor_tensor(xh[:, j, :], head_ps[n % 2][:, :], xh[:, j, :], ALU.add)
                                link(ins)
                                dve.sem_inc(head_used, 1)
                        elif head.kind == "experts":
                            g = (i * 2 + h) * GROUP
                            hold(dve, go, fetched[h], (i + 1) * 16 * GROUP)
                            yh = y[h][:, :, :]
                            link(nc.vector.tensor_tensor(yh, yh, bc(head.scale[:, bass.ds(g, GROUP)], D), ALU.mult))
                            link(nc.vector.tensor_tensor(odd[:, :, :], yh, yh, ALU.is_equal))
                            link(nc.vector.memset(clean[:, :, :], 0.0))
                            link(nc.vector.copy_predicated(clean[:, :, :], odd[:, :, :], yh))
                            link(nc.vector.tensor_scalar(odd[:, :, :], clean[:, :, :], FLT_MAX, None, ALU.is_gt))
                            link(nc.vector.copy_predicated(clean[:, :, :], odd[:, :, :], k.big[:, 0:1].unsqueeze(2).to_broadcast([P, GROUP, D])))
                            link(nc.vector.tensor_scalar(odd[:, :, :], clean[:, :, :], -FLT_MAX, None, ALU.is_lt))
                            nc.vector.copy_predicated(clean[:, :, :], odd[:, :, :], k.small[:, 0:1].unsqueeze(2).to_broadcast([P, GROUP, D])).then_inc(odd_go, 1)
                            hold(dve, go, odd_go, i * 2 + h + 3)
                            link(nc.vector.tensor_tensor(xh[:, :, :], xh[:, :, :], clean[:, :, :], ALU.add))
                        else:
                            sums = head.sums[:, bass.ds((i * 2 + h) * GROUP, GROUP), :]
                            link(nc.vector.tensor_tensor(part[:, :, :], sums, bc(head.gain[:, :], GROUP, 1), ALU.mult))
                            link(nc.vector.tensor_tensor(part[:, :, :], part[:, :, :], bc(head.offset[:, :], GROUP, 1), ALU.add))
                            link(nc.vector.scalar_tensor_tensor(xh[:, :, :], part[:, :, :], 0.0, xh[:, :, :], ALU.max, ALU.add))
                        dve.sem_inc(x_done, 1)
                        for j in range(GROUP):
                            link(nc.vector.bn_stats(stats[:, j, :], xh[:, j, :]))
                            link(nc.vector.bn_aggr(mv[:, j, :], stats[:, j, :]))
                        dve.sem_inc(var_done, 1)
                        dve.wait_ge(std_done, i * 2 + h + 1)
                        link(nc.vector.reciprocal(rstd[:, :], std[:, :]))
                        if again:
                            if fn is not None:
                                hold(dve, go, f_stored[h], i * 16)
                            hold(dve, go, tail_done, (i * 2 + h - 1) * GROUP)
                        for j in range(GROUP):
                            link(nc.vector.tensor_scalar(f[h][:, j, :], xh[:, j, :], mv[:, j, 0:1], rstd[:, j:j + 1], ALU.subtract, ALU.mult))
                            dve.sem_inc(f_done, 1)
                    assert link.n == PER, (link.n, PER)

                turn(0, False)
                with dve.Fori(1, turns) as i:
                    turn(i, True)


FLT_MAX = 3.4028234663852886e38


def route_tokens(nc, k, logits, send, fetch, scale):
    T, E = TILES, EXPERTS
    with Stage(nc) as s:
        prob, hot, rank, run, tot = (s.sb(n, [P, T, E], F32) for n in ("prob", "hot", "rank", "run", "tot"))
        top, best, kept, place = (s.sb(n, [P, T], F32) for n in ("top", "best", "kept", "place"))
        ranks = s.ps("ranks", [P, 2, 512])
        tots = s.ps("tots", [P, 2, 512])
        order = s.sb("order", [P, E], F32)
        chain, shifted, exped, hot_done, counted = (s.sem(n) for n in ("chain", "shifted", "exped", "hot_done", "counted"))
        half = T // 2 * E
        with nc.Block() as block:
            @block.scalar
            def _(act):
                act.wait_ge(shifted, 1)
                nc.scalar.activation(prob[:, :, :], prob[:, :, :], ACT.Exp).then_inc(exped, 1)

            @block.tensor
            def _(pe):
                pe.wait_ge(hot_done, 1)
                for c in range(2):
                    rhs = hot[:, c * T // 2:(c + 1) * T // 2, :].rearrange("p t e -> p (t e)")
                    nc.tensor.matmul(ranks[:, c, 0:half], k.before[:, :], rhs, start=True, stop=True)
                    nc.tensor.matmul(tots[:, c, 0:half], k.ones[:, :], rhs, start=True, stop=True).then_inc(counted, 1)

            @block.vector
            def _(dve):
                link = Chain(dve, chain)
                link(nc.vector.tensor_reduce(top[:, :], logits[:, :, :], AX.X, ALU.max))
                link(nc.vector.tensor_tensor(prob[:, :, :], logits[:, :, :], bc(top[:, :], E), ALU.subtract))
                dve.sem_inc(shifted, 1)
                dve.wait_ge(exped, 1)
                link(nc.vector.tensor_reduce(top[:, :], prob[:, :, :], AX.X, ALU.add))
                link(nc.vector.reciprocal(top[:, :], top[:, :]))
                link(nc.vector.tensor_tensor(prob[:, :, :], prob[:, :, :], bc(top[:, :], E), ALU.mult))
                link(nc.vector.tensor_reduce(top[:, :], prob[:, :, :], AX.X, ALU.max))
                link(nc.vector.tensor_tensor(hot[:, :, :], prob[:, :, :], bc(top[:, :], E), ALU.is_equal))
                link(nc.vector.tensor_scalar(order[:, :], k.iota[:, 0:E], -1.0, float(E), ALU.mult, ALU.add))
                link(nc.vector.tensor_tensor(prob[:, :, :], hot[:, :, :], bc(order[:, :], T, 1), ALU.mult))
                link(nc.vector.tensor_reduce(best[:, :], prob[:, :, :], AX.X, ALU.max))
                link(nc.vector.tensor_tensor(hot[:, :, :], prob[:, :, :], bc(best[:, :], E), ALU.is_equal))
                dve.sem_inc(hot_done, 1)
                dve.wait_ge(counted, 2)
                for c in range(2):
                    sl = slice(c * T // 2, (c + 1) * T // 2)
                    link(nc.vector.tensor_copy(rank[:, sl, :].rearrange("p t e -> p (t e)"), ranks[:, c, 0:half]))
                    link(nc.vector.tensor_copy(tot[:, sl, :].rearrange("p t e -> p (t e)"), tots[:, c, 0:half]))
                for e in range(E):
                    link(nc.vector.tensor_tensor_scan(run[:, :, e], tot[:, :, e], tot[:, :, e], 0.0, ALU.add, ALU.bypass))
                link(nc.vector.tensor_tensor(run[:, :, :], run[:, :, :], tot[:, :, :], ALU.subtract))
                link(nc.vector.tensor_tensor(rank[:, :, :], rank[:, :, :], run[:, :, :], ALU.add))
                link(nc.vector.tensor_tensor(rank[:, :, :], rank[:, :, :], hot[:, :, :], ALU.mult))
                link(nc.vector.tensor_reduce(place[:, :], rank[:, :, :], AX.X, ALU.add))
                link(nc.vector.tensor_scalar(kept[:, :], place[:, :], float(CAP), None, ALU.is_lt))
                link(nc.vector.tensor_tensor(scale[:, :], top[:, :], kept[:, :], ALU.mult))
                link(nc.vector.tensor_scalar(best[:, :], best[:, :], -float(SLOTS), float(E * SLOTS), ALU.mult, ALU.add))
                link(nc.vector.scalar_tensor_tensor(fetch[:, :], place[:, :], float(CAP - 1), best[:, :], ALU.min, ALU.add))
                link(nc.vector.tensor_scalar(kept[:, :], kept[:, :], -float(E * SLOTS), float(E * SLOTS), ALU.mult, ALU.add))
                link(nc.vector.tensor_tensor(place[:, :], place[:, :], best[:, :], ALU.add))
                link(nc.vector.tensor_tensor(send[:, :], place[:, :], kept[:, :], ALU.add))


def dispatch_tokens(nc, k, f, send, dest):
    fv = f[0:NPAD, :].rearrange("(g j p) d -> g p j d", j=GROUP, p=P)
    with Stage(nc) as s:
        rows = [s.sb(f"rows{h}", [P, GROUP, D], F32) for h in range(2)]
        idx = s.sb("idx", [P, 2, GROUP], I32)
        zeroed, staged, go = s.sem("zeroed"), s.sem("staged"), s.sem("go")
        loaded, sent = ([s.sem(f"{n}{h}") for h in range(2)] for n in ("loaded", "sent"))
        turns = GROUPS // 2
        with nc.Block() as block:
            @block.sync
            def _(sp):
                sp.dma_start(dest.rearrange("(p r) d -> p r d", p=P), bc(k.zero[:, :], EXPERTS * SLOTS // P, 1)).then_inc(zeroed, 16)

                def turn(i, again):
                    for h in range(2):
                        if again:
                            hold(sp, go, sent[h], i * 16 * GROUP)
                        sp.dma_start(rows[h][:, :, :], fv[bass.ds(i * 2 + h, 1), :, :, :].rearrange("o p j d -> (o p) j d")).then_inc(loaded[h], 16)

                turn(0, False)
                with sp.Fori(1, turns) as i:
                    turn(i, True)

            @block.gpsimd
            def _(pool):
                pool.sem_inc(go, 1)
                pool.wait_ge(zeroed, 16)

                def turn(i, again):
                    for h in range(2):
                        if again:
                            hold(pool, go, sent[h], i * 16 * GROUP)
                        nc.gpsimd.tensor_copy(idx[:, h, :], send[:, bass.ds((i * 2 + h) * GROUP, GROUP)]).then_inc(staged, 1)
                        hold(pool, go, staged, i * 2 + h + 1)
                        hold(pool, go, loaded[h], i * 16 + 16)
                        for j in range(GROUP):
                            pool.indirect_dma_start(out=dest, out_offset=bass.IndirectOffsetOnAxis(ap=idx[:, h, j:j + 1], axis=0),
                                                    in_=rows[h][:, j, :], in_offset=None,
                                                    bounds_check=EXPERTS * SLOTS - 1, oob_is_err=False).then_inc(sent[h], 16)

                turn(0, False)
                with pool.Fori(1, turns) as i:
                    turn(i, True)
                for h in range(2):
                    pool.wait_ge(sent[h], turns * 16 * GROUP)


def run_experts(nc, k, xbuf, w1, b1, w2, b2, ybuf):
    W, FC, BLOCKS = 512, HID // P, SLOTS // 512
    xv = xbuf.rearrange("(e b c p) d -> e b p c d", p=P, c=4, b=BLOCKS)
    yv = ybuf.rearrange("(e b c p) d -> e b p c d", p=P, c=4, b=BLOCKS)
    one = lambda v, e: v[bass.ds(e, 1), :, :, :].rearrange("o p c d -> (o p) c d")
    with Stage(nc) as s:
        w1s = [s.sb(f"w1s{n}", [P, 2, HID], F32) for n in range(2)]
        w2s = [s.sb(f"w2s{n}", [P, FC, D], F32) for n in range(2)]
        b1s = [s.sb(f"b1s{n}", [P, FC], F32) for n in range(2)]
        b2s = [s.sb(f"b2s{n}", [1, D], F32) for n in range(2)]
        x = [s.sb(f"x{n}", [P, 4, D], F32) for n in range(2)]
        xt = [s.sb(f"xt{n}", [P, 2, W], F32) for n in range(2)]
        hid = [s.sb(f"hid{n}", [P, FC, W], F32) for n in range(2)]
        y = [s.sb(f"y{n}", [P, 4, D], F32) for n in range(2)]
        xt_ps = [s.ps(f"xt_ps{c}", [P, W]) for c in range(2)]
        hid_ps = [s.ps(f"hid_ps{n}", [P, W]) for n in range(4)]
        y_ps = [s.ps(f"y_ps{n}", [P, 512]) for n in range(2)]
        weights, x_loaded, y_stored = ([s.sem(f"{n}{h}") for h in range(2)] for n in ("weights", "x_loaded", "y_stored"))
        go, turned, xt_done, hid_mult, hid_done, y_mult, y_done, b1_ok = (s.sem(n) for n in (
            "go", "turned", "xt_done", "hid_mult", "hid_done", "y_mult", "y_done", "b1_ok"))
        NB = 2 * BLOCKS
        turns = EXPERTS // 2
        with nc.Block() as block:
            @block.sync
            def _(sp):
                def turn(i, again):
                    for n in range(2):
                        e = i * 2 + n
                        if again:
                            hold(sp, go, y_mult, (i * NB - NB + (n + 1) * BLOCKS) * 4)
                        pick = lambda v: v[bass.ds(e, 1)]
                        sp.dma_start(w1s[n][:, :, :], pick(w1).rearrange("o (c p) f -> (o p) c f", p=P)).then_inc(weights[n], 16)
                        sp.dma_start(w2s[n][:, :, :], pick(w2).rearrange("o (c p) d -> (o p) c d", p=P)).then_inc(weights[n], 16)
                        sp.dma_start(b1s[n][:, :], pick(b1).rearrange("o (c p) -> (o p) c", p=P), allow_slow_non_contiguous=True).then_inc(weights[n], 16)
                        sp.dma_start(b2s[n][:, :], pick(b2)).then_inc(weights[n], 16)
                        for b in range(BLOCKS):
                            m = n * BLOCKS + b
                            if again or m >= 2:
                                hold(sp, go, turned, (i * NB + m - 1) * 2)
                            sp.dma_start(x[m % 2][:, :, :], one(xv[:, b, :, :, :], e)).then_inc(x_loaded[m % 2], 16)

                turn(0, False)
                with sp.Fori(1, turns) as i:
                    turn(i, True)

            @block.tensor
            def _(pe):
                pe.wait_ge(go, 1)
                with pe.Fori(0, turns) as i:
                    for m in range(NB):
                        n = m // BLOCKS
                        pe.wait_ge(x_loaded[m % 2], i * (16 * NB // 2) + 16 * (m // 2 + 1))
                        pe.wait_ge(xt_done, (i * NB + m) * 2 + 2)
                        for c in range(2):
                            for r in range(4):
                                ins = nc.tensor.transpose(xt_ps[c][:, r * P:(r + 1) * P], x[m % 2][:, r, c * P:(c + 1) * P], k.ident[:, :])
                            ins.then_inc(turned, 1)
                        pe.wait_ge(xt_done, (i * NB + m) * 2 + 4)
                        pe.wait_ge(weights[n], i * 64 + 64)
                        for fc in range(FC):
                            pe.wait_ge(hid_done, (i * NB + m) * FC + fc + 1)
                            for c in range(2):
                                ins = nc.tensor.matmul(hid_ps[fc % 4][:, :], w1s[n][:, c, fc * P:(fc + 1) * P], xt[m % 2][:, c, :],
                                                       start=c == 0, stop=c == 1)
                            ins.then_inc(hid_mult, 1)
                        for r in range(4):
                            pe.wait_ge(y_done, (i * NB + m) * 4 + r + 1)
                            out = y_ps[r % 2][:, 0:D]
                            nc.tensor.matmul(out, k.ones[0:1, :], b2s[n][:, :], start=True, stop=False)
                            for fc in range(FC):
                                if r == 0:
                                    pe.wait_ge(hid_done, (i * NB + m) * FC + fc + 5)
                                ins = nc.tensor.matmul(out, hid[m % 2][:, fc, r * P:(r + 1) * P], w2s[n][:, fc, :], start=False, stop=fc == FC - 1)
                            ins.then_inc(y_mult, 1)

            @block.scalar
            def _(act):
                act.sem_inc(hid_done, 4)
                act.sem_inc(go, 1)

                with act.Fori(0, turns) as i:
                    for m in range(NB):
                        n = m // BLOCKS
                        hold(act, go, weights[n], i * 64 + 64)
                        for fc in range(FC):
                            act.wait_ge(hid_mult, (i * NB + m) * FC + fc + 1)
                            nc.scalar.activation(hid[m % 2][:, fc, :], hid_ps[fc % 4][:, :], ACT.Relu, bias=b1s[n][:, fc:fc + 1]).then_inc(hid_done, 1)

            @block.vector
            def _(dve):
                dve.sem_inc(xt_done, 2)
                dve.sem_inc(y_done, 2)
                dve.wait_ge(go, 1)

                def turn(i, again):
                    for m in range(NB):
                        for c in range(2):
                            dve.wait_ge(turned, (i * NB + m) * 2 + c + 1)
                            nc.vector.tensor_copy(xt[m % 2][:, c, :], xt_ps[c][:, :]).then_inc(xt_done, 1)
                        if again or m >= 2:
                            hold(dve, go, y_stored[m % 2], i * (16 * NB // 2) + 16 * (m // 2))
                        for r in range(4):
                            dve.wait_ge(y_mult, (i * NB + m) * 4 + r + 1)
                            nc.vector.tensor_copy(y[m % 2][:, r, :], y_ps[r % 2][:, 0:D]).then_inc(y_done, 1)

                turn(0, False)
                with dve.Fori(1, turns) as i:
                    turn(i, True)

            @block.gpsimd
            def _(pool):
                pool.wait_ge(go, 1)
                with pool.Fori(0, turns) as i:
                    for m in range(NB):
                        n, b = m // BLOCKS, m % BLOCKS
                        hold(pool, go, y_done, (i * NB + m) * 4 + 6)
                        pool.dma_start(one(yv[:, b, :, :, :], i * 2 + n), y[m % 2][:, :, :]).then_inc(y_stored[m % 2], 16)
                for h in range(2):
                    pool.wait_ge(y_stored[h], 16 * (NB // 2) * turns)


def node_statistics(nc, k, sums, gain, offset, params):
    bias, gamma, beta = params
    turns = GROUPS // 2
    with Stage(nc) as s:
        mean, var, std, tmp = (s.sb(n, [P, D], F32) for n in ("mean", "var", "std", "tmp"))
        dev = [s.sb(f"dev{h}", [P, GROUP, D], F32) for h in range(2)]
        rows = [s.sb(f"row{n}", [P, D], F32) for n in range(3)]
        last = s.sb("last", [P, P], F32)
        sum_ps, sq_ps = s.ps("sum_ps", [P, 512]), s.ps("sq_ps", [P, 512])
        loaded, go, summed, dev_done, squared, used, chain, var_done, std_done, mask_done = (s.sem(n) for n in (
            "loaded", "go", "summed", "dev_done", "squared", "used", "chain", "var_done", "std_done", "mask_done"))
        with nc.Block() as block:
            @block.sync
            def _(sp):
                for r, v in zip(rows, params):
                    sp.dma_start(r[:, :], v.unsqueeze(0).to_broadcast([P, D])).then_inc(loaded, 16)

            @block.gpsimd
            def _(pool):
                nc.gpsimd.affine_select(out=last[:, :], in_=k.ones[:, :], compare_op=ALU.is_gt, fill=0.0,
                                        base=N - (TILES - 1) * P, pattern=[[0, P]], channel_multiplier=-1).then_inc(mask_done, 1)

            @block.tensor
            def _(pe):
                pe.wait_ge(go, 1)
                out = sum_ps[:, 0:D]
                nc.tensor.matmul(out, k.ones[:, :], sums[:, 0, :], start=True, stop=False)
                with pe.Fori(1, TILES - 1) as t:
                    nc.tensor.matmul(out, k.ones[:, :], sums[:, bass.ds(t, 1), :].rearrange("p o d -> p (o d)"), start=False, stop=False)
                nc.tensor.matmul(out, k.ones[:, :], sums[:, TILES - 1, :], start=False, stop=True).then_inc(summed, 1)
                pe.wait_ge(mask_done, 1)

                def turn(i, first, end):
                    for h in range(2):
                        pe.wait_ge(squared, i * 2 + h + 1)
                        for j in range(GROUP):
                            is_last = end and h == 1 and j == GROUP - 1
                            ins = nc.tensor.matmul(sq_ps[:, 0:D], (last if is_last else k.ones)[:, :], dev[h][:, j, :],
                                                   start=first and h == 0 and j == 0, stop=is_last)
                        ins.then_inc(used, 1)

                turn(0, True, False)
                with pe.Fori(1, turns - 1) as i:
                    turn(i, False, False)
                turn(turns - 1, False, True)

            @block.scalar
            def _(act):
                act.sem_inc(go, 1)
                with act.Fori(0, turns) as i:
                    for h in range(2):
                        act.wait_ge(dev_done, i * 2 + h + 1)
                        nc.scalar.activation(dev[h][:, :, :], dev[h][:, :, :], ACT.Square).then_inc(squared, 1)
                act.wait_ge(var_done, 1)
                nc.scalar.activation(std[:, :], var[:, :], ACT.Sqrt, bias=k.eps[:, :]).then_inc(std_done, 1)

            @block.vector
            def _(dve):
                link = Chain(dve, chain)
                dve.wait_ge(go, 1)
                dve.wait_ge(loaded, 48)
                dve.wait_ge(summed, 1)
                link(nc.vector.tensor_scalar(mean[:, :], sum_ps[:, 0:D], 1.0 / N, None, ALU.mult))

                def turn(i, again):
                    for h in range(2):
                        if again:
                            hold(dve, go, used, i * 2 + h - 1)
                        nc.vector.tensor_tensor(dev[h][:, :, :], sums[:, bass.ds((i * 2 + h) * GROUP, GROUP), :], bc(mean[:, :], GROUP, 1),
                                                ALU.subtract).then_inc(dev_done, 1)

                turn(0, False)
                with dve.Fori(1, turns) as i:
                    turn(i, True)
                dve.wait_ge(used, 2 * turns)
                link(nc.vector.tensor_scalar(var[:, :], sq_ps[:, 0:D], 1.0 / N, None, ALU.mult))
                dve.sem_inc(var_done, 1)
                dve.wait_ge(std_done, 1)
                link(nc.vector.reciprocal(std[:, :], std[:, :]))
                link(nc.vector.tensor_tensor(gain[:, :], std[:, :], rows[1][:, :], ALU.mult))
                link(nc.vector.tensor_tensor(mean[:, :], mean[:, :], rows[0][:, :], ALU.add))
                link(nc.vector.tensor_tensor(tmp[:, :], rows[0][:, :], mean[:, :], ALU.subtract))
                link(nc.vector.tensor_tensor(tmp[:, :], tmp[:, :], gain[:, :], ALU.mult))
                link(nc.vector.tensor_tensor(offset[:, :], tmp[:, :], rows[2][:, :], ALU.add))


def attention_table(nc, k, a, heads, mine, target, table):
    W = HEADS * GEXP
    with Stage(nc) as s:
        att = [s.sb(f"att{n}", [P, W], F32) for n in range(2)]
        prod = s.sb("prod", [P, TILES, W], F32)
        rounded, rest = s.sb("rounded", [P, TILES, HEADS], BF16), s.sb("rest", [P, TILES, HEADS], F32)
        loaded, chain, made, stored = (s.sem(n) for n in ("loaded", "chain", "made", "stored"))
        with nc.Block() as block:
            @block.sync
            def _(sp):
                for r, name in zip(att, ("L1_ffn_att_src", "L1_ffn_att_dst")):
                    sp.dma_start(r[:, :], a[name].rearrange("h e -> (h e)").unsqueeze(0).to_broadcast([P, W])).then_inc(loaded, 16)
                sp.wait_ge(made, 1)
                sp.dma_start(table.rearrange("(t p) w -> p t w", p=P), mine[:, :, :]).then_inc(stored, 16)
                sp.wait_ge(stored, 16)

            @block.vector
            def _(dve):
                link = Chain(dve, chain)
                dve.wait_ge(loaded, 32)
                link(nc.vector.tensor_copy(mine[:, :, 0:W], heads[:, :, :]))
                for r, dest in zip(att, (mine[:, :, W:W + HEADS], target[:, 0:TILES, :])):
                    link(nc.vector.tensor_tensor(prod[:, :, :], heads[:, :, :], bc(r[:, :], TILES, 1), ALU.mult))
                    link(nc.vector.tensor_reduce(dest, prod[:, :, :].rearrange("p t (h e) -> p t h e", h=HEADS), AX.X, ALU.add))
                link(nc.vector.memset(target[:, TILES, :], 0.0))
                left, first = mine[:, :, W:W + HEADS], W + HEADS
                for c in range(3):
                    part = mine[:, :, first + c * HEADS:first + (c + 1) * HEADS]
                    link(nc.vector.tensor_copy(rounded[:, :, :], left))
                    link(nc.vector.tensor_copy(part, rounded[:, :, :]))
                    if c < 2:
                        link(nc.vector.tensor_tensor(rest[:, :, :], left, part, ALU.subtract))
                        left = rest[:, :, :]
                dve.sem_inc(made, 1)


def attend_maxima(nc, k, q, table, fetched, top):
    turns = GPAIRS // LANES
    W, S = HEADS * GEXP, 3 * HEADS
    with Stage(nc) as s:
        idx = s.sb("idx", [P, LANES], I32)
        rows = s.sb("rows", [P, LANES, W + HEADS + S], F32)
        score = [s.sb(f"score{h}", [P, HALF, S], BF16) for h in range(2)]
        score_t = [s.sb(f"score_t{h}", [HALF * S, P], BF16) for h in range(2)]
        pick = s.sb("pick", [HALF * S, HALF, HEADS], BF16)
        away = s.sb("away", [P, LANES, P], BF16)
        top_p = s.sb("top_p", [P, LANES, HEADS], F32)
        score_ps = [s.ps(f"score_ps{h}", [HALF * S, 1024], BF16) for h in range(2)]
        all_ps = [s.ps(f"all_ps{n}", [P, HEADS, P]) for n in range(4)]
        gathered = [s.sem(f"gathered{u}") for u in range(LANES)]
        go, staged, taken, turned, copied, away_done, listed, chain, used, drained = (s.sem(n) for n in (
            "go", "staged", "taken", "turned", "copied", "away_done", "listed", "chain", "used", "drained"))
        with nc.Block() as block:
            @block.gpsimd
            def _(pool):
                pool.wait_ge(go, 1)
                with pool.Fori(0, turns) as i:
                    for h in range(2):
                        hold(pool, go, taken, i * 2 + h + 1)
                        nc.gpsimd.tensor_copy(idx[:, h * HALF:(h + 1) * HALF], q.row[:, bass.ds(i * LANES + h * HALF, HALF)]).then_inc(staged, 1)
                        hold(pool, go, staged, i * 2 + h + 1)
                        for u in range(h * HALF, (h + 1) * HALF):
                            pool.indirect_dma_start(out=rows[:, u, :], out_offset=None, in_=table,
                                                    in_offset=bass.IndirectOffsetOnAxis(ap=idx[:, u:u + 1], axis=0)).then_inc(gathered[u], 16)

            @block.scalar
            def _(act):
                act.sem_inc(taken, 2)
                act.sem_inc(copied, 2)
                act.wait_ge(go, 1)
                with act.Fori(0, turns) as i:
                    for h in range(2):
                        half = rows[:, h * HALF:(h + 1) * HALF, :]
                        for u in range(h * HALF, (h + 1) * HALF):
                            hold(act, go, gathered[u], i * 16 + 16)
                        nc.scalar.activation(fetched[:, bass.ds(i * LANES + h * HALF, HALF), :], half[:, :, 0:W + HEADS], ACT.Copy).then_inc(drained, 1)
                        act.wait_ge(drained, i * 2 + h + 1)
                        nc.scalar.activation(score[h][:, :, :], half[:, :, W + HEADS:], ACT.Copy).then_inc(taken, 1)
                        act.wait_ge(turned, i * 2 + h + 1)
                        hold(act, go, listed, (i * 2 + h + 1) * HALF)
                        nc.scalar.activation(score_t[h][:, :], score_ps[h][:, 0:P], ACT.Copy).then_inc(copied, 1)

            @block.tensor
            def _(pe):
                pe.sem_inc(listed, 2 * HALF)
                pe.wait_ge(go, 1)
                with pe.Fori(0, turns) as i:
                    for h in range(2):
                        pe.wait_ge(taken, i * 2 + h + 3)
                        pe.wait_ge(copied, i * 2 + h + 1)
                        nc.tensor.transpose(score_ps[h][:, 0:P], score[h][:, :, :].rearrange("p u s -> p (u s)"), k.ident_bf[:, :]).then_inc(turned, 1)
                        pe.wait_ge(copied, i * 2 + h + 3)
                        for v in range(HALF):
                            u = h * HALF + v
                            pe.wait_ge(used, i * LANES + u + 1)
                            pe.wait_ge(away_done, i * LANES + u + 1)
                            for j in range(HEADS):
                                nc.tensor.matmul(all_ps[u % 4][:, j, :], pick[:, v, j:j + 1].to_broadcast([HALF * S, P]), score_t[h][:, :],
                                                 start=j == 0, stop=False)
                            nc.tensor.matmul(all_ps[u % 4][:, :, :], away[:, u, :], bc(k.ident_bf[:, :], HEADS, 1), start=False, stop=True).then_inc(listed, 1)

            @block.vector
            def _(dve):
                def mark(g, h):
                    for u in range(HALF):
                        nc.vector.tensor_scalar(away[:, h * HALF + u, :], k.iota[:, :], q.place[:, bass.ds(g * HALF + u, 1)], -1e30,
                                                ALU.not_equal, ALU.mult).then_inc(away_done, 1)

                regs = [dve.alloc_register(f"tile{n}_{nc.next_id()}") for n in range(4)]

                def maxima(g, h):
                    for four in range(0, HALF, 4):
                        for u in range(four, four + 4):
                            dve.wait_ge(listed, (g + 2) * HALF + u + 1)
                            nc.vector.tensor_reduce(top_p[:, h * HALF + u, :], all_ps[u % 4][:, :, :], AX.X, ALU.max).then_inc(used, 1)
                        tiles = load_tiles(nc, dve, q, g * HALF + four, regs)
                        hold(dve, go, used, g * HALF + four + 8)
                        for u in range(four, four + 4):
                            top_t = top[:, bass.ds(tiles[u % 4], 1), :].rearrange("p o s -> p (o s)")
                            dve.wait_ge(chain, g * HALF + u + 1)
                            nc.vector.tensor_tensor(top_t, top_t, top_p[:, h * HALF + u, :], ALU.max).then_inc(chain, 1)

                dve.sem_inc(used, 4)
                dve.sem_inc(chain, 1)
                nc.vector.tensor_reduce(pick[:, :, :], k.ident[0:HALF * S, 0:HALF * S].rearrange("p (v c j) -> p v j c", v=HALF, c=3),
                                        AX.X, ALU.max).then_inc(go, 1)
                dve.wait_ge(go, 1)
                mark(0, 0)
                with dve.Fori(0, turns - 1) as i:
                    for h in range(2):
                        mark(i * 2 + h + 1, 1 - h)
                        maxima(i * 2 + h, h)
                last = turns * 2 - 1
                mark(last, 1)
                maxima(last - 1, 0)
                maxima(last, 1)


def attend_self(nc, k, mine, target, top, score, sums):
    W, T = HEADS * GEXP, TILES
    with Stage(nc) as s:
        own = s.sb("own", [P, T, HEADS], F32)
        chain, shifted, exped = (s.sem(n) for n in ("chain", "shifted", "exped"))
        with nc.Block() as block:
            @block.vector
            def _(dve):
                link = Chain(dve, chain)
                link(nc.vector.memset(score[:, T, :], 0.0))
                link(nc.vector.memset(sums[:, T, :], 0.0))
                link(nc.vector.tensor_copy(score[:, 0:T, 0:HEADS], target[:, 0:T, :]))
                link(nc.vector.tensor_tensor(top[:, 0:T, :], top[:, 0:T, :], target[:, 0:T, :], ALU.add))
                link(nc.vector.scalar_tensor_tensor(score[:, 0:T, HEADS:2 * HEADS], top[:, 0:T, :], 0.2, top[:, 0:T, :], ALU.mult, ALU.max))
                link(nc.vector.tensor_tensor(own[:, :, :], mine[:, :, W:W + HEADS], target[:, 0:T, :], ALU.add))
                link(nc.vector.scalar_tensor_tensor(own[:, :, :], own[:, :, :], 0.2, own[:, :, :], ALU.mult, ALU.max))
                link(nc.vector.tensor_tensor(own[:, :, :], own[:, :, :], score[:, 0:T, HEADS:2 * HEADS], ALU.subtract))
                dve.sem_inc(shifted, 1)
                dve.wait_ge(exped, 1)
                link(nc.vector.tensor_copy(sums[:, 0:T, W:W + HEADS], own[:, :, :]))
                for j in range(HEADS):
                    link(nc.vector.tensor_tensor(sums[:, 0:T, j * GEXP:(j + 1) * GEXP], mine[:, :, j * GEXP:(j + 1) * GEXP],
                                                 bc(own[:, :, j], GEXP), ALU.mult))

            @block.scalar
            def _(act):
                act.wait_ge(shifted, 1)
                nc.scalar.activation(own[:, :, :], own[:, :, :], ACT.Exp).then_inc(exped, 1)


def attend_sums(nc, k, q, fetched, score, sums):
    turns = GPAIRS // LANES
    W = HEADS * GEXP
    with Stage(nc) as s:
        hot = s.sb("hot", [P, LANES, P], F32)
        hot_t = s.sb("hot_t", [P, LANES, P], F32)
        z = s.sb("z", [P, 2, HALF, HEADS], F32)
        val = s.sb("val", [P, 2, HALF, W + HEADS], F32)
        hot_ps = [s.ps(f"hot_ps{n}", [P, 4, P]) for n in range(2)]
        score_ps = [s.ps(f"score_ps{h}", [P, HALF, 64]) for h in range(2)]
        sum_ps = [s.ps(f"sum_ps{h}", [P, HALF, 64]) for h in range(2)]
        go, hot_done, turned, copied, scored, chain, shifted, exped, valued, summed, added = (s.sem(n) for n in (
            "go", "hot_done", "turned", "copied", "scored", "chain", "shifted", "exped", "valued", "summed", "added"))
        PER = 5

        def groups(eng, step):
            for h in range(2):
                step(h, h, h == 0, False)
            with eng.Fori(1, turns - 1) as i:
                for h in range(2):
                    step(i * 2 + h, h, False, False)
            for h in range(2):
                step(turns * 2 - 2 + h, h, False, h == 1)

        with nc.Block() as block:
            @block.vector
            def _(dve):
                def front(g, h, first):
                    if not first:
                        hold(dve, go, summed, g - 1)
                    for u in range(HALF):
                        nc.vector.tensor_scalar(hot[:, h * HALF + u, :], k.iota[:, :], q.place[:, bass.ds(g * HALF + u, 1)], None,
                                                ALU.is_equal).then_inc(hot_done, 1)

                regs = [dve.alloc_register(f"tile{n}_{nc.next_id()}") for n in range(4)]

                def back(g, h):
                    for u in range(HALF):
                        if u % 4 == 0:
                            tiles = load_tiles(nc, dve, q, g * HALF + u, regs)
                        sum_t = sums[:, bass.ds(tiles[u % 4], 1), :].rearrange("p o w -> p (o w)")
                        if u == 0:
                            hold(dve, go, summed, g + 1)
                        dve.wait_ge(added, (g + 1) * HALF + u + 1)
                        nc.vector.tensor_tensor(sum_t, sum_t, sum_ps[h][:, u, 0:W + HEADS], ALU.add).then_inc(added, 1)

                def step(g, h, first, last):
                    link = Chain(dve, chain, g * PER, go)
                    edges = fetched[:, bass.ds(g * HALF, HALF), :]
                    hold(dve, go, scored, g + 1)
                    zh, got = z[:, h, :, :], score_ps[h]
                    link(nc.vector.tensor_tensor(zh, edges[:, :, W:W + HEADS], got[:, :, 0:HEADS], ALU.add))
                    link(nc.vector.scalar_tensor_tensor(zh, zh, 0.2, zh, ALU.mult, ALU.max))
                    link(nc.vector.tensor_tensor(zh, zh, got[:, :, HEADS:2 * HEADS], ALU.subtract))
                    link(nc.vector.tensor_scalar(zh, zh, 0.0, None, ALU.min))
                    dve.sem_inc(shifted, 1)
                    if not last:
                        front(g + 1, 1 - h, first)
                    hold(dve, go, exped, g + 1)
                    v = val[:, h, :, :]
                    for j in range(HEADS):
                        ins = nc.vector.tensor_tensor(v[:, :, j * GEXP:(j + 1) * GEXP], edges[:, :, j * GEXP:(j + 1) * GEXP],
                                                      bc(v[:, :, W + j], GEXP), ALU.mult)
                        if j < HEADS - 1:
                            ins.then_inc(valued, 1)
                    link(ins)
                    dve.sem_inc(valued, 1)
                    if not first:
                        back(g - 1, 1 - h)

                dve.sem_inc(added, HALF + 1)
                dve.sem_inc(go, 1)
                front(0, 0, True)
                groups(dve, step)
                back(turns * 2 - 1, 1)

            @block.scalar
            def _(act):
                def copy(g, h):
                    for n in range(2):
                        act.wait_ge(turned, g * 2 + n + 1)
                        u = h * HALF + n * 4
                        nc.scalar.activation(hot_t[:, u:u + 4, :], hot_ps[n][:, :, :], ACT.Copy).then_inc(copied, 1)

                def step(g, h, first, last):
                    act.wait_ge(shifted, g + 1)
                    nc.scalar.activation(val[:, h, :, W:W + HEADS], z[:, h, :, :], ACT.Exp).then_inc(exped, 1)
                    if not last:
                        copy(g + 1, 1 - h)

                act.wait_ge(go, 1)
                copy(0, 0)
                groups(act, step)

            @block.tensor
            def _(pe):
                regs = [pe.alloc_register(f"tile{n}_{nc.next_id()}") for n in range(4)]

                def front(g, h):
                    for n in range(2):
                        for m in range(4):
                            pe.wait_ge(hot_done, g * HALF + n * 4 + m + 1)
                            ins = nc.tensor.transpose(hot_ps[n][:, m, :], hot[:, h * HALF + n * 4 + m, :], k.ident[:, :])
                        ins.then_inc(turned, 1)
                    for n in range(2):
                        tiles = load_tiles(nc, pe, q, g * HALF + n * 4, regs)
                        pe.wait_ge(copied, g * 2 + n + 1)
                        for m in range(4):
                            u = n * 4 + m
                            ins = nc.tensor.matmul(score_ps[h][:, u, 0:2 * HEADS], hot_t[:, h * HALF + u, :],
                                                   score[:, bass.ds(tiles[m], 1), :].rearrange("p o w -> p (o w)"), start=True, stop=True)
                    ins.then_inc(scored, 1)

                def step(g, h, first, last):
                    if not last:
                        front(g + 1, 1 - h)
                    pe.wait_ge(valued, g * HEADS + HEADS)
                    pe.wait_ge(added, g * HALF + 1)
                    for u in range(HALF):
                        ins = nc.tensor.matmul(sum_ps[h][:, u, 0:W + HEADS], hot[:, h * HALF + u, :], val[:, h, u, :], start=True, stop=True)
                    ins.then_inc(summed, 1)

                pe.wait_ge(go, 1)
                front(0, 0)
                groups(pe, step)


def attention_gates(nc, k, a, sums, gate):
    W, T, E = HEADS * GEXP, TILES, GEXP
    with Stage(nc) as s:
        v, sq = s.sb("v", [P, T, W], F32), s.sb("sq", [P, T, W], F32)
        rec = s.sb("rec", [P, T, HEADS], F32)
        row = [s.sb(f"row{n}", [P, W], F32) for n in range(3)]
        m1, m2, b, var = (s.sb(n, [P, T], F32) for n in ("m1", "m2", "b", "var"))
        sc, hot1, hot2, pick = (s.sb(n, [P, T, E], F32) for n in ("sc", "hot1", "hot2", "pick"))
        order = s.sb("order", [P, E], F32)
        loaded, chain, var_done, std_done, gap_done, exped = (s.sem(n) for n in (
            "loaded", "chain", "var_done", "std_done", "gap_done", "exped"))
        with nc.Block() as block:
            @block.sync
            def _(sp):
                for r, name in zip(row, ("L1_ffn_b_gat", "L1_ffn_ln_gamma", "L1_ffn_ln_beta")):
                    sp.dma_start(r[:, :], a[name].unsqueeze(0).to_broadcast([P, W])).then_inc(loaded, 16)

            @block.scalar
            def _(act):
                act.wait_ge(var_done, 1)
                nc.scalar.activation(var[:, :], var[:, :], ACT.Sqrt, bias=k.eps[:, :]).then_inc(std_done, 1)
                act.wait_ge(gap_done, 1)
                nc.scalar.activation(b[:, :], m2[:, :], ACT.Exp).then_inc(exped, 1)

            @block.vector
            def _(dve):
                link = Chain(dve, chain)
                dve.wait_ge(loaded, 48)
                link(nc.vector.tensor_scalar(rec[:, :, :], sums[:, 0:T, W:W + HEADS], 1e-16, None, ALU.add))
                link(nc.vector.reciprocal(rec[:, :, :], rec[:, :, :]))
                for j in range(HEADS):
                    link(nc.vector.tensor_tensor(v[:, :, j * E:(j + 1) * E], sums[:, 0:T, j * E:(j + 1) * E], bc(rec[:, :, j], E), ALU.mult))
                link(nc.vector.tensor_tensor(v[:, :, :], v[:, :, :], bc(row[0][:, :], T, 1), ALU.add))
                link(nc.vector.tensor_reduce(m1[:, :], v[:, :, :], AX.X, ALU.add))
                link(nc.vector.tensor_scalar(m1[:, :], m1[:, :], 1.0 / W, None, ALU.mult))
                link(nc.vector.tensor_tensor(v[:, :, :], v[:, :, :], bc(m1[:, :], W), ALU.subtract))
                link(nc.vector.tensor_tensor(sq[:, :, :], v[:, :, :], v[:, :, :], ALU.mult))
                link(nc.vector.tensor_reduce(var[:, :], sq[:, :, :], AX.X, ALU.add))
                link(nc.vector.tensor_scalar(var[:, :], var[:, :], 1.0 / W, None, ALU.mult))
                dve.sem_inc(var_done, 1)
                dve.wait_ge(std_done, 1)
                link(nc.vector.reciprocal(var[:, :], var[:, :]))
                link(nc.vector.tensor_tensor(v[:, :, :], v[:, :, :], bc(var[:, :], W), ALU.mult))
                link(nc.vector.tensor_tensor(v[:, :, :], v[:, :, :], bc(row[1][:, :], T, 1), ALU.mult))
                link(nc.vector.tensor_tensor(v[:, :, :], v[:, :, :], bc(row[2][:, :], T, 1), ALU.add))
                link(nc.vector.tensor_reduce(sc[:, :, :], v[:, :, :].rearrange("p t (h e) -> p t e h", h=HEADS), AX.X, ALU.add))
                link(nc.vector.tensor_scalar(sc[:, :, :], sc[:, :, :], 1.0 / HEADS, None, ALU.mult))
                link(nc.vector.tensor_scalar(order[:, :], k.iota[:, 0:E], -1.0, float(E), ALU.mult, ALU.add))
                for m, hot in ((m1, hot1), (m2, hot2)):
                    link(nc.vector.tensor_reduce(m[:, :], sc[:, :, :], AX.X, ALU.max))
                    link(nc.vector.tensor_tensor(pick[:, :, :], sc[:, :, :], bc(m[:, :], E), ALU.is_equal))
                    link(nc.vector.tensor_tensor(pick[:, :, :], pick[:, :, :], bc(order[:, :], T, 1), ALU.mult))
                    link(nc.vector.tensor_reduce(b[:, :], pick[:, :, :], AX.X, ALU.max))
                    link(nc.vector.tensor_tensor(hot[:, :, :], pick[:, :, :], bc(b[:, :], E), ALU.is_equal))
                    if m is m1:
                        link(nc.vector.scalar_tensor_tensor(sc[:, :, :], hot[:, :, :], -1e30, sc[:, :, :], ALU.mult, ALU.add))
                link(nc.vector.tensor_tensor(m2[:, :], m2[:, :], m1[:, :], ALU.subtract))
                dve.sem_inc(gap_done, 1)
                dve.wait_ge(exped, 1)
                link(nc.vector.tensor_scalar(m1[:, :], b[:, :], 1.0, None, ALU.add))
                link(nc.vector.reciprocal(m1[:, :], m1[:, :]))
                link(nc.vector.tensor_tensor(b[:, :], b[:, :], m1[:, :], ALU.mult))
                link(nc.vector.tensor_tensor(hot1[:, :, :], hot1[:, :, :], bc(m1[:, :], E), ALU.mult))
                link(nc.vector.tensor_tensor(hot2[:, :, :], hot2[:, :, :], bc(b[:, :], E), ALU.mult))
                link(nc.vector.tensor_tensor(gate[:, :, :], hot1[:, :, :], hot2[:, :, :], ALU.add))


def run_gated_experts(nc, k, a, x_old, f, gate, out):
    FC, W = GHID // P, GROUP * P // 2
    view = lambda v: v[0:NPAD, :].rearrange("(g j p) d -> g p j d", j=GROUP, p=P)
    at = lambda v, g: v[bass.ds(g, 1), :, :, :].rearrange("o p j d -> (o p) j d")
    xo, fv, ov = view(x_old), view(f), view(out)
    turns = GROUPS // 2
    with Stage(nc) as s:
        w1 = s.sb("w1", [P, GEXP, 2, GHID], F32)
        w2 = s.sb("w2", [P, GEXP, FC, D], F32)
        b1 = s.sb("b1", [P, GEXP, FC], F32)
        b2 = s.sb("b2", [P, GEXP, D], F32)
        x = [s.sb(f"x{h}", [P, GROUP, D], F32) for h in range(2)]
        fin = [s.sb(f"fin{h}", [P, GROUP, D], F32) for h in range(2)]
        ft = [s.sb(f"ft{h}", [P, 2, GROUP * P], F32) for h in range(2)]
        hid = [s.sb(f"hid{n}", [P, FC, GROUP * P], F32) for n in range(2)]
        ft_ps = [s.ps(f"ft_ps{n}", [P, 2, P]) for n in range(2)]
        hid_ps = [s.ps(f"hid_ps{n}", [P, 512]) for n in range(HB)]
        y_ps = [s.ps(f"y_ps{n}", [P, 512]) for n in range(YB)]
        go, weights, turned, copied, hid_mult, hid_done, y_mult, y_done, x_done, chain = (s.sem(n) for n in (
            "go", "weights", "turned", "copied", "hid_mult", "hid_done", "y_mult", "y_done", "x_done", "chain"))
        x_loaded, f_loaded, stored = ([s.sem(f"{n}{h}") for h in range(2)] for n in ("x_loaded", "f_loaded", "stored"))
        NH, NY, NT = GEXP * FC * 2, GEXP * GROUP, GROUP
        with nc.Block() as block:
            @block.sync
            def _(sp):
                sp.sem_inc(go, 1)
                for e in range(GEXP):
                    sp.dma_start(w1[:, e, :, :], a["L1_ffn_W1"][e, :, :].rearrange("(c p) f -> p c f", p=P)).then_inc(weights, 16)
                    sp.dma_start(w2[:, e, :, :], a["L1_ffn_W2"][e, :, :].rearrange("(c p) d -> p c d", p=P)).then_inc(weights, 16)
                    sp.dma_start(b1[:, e, :], a["L1_ffn_b1"][e, :].rearrange("(c p) -> p c", p=P), allow_slow_non_contiguous=True).then_inc(weights, 16)
                    sp.dma_start(b2[:, e, :], a["L1_ffn_b2"][e:e + 1, :].to_broadcast([P, D])).then_inc(weights, 16)

                def turn(i, again):
                    for h in range(2):
                        if again:
                            hold(sp, go, turned, (i * 2 + h - 1) * NT)
                        sp.dma_start(fin[h][:, :, :], at(fv, i * 2 + h)).then_inc(f_loaded[h], 16)
                        if again:
                            hold(sp, go, stored[h], i * 16)
                        sp.dma_start(x[h][:, :, :], at(xo, i * 2 + h)).then_inc(x_loaded[h], 16)

                turn(0, False)
                with sp.Fori(1, turns) as i:
                    turn(i, True)

            @block.gpsimd
            def _(pool):
                pool.wait_ge(go, 1)
                with pool.Fori(0, turns) as i:
                    for h in range(2):
                        hold(pool, go, x_done, i * 2 + h + 1)
                        pool.dma_start(at(ov, i * 2 + h), x[h][:, :, :]).then_inc(stored[h], 16)
                for h in range(2):
                    pool.wait_ge(stored[h], 16 * turns)

            @block.tensor
            def _(pe):
                pe.wait_ge(weights, 64 * GEXP)
                pe.wait_ge(go, 1)
                with pe.Fori(0, turns) as i:
                    for h in range(2):
                        nh, ny, nt = (i * 2 + h) * NH, (i * 2 + h) * NY, (i * 2 + h) * NT
                        pe.wait_ge(f_loaded[h], i * 16 + 16)
                        for j in range(GROUP):
                            pe.wait_ge(copied, nt + j + 1)
                            for c in range(2):
                                ins = nc.tensor.transpose(ft_ps[(h * GROUP + j) % 2][:, c, :], fin[h][:, j, c * P:(c + 1) * P], k.ident[:, :])
                            ins.then_inc(turned, 1)
                        pe.wait_ge(copied, nt + NT + 2)
                        for e in range(GEXP):
                            for c in range(FC):
                                for r in range(2):
                                    n = e * FC * 2 + c * 2 + r
                                    pe.wait_ge(hid_done, nh + n + 1)
                                    bank = hid_ps[(h * NH + n) % HB][:, 0:W]
                                    for d in range(2):
                                        ins = nc.tensor.matmul(bank, w1[:, e, d, c * P:(c + 1) * P], ft[h][:, d, r * W:(r + 1) * W], start=d == 0, stop=d == 1)
                                    ins.then_inc(hid_mult, 1)
                            for j in range(GROUP):
                                n = e * GROUP + j
                                pe.wait_ge(y_done, ny + n + 1)
                                if j == 0:
                                    pe.wait_ge(hid_done, nh + (e + 1) * FC * 2 + HB)
                                for c in range(FC):
                                    ins = nc.tensor.matmul(y_ps[(h * NY + n) % YB][:, 0:D], hid[e % 2][:, c, j * P:(j + 1) * P], w2[:, e, c, :],
                                                           start=c == 0, stop=c == FC - 1)
                                ins.then_inc(y_mult, 1)

            @block.scalar
            def _(act):
                act.sem_inc(hid_done, HB)
                act.wait_ge(weights, 64 * GEXP)
                act.wait_ge(go, 1)
                with act.Fori(0, turns) as i:
                    for h in range(2):
                        nh, ny = (i * 2 + h) * NH, (i * 2 + h) * NY
                        for e in range(GEXP):
                            for c in range(FC):
                                for r in range(2):
                                    n = e * FC * 2 + c * 2 + r
                                    act.wait_ge(hid_mult, nh + n + 1)
                                    nc.scalar.activation(hid[e % 2][:, c, r * W:(r + 1) * W], hid_ps[(h * NH + n) % HB][:, 0:W], ACT.Gelu,
                                                         bias=b1[:, e, c:c + 1]).then_inc(hid_done, 1)

            @block.vector
            def _(dve):
                dve.sem_inc(copied, 2)
                dve.sem_inc(y_done, YB)
                dve.wait_ge(weights, 64 * GEXP)
                dve.wait_ge(go, 1)
                with dve.Fori(0, turns) as i:
                    PER = 2 * GROUP * 2 * GEXP
                    link = Chain(dve, chain, i * PER, go)
                    for h in range(2):
                        ny, nt = (i * 2 + h) * NY, (i * 2 + h) * NT
                        for j in range(GROUP):
                            dve.wait_ge(turned, nt + j + 1)
                            nc.vector.tensor_copy(ft[h][:, :, j * P:(j + 1) * P], ft_ps[(h * GROUP + j) % 2][:, :, :]).then_inc(copied, 1)
                        hold(dve, go, x_loaded[h], i * 16 + 16)
                        for e in range(GEXP):
                            for j in range(GROUP):
                                g = gate[:, bass.ds((i * 2 + h) * GROUP + j, 1), e:e + 1].rearrange("p o e -> p (o e)")
                                link(nc.vector.scalar_tensor_tensor(x[h][:, j, :], b2[:, e, :], g, x[h][:, j, :], ALU.mult, ALU.add))
                            for j in range(GROUP):
                                n = e * GROUP + j
                                g = gate[:, bass.ds((i * 2 + h) * GROUP + j, 1), e:e + 1].rearrange("p o e -> p (o e)")
                                hold(dve, go, y_mult, ny + n + 1)
                                link(nc.vector.scalar_tensor_tensor(x[h][:, j, :], y_ps[(h * NY + n) % YB][:, 0:D], g, x[h][:, j, :], ALU.mult, ALU.add))
                                dve.sem_inc(y_done, 1)
                        dve.sem_inc(x_done, 1)
                    assert link.n == PER


HB, YB = 4, 2


def start_maxima(nc, k, mine, top):
    with Stage(nc) as s, nc.Block() as block:
        done = s.sem("done")

        @block.vector
        def _(dve):
            nc.vector.tensor_copy(top[:, 0:TILES, :], mine[:, :, HEADS * GEXP:HEADS * GEXP + HEADS]).then_inc(done, 1)
            nc.vector.memset(top[:, TILES, :], 0.0).then_inc(done, 1)


def pair_buffers(s, blocks):
    return Pairs(row=s.sb("row", [P, blocks * P], I32), place=s.sb("place", [P, blocks * P], F32),
                           weight=s.sb("weight", [P, blocks * P], F32), tile=s.sb("tile", [1, blocks * P], I32))


def program(nc, a, out, scratch):
    with ExitStack() as ctx:
        k = Kept()

        def const(name, shape, dt):
            return ctx.enter_context(nc.sbuf_tensor(name, shape, dt))

        k.iota_i = const("iota_i", [P, P], I32)
        k.iota = const("iota", [P, P], F32)
        k.ones = const("ones", [P, P], F32)
        k.ident = const("ident", [P, P], F32)
        k.ident_bf = const("ident_bf", [P, P], BF16)
        k.before = const("before", [P, P], F32)
        k.qcol_i = const("qcol_i", [P, EBLK], I32)
        k.qcol = const("qcol", [P, EBLK], F32)
        k.zero = const("zero", [P, D], F32)
        k.eps = const("eps", [P, 1], F32)
        constants(nc, k)
        f0 = scratch("f0", [NPAD + P, D], F32)
        layer_norm_in(nc, k, a["x"], f0)

        def plan(name, pairs, blocks, chunks):
            return Plan(pairs, blocks, chunks, scratch(f"tiles_{name}", [blocks * P], I32),
                        const(f"chunk_{name}", [P, blocks], I32), const(f"shift_{name}", [P, blocks], F32))

        plans = [plan("a", EPAIRS, EBLK, ECH), plan("e", EPAIRS, EBLK, ECH), plan("g", GPAIRS, GBLK, GCH)]
        sorted_e, sorted_g = scratch("sorted_e", [ECH * P, 4], F32), scratch("sorted_g", [GCH * P, 2], F32)
        edge_tables(nc, k, a, plans, sorted_e, sorted_g)
        by_target = Fields(rows=[a["dst"], a["src"], a["w"]], fields=[(0, 0, 1), (1, 0, 1), (2, 0, 1)])
        by_source = Fields(rows=[sorted_e.rearrange("(c e) f -> c (e f)", e=P)], fields=[(0, 1, 4), (0, 0, 4), (0, 2, 4)])
        k.w0t = const("w0t", [P, 2, D], F32)
        k.b0 = const("b0", [1, D], F32)
        k.gate_w = const("gate_w", [P, 2, EXPERTS], F32)
        k.gate_b = const("gate_b", [1, EXPERTS], F32)
        k.w1g = const("w1g", [P, 2, D], F32)
        k.big = const("big", [P, 1], F32)
        k.small = const("small", [P, 1], F32)
        k.send = const("send", [P, TILES], I32)
        k.fetch = const("fetch", [P, TILES], I32)
        k.scale = const("scale", [P, TILES], F32)
        turn_weights(nc, k, [(a["L0_gnn_W"], k.w0t)])
        row = lambda v: v.unsqueeze(0)
        halves = lambda v: v.rearrange("(c p) o -> p c o", p=P)
        load_small(nc, k, [(k.b0[:, :], row(a["L0_gnn_b"])), (k.gate_w[:, :, :], halves(a["L0_ffn_gate_w"])),
                           (k.gate_b[:, :], row(a["L0_ffn_gate_b"])), (k.w1g[:, :, :], halves(a["L1_gnn_W"]))])
        x1, x2 = scratch("x1", [NPAD, D], F32), scratch("x2", [NPAD, D], F32)
        f1 = scratch("f1", [NPAD, D], F32)
        with Stage(nc) as s:
            agg = s.sb("agg", [P, BUCKETS, D], F32)
            with Stage(nc) as s2:
                q = pair_buffers(s2, EBLK)
                pair_arrays(nc, k, plans[0], q, by_target)
                aggregate_edges(nc, k, f0, q, agg)
            with Stage(nc) as s2:
                logits = s2.sb("logits", [P, TILES, EXPERTS], F32)
                update_nodes(nc, k, Product(kind="product", sums=agg, w=k.w0t, bias=k.b0[:, :]), a["x"], x1, f1,
                             k.gate_w, EXPERTS, k.gate_b[:, :], logits)
                route_tokens(nc, k, logits, k.send, k.fetch, k.scale)
        xbuf, ybuf = scratch("xbuf", [EXPERTS * SLOTS, D], F32), scratch("ybuf", [EXPERTS * SLOTS, D], F32)
        dispatch_tokens(nc, k, f1, k.send, xbuf)
        run_experts(nc, k, xbuf, a["L0_ffn_w1"], a["L0_ffn_b1"], a["L0_ffn_w2"], a["L0_ffn_b2"], ybuf)
        h1 = scratch("h1", [NPAD + P, D], F32)
        load_small(nc, k, [(h1[NPAD:NPAD + P, :], k.zero[:, :])])
        update_nodes(nc, k, Routed(kind="experts", table=ybuf, rows=k.fetch, scale=k.scale), x1, x2, None,
                     k.w1g, D, None, h1)
        W = HEADS * GEXP
        k.gat_w = const("gat_w", [P, 2, W], F32)
        k.gate = const("gate", [P, TILES, GEXP], F32)
        load_small(nc, k, [(k.gat_w[:, :, :], halves(a["L1_ffn_W_gat"]))])
        x3, f3 = scratch("x3", [NPAD, D], F32), scratch("f3", [NPAD, D], F32)
        with Stage(nc) as s0:
            heads = s0.sb("heads", [P, TILES, W], F32)
            with Stage(nc) as s:
                agg = s.sb("agg1", [P, BUCKETS, D], F32)
                with Stage(nc) as s2:
                    q = pair_buffers(s2, EBLK)
                    pair_arrays(nc, k, plans[1], q, by_source)
                    aggregate_edges(nc, k, h1, q, agg)
                with Stage(nc) as s2:
                    gain, offset = s2.sb("gain", [P, D], F32), s2.sb("offset", [P, D], F32)
                    node_statistics(nc, k, agg, gain, offset, (a["L1_gnn_bias"], a["L1_gnn_gamma"], a["L1_gnn_beta"]))
                    update_nodes(nc, k, Normed(kind="batch_norm", sums=agg, gain=gain, offset=offset), x2, x3, f3,
                                 k.gat_w, W, None, heads)
            with Stage(nc) as s:
                table = scratch("gat", [NPAD, W + 4 * HEADS], F32)
                mine, target = s.sb("mine", [P, TILES, W + 4 * HEADS], F32), s.sb("target", [P, BUCKETS, HEADS], F32)
                top, score = s.sb("top", [P, BUCKETS, HEADS], F32), s.sb("score", [P, BUCKETS, 2 * HEADS], F32)
                sums = s.sb("sums", [P, BUCKETS, W + HEADS], F32)
                attention_table(nc, k, a, heads, mine, target, table)
                with Stage(nc) as s2:
                    q = pair_buffers(s2, GBLK)
                    fetched = s2.sb("fetched", [P, GPAIRS, W + HEADS], F32)
                    pair_arrays(nc, k, plans[2], q, Fields(rows=[sorted_g.rearrange("(c e) f -> c (e f)", e=P)],
                                                                     fields=[(0, 1, 2), (0, 0, 2)]))
                    start_maxima(nc, k, mine, top)
                    attend_maxima(nc, k, q, table, fetched, top)
                    attend_self(nc, k, mine, target, top, score, sums)
                    attend_sums(nc, k, q, fetched, score, sums)
                attention_gates(nc, k, a, sums, k.gate)
        run_gated_experts(nc, k, a, x3, f3, k.gate, out)


def kernel(**inputs):
    import numpy as np
    import concourse.bacc as bacc
    from concourse.bass_utils import run_bass_kernel_spmd

    def rows(name, n_rows, fill):
        v = np.ascontiguousarray(inputs[name]).reshape(-1)
        full = np.full(n_rows * P, fill, v.dtype)
        full[:v.size] = v
        return full.reshape(n_rows, P)

    nc = bacc.Bacc("TRN2", target_bir_lowering=False, num_devices=1)
    arrays = {}
    x = np.ascontiguousarray(inputs["x"])
    arrays["x"] = np.concatenate([x, np.zeros((NPAD - N, D), x.dtype)])
    arrays["src"] = rows("src", EROWS, NPAD)
    arrays["dst"] = rows("dst", EROWS, NPAD)
    arrays["w"] = rows("edge_weight", EROWS, 0)
    ge = np.ascontiguousarray(inputs["L1_ffn_edge_index"])
    arrays["gsrc"], arrays["gdst"] = ge[0].reshape(GCH, P), ge[1].reshape(GCH, P)
    for name in inputs:
        if name.startswith("L") and name != "L1_ffn_edge_index":
            arrays[name] = np.ascontiguousarray(inputs[name])
    a = {n: nc.dram_tensor(f"in_{n}", v.shape, mybir.dt.from_np(v.dtype), kind="ExternalInput").ap() for n, v in arrays.items()}
    out = nc.dram_tensor("out_x", (NPAD, D), F32, kind="ExternalOutput").ap()

    def scratch(name, shape, dt):
        return nc.dram_tensor(name, shape, dt, kind="Internal").ap()

    program(nc, a, out, scratch)
    r = run_bass_kernel_spmd(nc, [{f"in_{n}": v for n, v in arrays.items()}], core_ids=[0])
    return np.ascontiguousarray(r.results[0]["out_x"])[:N]
```

```python
import concourse.bass as bass
from concourse import mybir
from contextlib import ExitStack
from collections import namedtuple

F32, I32, BF16, U16 = mybir.dt.float32, mybir.dt.int32, mybir.dt.bfloat16, mybir.dt.uint16
ALU, ACT, AX = mybir.AluOpType, mybir.ActivationFunctionType, mybir.AxisListType

P = 128
N, D = 12500, 256
TILES = -(-N // P)
NPAD = TILES * P
BUCKETS = TILES + 1
GROUP = 7
GROUPS = TILES // GROUP
EDGES, GEDGES = 200000, 131072
LANES = 16
HALF = LANES // 2
BANKS, RING = 8, 4
ECH = -(-(-(-EDGES // P)) // LANES) * LANES
GCH = GEDGES // P
EROWS = -(-ECH // P) * P
EPAIRS = -(-(-(-EDGES // P) + TILES) // LANES) * LANES
GPAIRS = -(-(GCH + TILES) // LANES) * LANES
EBLK, GBLK = -(-EPAIRS // P), -(-GPAIRS // P)
EXPERTS, CAP, HID = 8, -(-5 * N // (4 * 8)), 1024
SLOTS = 2048
GEXP, GHID, HEADS = 4, 512, 4
LN_EPS = BN_EPS = 1e-5


Plan = namedtuple("Plan", "pairs blocks chunks tiles chunk shift")
Fields = namedtuple("Fields", "rows fields")
Pairs = namedtuple("Pairs", "row place weight tile")
Product = namedtuple("Product", "kind sums w bias")
Routed = namedtuple("Routed", "kind table rows scale")
Normed = namedtuple("Normed", "kind sums gain offset")


class Kept:
    pass


class Stage:

    def __init__(self, nc):
        self.nc, self.ctx, self.sems = nc, ExitStack(), []

    def sb(self, name, shape, dt):
        return self.ctx.enter_context(self.nc.sbuf_tensor(f"{name}_{self.nc.next_id()}", shape, dt))

    def ps(self, name, shape, dt=F32):
        return self.ctx.enter_context(self.nc.psum_tensor(f"{name}_{self.nc.next_id()}", shape, dt))

    def sem(self, name):
        s = self.nc.alloc_semaphore(f"{name}_{self.nc.next_id()}")
        self.sems.append(s)
        return s

    def __enter__(self):
        return self

    def __exit__(self, *exc):
        if exc[0] is None:
            if self.sems:
                self.nc.clear_and_free_semaphores(self.sems)
            self.nc.all_engine_barrier()
        self.ctx.close()


class Chain:

    def __init__(self, eng, sem, base=0, once=None):
        self.eng, self.sem, self.base, self.n, self.once = eng, sem, base, 0, once

    def __call__(self, *instructions):
        for ins in instructions:
            ins.then_inc(self.sem, 1)
        self.n += len(instructions)
        if self.once is None:
            self.eng.wait_ge(self.sem, self.base + self.n)
        else:
            hold(self.eng, self.once, self.sem, self.base + self.n)


def hold(eng, once, sem, value):
    reg = eng.to_reg(value)
    eng.wait_ge(once, 1)
    eng.wait_ge(sem, reg)


def load_tiles(nc, eng, q, first, regs):
    for four in range(0, len(regs), 4):
        eng.reg_load(regs[four:four + 4], q.tile[0:1, bass.ds(first + four, 4)])
    return [nc.s_assert_within(eng.snap(r), 0, BUCKETS - 1, skip_runtime_bounds_check_because="a tile counts buckets begun before a pair, of which the first is left out")
            for r in regs]


def bc(ap, n, axis=2):
    a = ap.unsqueeze(axis)
    shape = list(a.shape)
    shape[axis] = n
    return a.to_broadcast(shape)


def constants(nc, k):
    with Stage(nc) as s, nc.Block() as block:
        done = s.sem("constants_done")

        @block.gpsimd
        def _(pool):
            n = [0]

            def link(ins):
                n[0] += 1
                ins.then_inc(done, 1)
                pool.wait_ge(done, n[0])

            link(nc.gpsimd.iota(k.iota_i[:, :], pattern=[[1, P]], base=0, channel_multiplier=0))
            link(nc.gpsimd.tensor_copy(k.iota[:, :], k.iota_i[:, :]))
            link(nc.gpsimd.memset(k.ones[:, :], 1.0))
            link(nc.gpsimd.memset(k.ident[:, :], 0.0))
            link(nc.gpsimd.affine_select(out=k.ident[:, :], in_=k.ident[:, :], compare_op=ALU.not_equal, fill=1.0,
                                         base=0, pattern=[[-1, P]], channel_multiplier=1))
            link(nc.gpsimd.affine_select(out=k.before[:, :], in_=k.ones[:, :], compare_op=ALU.is_gt, fill=0.0,
                                         base=0, pattern=[[1, P]], channel_multiplier=-1))
            link(nc.gpsimd.iota(k.qcol_i[:, :], pattern=[[P, EBLK]], base=0, channel_multiplier=1))
            link(nc.gpsimd.tensor_copy(k.qcol[:, :], k.qcol_i[:, :]))
            link(nc.gpsimd.tensor_copy(k.ident_bf[:, :], k.ident[:, :]))
            link(nc.gpsimd.memset(k.eps[:, :], LN_EPS))
            nc.gpsimd.memset(k.zero[:, :], 0.0).then_inc(done, 1)


def layer_norm_in(nc, k, x, f):
    xv = x.rearrange("(g j p) d -> g p j d", j=GROUP, p=P)
    fv = f[0:NPAD, :].rearrange("(g j p) d -> g p j d", j=GROUP, p=P)
    with Stage(nc) as s:
        xin = [s.sb(f"xin{h}", [P, GROUP, D], F32) for h in range(2)]
        fout = [s.sb(f"fout{h}", [P, GROUP, D], F32) for h in range(2)]
        stats, mv = s.sb("stats", [P, GROUP, 6], F32), s.sb("mv", [P, GROUP, 2], F32)
        std, rstd = s.sb("std", [P, GROUP], F32), s.sb("rstd", [P, GROUP], F32)
        loaded = [s.sem(f"loaded{h}") for h in range(2)]
        stored = [s.sem(f"stored{h}") for h in range(2)]
        normed, chain, var_done, std_done, zeros = (s.sem(n) for n in ("normed", "chain", "var_done", "std_done", "zeros"))
        PER = 2 * (3 * GROUP + 1)
        with nc.Block() as block:
            @block.sync
            def _(sp):
                sp.dma_start(f[NPAD:NPAD + P, :], k.zero[:, :]).then_inc(zeros, 16)
                sp.sem_inc(normed, 2)
                with sp.Fori(0, GROUPS // 2) as i:
                    for h in range(2):
                        hold(sp, normed, normed, i * 2 + h + 1)
                        sp.dma_start(xin[h][:, :, :], xv[bass.ds(i * 2 + h, 1), :, :, :].rearrange("o p j d -> (o p) j d")).then_inc(loaded[h], 16)

            @block.vector
            def _(dve):
                def turn(i, again):
                    link = Chain(dve, chain, i * PER, normed)
                    for h in range(2):
                        hold(dve, normed, loaded[h], i * 16 + 16)
                        for j in range(GROUP):
                            link(nc.vector.bn_stats(stats[:, j, :], xin[h][:, j, :]))
                            link(nc.vector.bn_aggr(mv[:, j, :], stats[:, j, :]))
                        dve.sem_inc(var_done, 1)
                        dve.wait_ge(std_done, i * 2 + h + 1)
                        link(nc.vector.reciprocal(rstd[:, :], std[:, :]))
                        if again:
                            hold(dve, normed, stored[h], i * 16)
                        for j in range(GROUP):
                            link(nc.vector.tensor_scalar(fout[h][:, j, :], xin[h][:, j, :], mv[:, j, 0:1], rstd[:, j:j + 1], ALU.subtract, ALU.mult))
                        dve.sem_inc(normed, 1)
                    assert link.n == PER

                turn(0, False)
                with dve.Fori(1, GROUPS // 2) as i:
                    turn(i, True)

            @block.scalar
            def _(act):
                act.wait_ge(zeros, 16)
                with act.Fori(0, GROUPS // 2) as i:
                    for h in range(2):
                        act.wait_ge(var_done, i * 2 + h + 1)
                        nc.scalar.activation(std[:, :], mv[:, :, 1], ACT.Sqrt, bias=k.eps[:, :]).then_inc(std_done, 1)
                        hold(act, normed, normed, i * 2 + h + 3)
                        act.dma_start(fv[bass.ds(i * 2 + h, 1), :, :, :].rearrange("o p j d -> (o p) j d"), fout[h][:, :, :]).then_inc(stored[h], 16)
                for h in range(2):
                    act.wait_ge(stored[h], GROUPS // 2 * 16)


def edge_ranks(nc, k, a, plans, rec_e, rec_g, pos_e, pos_g, xbuf, scatter):
    B = BUCKETS
    with Stage(nc) as s:
        fields = [(a["dst"], rec_e, 0, ECH), (a["src"], rec_e, 1, ECH), (a["w"], rec_e, 2, ECH),
                  (a["gsrc"], rec_g, 0, GCH), (a["gdst"], rec_g, 1, GCH)]
        raw = [s.sb(f"raw{n}", [P, -(-c // P), P], src.tensor.dtype if n == 2 else I32) for n, (src, _, _, c) in enumerate(fields)]
        asf = s.sb("asf", [P, EROWS], F32)
        key_i = s.sb("key_i", [P, ECH], I32)
        keys = [s.sb("key_a", [P, ECH], BF16), s.sb("key_e", [P, ECH], BF16), s.sb("key_g", [P, GCH], BF16)]
        hit = s.sb("hit", [P, 3, ECH], BF16)
        mask = [s.sb(f"mask{n}", [P, ECH], U16) for n in range(2)]
        posf = [s.sb(f"posf{n}", [P, c], F32) for n, c in enumerate((GCH, ECH))]
        cnt = s.sb("cnt", [P, 3, B], F32)
        prior = s.sb("prior", [P, 3, B], F32)
        tot, start, first, last, pairs, begin, rel, drel = (s.sb(n, [P, 3, B], F32) for n in ("tot", "start", "first", "last", "pairs", "begin", "rel", "drel"))
        whole = s.sb("whole", [P, 3, B], I32)
        sel = s.sb("sel", [P, B], F32)
        tcol, ccol = s.sb("tcol", [P, 3, EBLK], F32), s.sb("ccol", [P, 3, EBLK], F32)
        tint = s.sb("tint", [P, 3, EBLK], I32)
        turned = [s.ps(f"turned{n}", [P, P]) for n in range(2)]
        ranks = s.ps("ranks", [P, 4 * 512])
        sums = s.ps("sums", [P, 3 * B])
        loaded = [s.sem(f"loaded{n}") for n in range(len(fields))]
        converted, transposed, copied, chain, counted, summed, stored, marked, scanned, taken, ranked = (s.sem(n) for n in (
            "converted", "transposed", "copied", "chain", "counted", "summed", "stored", "marked", "scanned", "taken", "ranked"))
        zeroed = s.sem("zeroed")
        scatter.place(s)
        steps = [(n, b) for n, (_, _, _, c) in enumerate(fields) for b in range(-(-c // P))]
        with nc.Block() as block:
            @block.sync
            def _(sp):
                for n, (src, _, _, c) in enumerate(fields):
                    nb = -(-c // P)
                    sp.dma_start(raw[n][:, :, :], src[0:nb * P, :].rearrange("(b p) e -> p b e", p=P)).then_inc(loaded[n], 16)
                sp.dma_start(xbuf.rearrange("(p r) d -> p r d", p=P), bc(k.zero[:, :], EXPERTS * SLOTS // P, 1)).then_inc(zeroed, 16)
                sp.wait_ge(chain, 1)
                sp.wait_ge(stored, 1)
                for n in range(3):
                    sp.dma_start(plans[n].tiles.rearrange("(b p) -> p b", p=P), tint[:, n, 0:plans[n].blocks],
                                 allow_slow_non_contiguous=True).then_inc(stored, 16)
                sp.wait_ge(stored, 49)
                sp.wait_ge(zeroed, 16)

            @block.tensor
            def _(pe):
                for i, (n, b) in enumerate(steps):
                    c = min(P, fields[n][3] - b * P)
                    pe.wait_ge(converted, n + 1)
                    if i >= 2:
                        pe.wait_ge(copied, i - 1)
                    nc.tensor.transpose(turned[i % 2][:, 0:c], asf[0:c, b * P:(b + 1) * P], k.ident[0:c, 0:c]).then_inc(transposed, 1)
                pe.wait_ge(counted, 1)
                flat = cnt[:, :, :].rearrange("p n b -> p (n b)")
                nc.tensor.matmul(sums[:, :], k.ones[:, :], flat, start=True, stop=True).then_inc(summed, 1)
                pe.wait_ge(counted, 2)
                nc.tensor.matmul(sums[:, :], k.before[:, :], flat, start=True, stop=True).then_inc(summed, 1)

            @block.vector
            def _(dve):
                link = Chain(dve, chain)
                i = 0
                for n, (_, rec, f, c) in enumerate(fields):
                    nb = -(-c // P)
                    dve.wait_ge(loaded[n], 16)
                    if i:
                        dve.wait_ge(transposed, i)
                    nc.vector.tensor_copy(asf[:, 0:nb * P], raw[n][:, :, :].rearrange("p b e -> p (b e)")).then_inc(converted, 1)
                    for b in range(nb):
                        m = min(P, c - b * P)
                        dve.wait_ge(transposed, i + 1)
                        nc.vector.tensor_copy(rec[:, b * P:b * P + m, f], turned[i % 2][:, 0:m]).then_inc(copied, 1)
                        i += 1
                dve.wait_ge(copied, i)
                for key, src, c in ((keys[0], rec_e[:, :, 0], ECH), (keys[1], rec_e[:, :, 1], ECH), (keys[2], rec_g[:, :, 1], GCH)):
                    link(nc.vector.tensor_copy(key_i[:, 0:c], src))
                    link(nc.vector.tensor_scalar(key_i[:, 0:c], key_i[:, 0:c], 7, None, ALU.arith_shift_right))
                    link(nc.vector.tensor_copy(key[:, :], key_i[:, 0:c]))
                at = link.n
                with dve.Fori(0, B) as b:
                    turn = Chain(dve, chain, b * 3 + at, converted)
                    turn(*[nc.vector.tensor_scalar(hit[:, n, 0:c], keys[n][:, :], k.iota[:, bass.ds(b, 1)], None, ALU.is_equal, ALU.add,
                                                   accum_out=cnt[:, n, bass.ds(b, 1)]) for n, c in enumerate((ECH, ECH, GCH))])
                link.n = at + 3 * B
                dve.sem_inc(counted, 1)
                dve.wait_ge(summed, 1)
                link(nc.vector.tensor_copy(tot[:, :, :].rearrange("p n b -> p (n b)"), sums[:, :]))
                dve.sem_inc(counted, 1)
                dve.wait_ge(summed, 2)
                link(nc.vector.tensor_copy(prior[:, :, :].rearrange("p n b -> p (n b)"), sums[:, :]))
                for n in range(3):
                    link(nc.vector.tensor_tensor_scan(start[:, n, :], tot[:, n, :], tot[:, n, :], 0.0, ALU.add, ALU.bypass))
                link(nc.vector.tensor_tensor(start[:, :, :], start[:, :, :], tot[:, :, :], ALU.subtract))
                link(nc.vector.tensor_copy(whole[:, :, :], start[:, :, :]))
                link(nc.vector.tensor_scalar(whole[:, :, :], whole[:, :, :], 7, None, ALU.arith_shift_right))
                link(nc.vector.tensor_copy(first[:, :, :], whole[:, :, :]))
                link(nc.vector.tensor_tensor(last[:, :, :], start[:, :, :], tot[:, :, :], ALU.add))
                link(nc.vector.tensor_scalar(whole[:, :, :], last[:, :, :], -1.0, None, ALU.add))
                link(nc.vector.tensor_scalar(whole[:, :, :], whole[:, :, :], 7, None, ALU.arith_shift_right))
                link(nc.vector.tensor_copy(last[:, :, :], whole[:, :, :]))
                link(nc.vector.tensor_tensor(last[:, :, :], last[:, :, :], first[:, :, :], ALU.subtract))
                link(nc.vector.tensor_scalar(pairs[:, :, :], tot[:, :, :], 0.0, None, ALU.is_gt))
                link(nc.vector.scalar_tensor_tensor(pairs[:, :, :], last[:, :, :], 1.0, pairs[:, :, :], ALU.add, ALU.mult))
                for n in range(3):
                    link(nc.vector.tensor_tensor_scan(begin[:, n, :], pairs[:, n, :], pairs[:, n, :], 0.0, ALU.add, ALU.bypass))
                link(nc.vector.tensor_tensor(begin[:, :, :], begin[:, :, :], pairs[:, :, :], ALU.subtract))
                link(nc.vector.tensor_tensor(rel[:, :, :], first[:, :, :], begin[:, :, :], ALU.subtract))
                link(nc.vector.tensor_copy(drel[:, :, 0:1], rel[:, :, 0:1]))
                link(nc.vector.tensor_tensor(drel[:, :, 1:B], rel[:, :, 1:B], rel[:, :, 0:B - 1], ALU.subtract))
                for n in range(3):
                    for q in range(plans[n].blocks):
                        link(nc.vector.tensor_scalar(sel[:, 1:B], begin[:, n, 1:B], k.qcol[:, q:q + 1], None, ALU.is_le, ALU.add,
                                                     accum_out=tcol[:, n, q:q + 1]))
                        link(nc.vector.scalar_tensor_tensor(sel[:, :], begin[:, n, :], k.qcol[:, q:q + 1], drel[:, n, :], ALU.is_le, ALU.mult,
                                                            accum_out=ccol[:, n, q:q + 1]))
                    m = plans[n].blocks
                    link(nc.vector.tensor_tensor(ccol[:, n, 0:m], ccol[:, n, 0:m], k.qcol[:, 0:m], ALU.add))
                    link(nc.vector.tensor_scalar(plans[n].chunk[:, 0:m], ccol[:, n, 0:m], float(plans[n].chunks - 1), None, ALU.min))
                    link(nc.vector.tensor_scalar(plans[n].shift[:, 0:m], tcol[:, n, 0:m], float(P), None, ALU.mult))
                    link(nc.vector.tensor_copy(tint[:, n, 0:m], tcol[:, n, 0:m]))
                dve.sem_inc(stored, 1)
                link(nc.vector.scalar_tensor_tensor(prior[:, :, :], start[:, :, :], -1.0, prior[:, :, :], ALU.add, ALU.add))
                for order, (n, c, pos) in enumerate(((2, GCH, pos_g), (1, ECH, pos_e))):
                    def mark(b, h):
                        nc.vector.tensor_scalar(mask[h][:, 0:c], keys[n][:, :], k.iota[:, bass.ds(b, 1)], None, ALU.is_equal).then_inc(marked, 1)

                    def rank(b, h, ahead):
                        hold(dve, converted, marked, order * B + b + 1)
                        hold(dve, converted, taken, order * B + b + 1)
                        nc.vector.tensor_tensor_scan(ranks[:, 0:c], mask[h][:, 0:c], mask[h][:, 0:c], prior[:, n, bass.ds(b, 1)],
                                                     ALU.add, ALU.bypass).then_inc(scanned, 1)
                        if ahead:
                            mark(b + 1, 1 - h)
                        hold(dve, converted, scanned, order * B + b + 1)
                        nc.vector.copy_predicated(posf[order][:, 0:c], mask[h][:, 0:c], ranks[:, 0:c]).then_inc(taken, 1)

                    if order == 0:
                        dve.sem_inc(taken, 1)
                    mark(0, 0)
                    with dve.Fori(0, B // 2) as i:
                        for h in range(2):
                            rank(i * 2 + h, h, True)
                    assert B % 2 == 1
                    rank(B - 1, 0, False)
                    dve.wait_ge(taken, (order + 1) * B + 1)
                    link(nc.vector.tensor_copy(pos[:, :], posf[order][:, 0:c]))
                    dve.sem_inc(ranked, 1)

            @block.gpsimd
            def _(pool):
                pool.wait_ge(ranked, 1)
                scatter_records(nc, pool, scatter)


class Scatter:

    def __init__(self, rec, pos, dest, width, first, turns):
        self.rec, self.pos, self.dest, self.width, self.first, self.turns = rec, pos, dest, width, first, turns

    def place(self, s):
        self.idx = s.sb("idx_s", [P, LANES], I32)
        self.pay = s.sb("pay_s", [P, LANES, self.width], F32)
        self.staged, self.ready = s.sem("staged_s"), s.sem("ready_s")
        self.landed = [s.sem(f"landed_s{h}") for h in range(2)]


def scatter_turn(nc, pool, w, i, again):
    for h in range(2):
        lo = slice(h * HALF, (h + 1) * HALF)
        chunks = bass.ds((i + w.first) * LANES + h * HALF, HALF)
        if again:
            hold(pool, w.ready, w.landed[h], i * (16 * HALF))
        nc.gpsimd.tensor_copy(w.idx[:, lo], w.pos[:, chunks]).then_inc(w.staged, 1)
        nc.gpsimd.tensor_copy(w.pay[:, lo, :], w.rec[:, chunks, :]).then_inc(w.staged, 1)
        hold(pool, w.ready, w.staged, i * 4 + 2 * h + 2)
        for u in range(h * HALF, (h + 1) * HALF):
            pool.indirect_dma_start(out=w.dest, out_offset=bass.IndirectOffsetOnAxis(ap=w.idx[:, u:u + 1], axis=0),
                                    in_=w.pay[:, u, :], in_offset=None).then_inc(w.landed[h], 16)


def scatter_records(nc, pool, w):
    pool.sem_inc(w.ready, 1)
    scatter_turn(nc, pool, w, 0, False)
    with pool.Fori(1, w.turns) as i:
        scatter_turn(nc, pool, w, i, True)
    scatter_end(pool, w)


def scatter_end(pool, w):
    for h in range(2):
        pool.wait_ge(w.landed[h], 16 * HALF * w.turns)


def pair_arrays(nc, k, plan, q, sources):
    with Stage(nc) as s:
        nb = plan.blocks
        got = [s.sb(f"got{n}", [P, nb, r.shape[1]], r.tensor.dtype) for n, r in enumerate(sources.rows)]
        asf = s.sb("asf", [P, 2, 3, P], F32)
        turned = [s.ps(f"turned{n}", [P, 3, P]) for n in range(2)]
        gathered, made, transposed, copied, tiles = (s.sem(n) for n in ("gathered", "made", "transposed", "copied", "tiles"))
        nf = len(sources.fields)
        with nc.Block() as block:
            @block.gpsimd
            def _(pool):
                for b in range(nb):
                    for n, r in enumerate(sources.rows):
                        pool.indirect_dma_start(out=got[n][:, b, :], out_offset=None, in_=r,
                                                in_offset=bass.IndirectOffsetOnAxis(ap=plan.chunk[:, b:b + 1], axis=0)).then_inc(gathered, 16)

            @block.sync
            def _(sp):
                sp.dma_start(q.tile[0:1, 0:nb * P], plan.tiles.unsqueeze(0)).then_inc(tiles, 16)
                sp.wait_ge(tiles, 16)

            @block.vector
            def _(dve):
                dve.wait_ge(gathered, 16 * nb * len(sources.rows))
                for b in range(nb):
                    if b >= 2:
                        dve.wait_ge(transposed, nf * (b - 1))
                    for f, (n, first, step) in enumerate(sources.fields):
                        src = got[n][:, b, first:first + (P - 1) * step + 1:step]
                        if f == 0:
                            ins = nc.vector.tensor_scalar(asf[:, b % 2, f, :], src, plan.shift[:, b:b + 1], None, ALU.subtract)
                        else:
                            ins = nc.vector.tensor_copy(asf[:, b % 2, f, :], src)
                        ins.then_inc(made, 1)
                    dve.wait_ge(transposed, nf * (b + 1))
                    for f, dest in enumerate((q.place, q.row, q.weight)[:nf]):
                        nc.vector.tensor_copy(dest[:, b * P:(b + 1) * P], turned[b % 2][:, f, :]).then_inc(copied, 1)

            @block.tensor
            def _(pe):
                for b in range(nb):
                    if b >= 2:
                        pe.wait_ge(copied, nf * (b - 1))
                    for f in range(nf):
                        pe.wait_ge(made, nf * b + f + 1)
                        nc.tensor.transpose(turned[b % 2][:, f, :], asf[:, b % 2, f, :], k.ident[:, :]).then_inc(transposed, 1)


def aggregate_edges(nc, k, table, q, agg):
    turns = EPAIRS // (RING * BANKS)
    SPAN = RING * BANKS
    with Stage(nc) as s:
        idx = s.sb("idx", [P, SPAN], I32)
        rows = s.sb("rows", [P, SPAN, D], F32)
        spread = s.sb("spread", [P, 2 * BANKS, P], F32)
        part = s.ps("part", [P, BANKS, 512])
        gathered = [s.sem(f"gathered{u}") for u in range(SPAN)]
        ready, staged, spread_done, multiplied, added = (s.sem(n) for n in ("ready", "staged", "spread_done", "multiplied", "added"))
        with nc.Block() as block:
            @block.gpsimd
            def _(pool):
                pool.wait_ge(ready, 1)
                with pool.Fori(0, turns) as i:
                    for r in range(RING):
                        hold(pool, ready, multiplied, (i * RING + r + 1) * BANKS)
                        nc.gpsimd.tensor_copy(idx[:, r * BANKS:(r + 1) * BANKS], q.row[:, bass.ds((i * RING + r) * BANKS, BANKS)]).then_inc(staged, 1)
                        hold(pool, ready, staged, i * RING + r + 1)
                        for u in range(r * BANKS, (r + 1) * BANKS):
                            pool.indirect_dma_start(out=rows[:, u, :], out_offset=None, in_=table,
                                                    in_offset=bass.IndirectOffsetOnAxis(ap=idx[:, u:u + 1], axis=0)).then_inc(gathered[u], 16)

            @block.vector
            def _(dve):
                def spread_weights(g, h):
                    for u in range(BANKS):
                        nc.vector.tensor_scalar(spread[:, h * BANKS + u, :], k.iota[:, :], q.place[:, bass.ds(g * BANKS + u, 1)],
                                                q.weight[:, bass.ds(g * BANKS + u, 1)], ALU.is_equal, ALU.mult).then_inc(spread_done, 1)

                regs = [dve.alloc_register(f"tile{n}_{nc.next_id()}") for n in range(4)]

                def add(g):
                    for u in range(BANKS):
                        if u % 4 == 0:
                            tiles = load_tiles(nc, dve, q, g * BANKS + u, regs)
                            hold(dve, ready, multiplied, (g + RING) * BANKS + u + 4)
                        sum_t = agg[:, bass.ds(tiles[u % 4], 1), :].rearrange("p o d -> p (o d)")
                        dve.wait_ge(added, (g + 1) * BANKS + u)
                        nc.vector.tensor_tensor(sum_t, sum_t, part[:, u, 0:D], ALU.add).then_inc(added, 1)

                nc.vector.memset(agg[:, :, :], 0.0).then_inc(ready, 1)
                dve.wait_ge(ready, 1)
                dve.sem_inc(added, BANKS)
                spread_weights(0, 0)
                with dve.Fori(0, EPAIRS // (2 * BANKS) - 1) as i:
                    for h in range(2):
                        spread_weights(i * 2 + h + 1, 1 - h)
                        add(i * 2 + h)
                last = EPAIRS // BANKS - 1
                spread_weights(last, 1)
                add(last - 1)
                add(last)

            @block.tensor
            def _(pe):
                pe.wait_ge(ready, 1)
                pe.sem_inc(multiplied, RING * BANKS)
                with pe.Fori(0, turns) as i:
                    for u in range(SPAN):
                        pe.wait_ge(spread_done, i * SPAN + u + 1)
                        pe.wait_ge(added, i * SPAN + u + 1)
                        pe.wait_ge(gathered[u], i * 16 + 16)
                        nc.tensor.matmul(part[:, u % BANKS, 0:D], spread[:, u % (2 * BANKS), :], rows[:, u, :], start=True, stop=True).then_inc(multiplied, 1)


def turn_weights(nc, k, pairs):
    with Stage(nc) as s:
        nat = s.sb("nat", [P, 2, D], F32)
        turned = [s.ps(f"turned{n}", [P, P]) for n in range(2)]
        loaded, transposed, copied = s.sem("loaded"), s.sem("transposed"), s.sem("copied")
        with nc.Block() as block:
            @block.sync
            def _(sp):
                for n, (w, _) in enumerate(pairs):
                    if n:
                        sp.wait_ge(transposed, 4 * n)
                    sp.dma_start(nat[:, :, :], w.rearrange("(c p) i -> p c i", p=P)).then_inc(loaded, 16)

            @block.tensor
            def _(pe):
                for m in range(4 * len(pairs)):
                    c, i = m % 4 // 2, m % 2
                    pe.wait_ge(loaded, 16 * (m // 4 + 1))
                    if m >= 2:
                        pe.wait_ge(copied, m - 1)
                    nc.tensor.transpose(turned[m % 2][:, :], nat[:, c, i * P:(i + 1) * P], k.ident[:, :]).then_inc(transposed, 1)

            @block.vector
            def _(dve):
                for m in range(4 * len(pairs)):
                    c, i = m % 4 // 2, m % 2
                    dve.wait_ge(transposed, m + 1)
                    nc.vector.tensor_copy(pairs[m // 4][1][:, i, c * P:(c + 1) * P], turned[m % 2][:, :]).then_inc(copied, 1)


def load_small(nc, k, loads):
    with Stage(nc) as s, nc.Block() as block:
        loaded = s.sem("loaded")

        @block.sync
        def _(sp):
            for sbuf, dram in loads:
                sp.dma_start(sbuf, dram).then_inc(loaded, 16)
            sp.wait_ge(loaded, 16 * len(loads))


def update_nodes(nc, k, head, x_old, x_new, f_new, w, width, bias, result, scatter=None):
    rows = lambda v: v[0:NPAD, :].rearrange("(g j p) d -> g p j d", j=GROUP, p=P)
    at = lambda v, g: v[bass.ds(g, 1), :, :, :].rearrange("o p j d -> (o p) j d")
    xo, xn = rows(x_old), rows(x_new)
    fn = rows(f_new) if f_new is not None else None
    res_dram = rows(result) if width == D else None
    product = head.kind == "product"
    PT = 2 * GROUP * (2 if product else 1)
    NH = {"product": GROUP, "experts": 8, "batch_norm": 3}[head.kind]
    PER = 2 * (NH + 3 * GROUP + 1)
    with Stage(nc) as s:
        if scatter:
            scatter.place(s)
        x = [s.sb(f"x{h}", [P, GROUP, D], F32) for h in range(2)]
        f = [s.sb(f"f{h}", [P, GROUP, D], F32) for h in range(2)]
        part = s.sb("part", [P, GROUP, D], F32) if head.kind != "experts" else None
        xt = [s.sb(f"xt{n}", [P, 2, P], F32) for n in range(2)]
        res = s.sb("res", [P, 2, GROUP, D], F32) if width == D else None
        stats, mv = s.sb("stats", [P, GROUP, 6], F32), s.sb("mv", [P, GROUP, 2], F32)
        std, rstd = s.sb("std", [P, GROUP], F32), s.sb("rstd", [P, GROUP], F32)
        if head.kind == "experts":
            y = [s.sb(f"y{h}", [P, GROUP, D], F32) for h in range(2)]
            idx = s.sb("idx", [P, 2, GROUP], I32)
            clean, odd = s.sb("clean", [P, GROUP, D], F32), s.sb("odd", [P, GROUP, D], U16)
        xt_ps = [s.ps(f"xt_ps{n}", [P, 2, P]) for n in range(2)]
        head_ps = [s.ps(f"head_ps{n}", [P, D]) for n in range(2)]
        tail_ps = [s.ps(f"tail_ps{n}", [P, D]) for n in range(2)]
        (go, x_done, f_done, chain, var_done, std_done, part_done, transposed, turned, head_done, head_used, tail_done,
         tail_used, staged, odd_go) = (s.sem(n) for n in (
             "go", "x_done", "f_done", "chain", "var_done", "std_done", "part_done", "transposed", "turned", "head_done",
             "head_used", "tail_done", "tail_used", "staged", "odd_go"))
        loaded, x_stored, f_stored, r_stored, fetched = ([s.sem(f"{n}{h}") for h in range(2)] for n in (
            "loaded", "x_stored", "f_stored", "r_stored", "fetched"))
        turns = GROUPS // 2
        with nc.Block() as block:
            @block.sync
            def _(sp):
                sp.wait_ge(go, 1)

                def turn(i, again):
                    for h in range(2):
                        if again:
                            hold(sp, go, x_stored[h], i * 16)
                            hold(sp, go, f_done, (i * 2 + h - 1) * GROUP)
                        sp.dma_start(x[h][:, :, :], at(xo, i * 2 + h)).then_inc(loaded[h], 16)
                    for h in range(2):
                        hold(sp, go, x_done, i * 2 + h + 1)
                        sp.dma_start(at(xn, i * 2 + h), x[h][:, :, :]).then_inc(x_stored[h], 16)
                        if fn is not None:
                            hold(sp, go, f_done, (i * 2 + h + 1) * GROUP)
                            sp.dma_start(at(fn, i * 2 + h), f[h][:, :, :]).then_inc(f_stored[h], 16)
                        if res is not None:
                            hold(sp, go, tail_used, (i * 2 + h + 1) * GROUP + 2)
                            sp.dma_start(at(res_dram, i * 2 + h), res[:, h, :, :]).then_inc(r_stored[h], 16)

                turn(0, False)
                with sp.Fori(1, turns) as i:
                    turn(i, True)
                for h in range(2):
                    sp.wait_ge(x_stored[h], 16 * turns)
                    if fn is not None:
                        sp.wait_ge(f_stored[h], 16 * turns)
                    if res is not None:
                        sp.wait_ge(r_stored[h], 16 * turns)

            if head.kind == "experts":
                @block.gpsimd
                def _(pool):
                    pool.wait_ge(go, 1)

                    def turn(i, again):
                        for h in range(2):
                            if again:
                                hold(pool, go, x_done, i * 2 + h - 1)
                            nc.gpsimd.tensor_copy(idx[:, h, :], head.rows[:, bass.ds((i * 2 + h) * GROUP, GROUP)]).then_inc(staged, 1)
                            hold(pool, go, staged, i * 2 + h + 1)
                            for j in range(GROUP):
                                pool.indirect_dma_start(out=y[h][:, j, :], out_offset=None, in_=head.table,
                                                        in_offset=bass.IndirectOffsetOnAxis(ap=idx[:, h, j:j + 1], axis=0)).then_inc(fetched[h], 16)
                            for r in range(2 - h):
                                scatter_turn(nc, pool, scatter, i * 3 + h * 2 + r, again or h or r)

                    assert scatter.turns == 3 * turns
                    pool.sem_inc(scatter.ready, 1)
                    turn(0, False)
                    with pool.Fori(1, turns) as i:
                        turn(i, True)
                    scatter_end(pool, scatter)
            elif scatter:
                @block.gpsimd
                def _(pool):
                    scatter_records(nc, pool, scatter)

            @block.tensor
            def _(pe):
                pe.wait_ge(go, 1)
                with pe.Fori(0, turns) as i:
                    m = 0

                    def multiply(src, src_ready, value, weights, out, done, used, used_value, row):
                        nonlocal m
                        pe.wait_ge(src_ready, value)
                        pe.wait_ge(turned, i * PT + m + 1)
                        for c in range(2):
                            ins = nc.tensor.transpose(xt_ps[m % 2][:, c, :], src[:, c * P:(c + 1) * P], k.ident[:, :])
                        ins.then_inc(transposed, 1)
                        pe.wait_ge(used, used_value)
                        pe.wait_ge(turned, i * PT + m + 3)
                        if row is not None:
                            nc.tensor.matmul(out, k.ones[0:1, :], row, start=True, stop=False)
                        nc.tensor.matmul(out, xt[m % 2][:, 0, :], weights[:, 0, :], start=row is None, stop=False)
                        nc.tensor.matmul(out, xt[m % 2][:, 1, :], weights[:, 1, :], start=False, stop=True).then_inc(done, 1)
                        m += 1

                    for h in range(2):
                        for j in range(GROUP if product else 0):
                            n = h * GROUP + j
                            multiply(part[:, j, :], part_done, i * 2 + h + 1, head.w, head_ps[n % 2][:, :], head_done,
                                     head_used, i * 2 * GROUP + n + 1, head.bias)
                        for j in range(GROUP):
                            n = h * GROUP + j
                            multiply(f[h][:, j, :], f_done, i * 2 * GROUP + n + 1, w, tail_ps[n % 2][:, 0:width], tail_done,
                                     tail_used, i * 2 * GROUP + n + 1, bias)
                    assert m == PT

            @block.scalar
            def _(act):
                act.sem_inc(turned, 2)
                act.sem_inc(tail_used, 2)
                act.sem_inc(go, 1)

                def turn(i, again):
                    m = 0

                    def copy_turned():
                        nonlocal m
                        act.wait_ge(transposed, i * PT + m + 1)
                        nc.scalar.activation(xt[m % 2][:, :, :], xt_ps[m % 2][:, :, :], ACT.Copy).then_inc(turned, 1)
                        m += 1

                    for h in range(2):
                        if product:
                            if again or h:
                                hold(act, go, head_done, (i * 2 + h) * GROUP)
                            nc.scalar.activation(part[:, :, :], head.sums[:, bass.ds((i * 2 + h) * GROUP, GROUP), :], ACT.Copy).then_inc(part_done, 1)
                            for j in range(GROUP):
                                copy_turned()
                        act.wait_ge(var_done, i * 2 + h + 1)
                        nc.scalar.activation(std[:, :], mv[:, :, 1], ACT.Sqrt, bias=k.eps[:, :]).then_inc(std_done, 1)
                        for j in range(GROUP):
                            n = h * GROUP + j
                            copy_turned()
                            if res is not None:
                                if again and j == 0:
                                    hold(act, go, r_stored[h], i * 16)
                                act.wait_ge(tail_done, i * 2 * GROUP + n + 1)
                                nc.scalar.activation(res[:, h, j, :], tail_ps[n % 2][:, :], ACT.Copy).then_inc(tail_used, 1)
                            else:
                                hold(act, go, tail_done, i * 2 * GROUP + n + 1)
                                nc.scalar.activation(result[:, bass.ds(i * 2 * GROUP + n, 1), :].rearrange("p o w -> p (o w)"),
                                                     tail_ps[n % 2][:, 0:width], ACT.Copy).then_inc(tail_used, 1)

                turn(0, False)
                with act.Fori(1, turns) as i:
                    turn(i, True)

            @block.vector
            def _(dve):
                dve.sem_inc(head_used, 2)
                dve.wait_ge(go, 1)
                if head.kind == "experts":
                    nc.vector.memset(k.big[:, :], 1e4).then_inc(odd_go, 1)
                    nc.vector.memset(k.small[:, :], -1e4).then_inc(odd_go, 1)
                    dve.wait_ge(odd_go, 2)

                def turn(i, again):
                    link = Chain(dve, chain, i * PER, go)
                    for h in range(2):
                        hold(dve, go, loaded[h], i * 16 + 16)
                        xh = x[h]
                        if product:
                            for j in range(GROUP):
                                n = h * GROUP + j
                                dve.wait_ge(head_done, i * 2 * GROUP + n + 1)
                                ins = nc.vector.tensor_tensor(xh[:, j, :], head_ps[n % 2][:, :], xh[:, j, :], ALU.add)
                                link(ins)
                                dve.sem_inc(head_used, 1)
                        elif head.kind == "experts":
                            g = (i * 2 + h) * GROUP
                            hold(dve, go, fetched[h], (i + 1) * 16 * GROUP)
                            yh = y[h][:, :, :]
                            link(nc.vector.tensor_tensor(yh, yh, bc(head.scale[:, bass.ds(g, GROUP)], D), ALU.mult))
                            link(nc.vector.tensor_tensor(odd[:, :, :], yh, yh, ALU.is_equal))
                            link(nc.vector.memset(clean[:, :, :], 0.0))
                            link(nc.vector.copy_predicated(clean[:, :, :], odd[:, :, :], yh))
                            link(nc.vector.tensor_scalar(odd[:, :, :], clean[:, :, :], FLT_MAX, None, ALU.is_gt))
                            link(nc.vector.copy_predicated(clean[:, :, :], odd[:, :, :], k.big[:, 0:1].unsqueeze(2).to_broadcast([P, GROUP, D])))
                            link(nc.vector.tensor_scalar(odd[:, :, :], clean[:, :, :], -FLT_MAX, None, ALU.is_lt))
                            nc.vector.copy_predicated(clean[:, :, :], odd[:, :, :], k.small[:, 0:1].unsqueeze(2).to_broadcast([P, GROUP, D])).then_inc(odd_go, 1)
                            hold(dve, go, odd_go, i * 2 + h + 3)
                            link(nc.vector.tensor_tensor(xh[:, :, :], xh[:, :, :], clean[:, :, :], ALU.add))
                        else:
                            sums = head.sums[:, bass.ds((i * 2 + h) * GROUP, GROUP), :]
                            link(nc.vector.tensor_tensor(part[:, :, :], sums, bc(head.gain[:, :], GROUP, 1), ALU.mult))
                            link(nc.vector.tensor_tensor(part[:, :, :], part[:, :, :], bc(head.offset[:, :], GROUP, 1), ALU.add))
                            link(nc.vector.scalar_tensor_tensor(xh[:, :, :], part[:, :, :], 0.0, xh[:, :, :], ALU.max, ALU.add))
                        dve.sem_inc(x_done, 1)
                        for j in range(GROUP):
                            link(nc.vector.bn_stats(stats[:, j, :], xh[:, j, :]))
                            link(nc.vector.bn_aggr(mv[:, j, :], stats[:, j, :]))
                        dve.sem_inc(var_done, 1)
                        dve.wait_ge(std_done, i * 2 + h + 1)
                        link(nc.vector.reciprocal(rstd[:, :], std[:, :]))
                        if again:
                            if fn is not None:
                                hold(dve, go, f_stored[h], i * 16)
                            hold(dve, go, tail_done, (i * 2 + h - 1) * GROUP)
                        for j in range(GROUP):
                            link(nc.vector.tensor_scalar(f[h][:, j, :], xh[:, j, :], mv[:, j, 0:1], rstd[:, j:j + 1], ALU.subtract, ALU.mult))
                            dve.sem_inc(f_done, 1)
                    assert link.n == PER, (link.n, PER)

                turn(0, False)
                with dve.Fori(1, turns) as i:
                    turn(i, True)


FLT_MAX = 3.4028234663852886e38


def route_tokens(nc, k, logits, send, fetch, scale):
    T, E = TILES, EXPERTS
    with Stage(nc) as s:
        prob, hot, rank, run, tot = (s.sb(n, [P, T, E], F32) for n in ("prob", "hot", "rank", "run", "tot"))
        top, best, kept, place = (s.sb(n, [P, T], F32) for n in ("top", "best", "kept", "place"))
        ranks = s.ps("ranks", [P, 2, 512])
        tots = s.ps("tots", [P, 2, 512])
        order = s.sb("order", [P, E], F32)
        chain, shifted, exped, hot_done, counted = (s.sem(n) for n in ("chain", "shifted", "exped", "hot_done", "counted"))
        half = T // 2 * E
        with nc.Block() as block:
            @block.scalar
            def _(act):
                act.wait_ge(shifted, 1)
                nc.scalar.activation(prob[:, :, :], prob[:, :, :], ACT.Exp).then_inc(exped, 1)

            @block.tensor
            def _(pe):
                pe.wait_ge(hot_done, 1)
                for c in range(2):
                    rhs = hot[:, c * T // 2:(c + 1) * T // 2, :].rearrange("p t e -> p (t e)")
                    nc.tensor.matmul(ranks[:, c, 0:half], k.before[:, :], rhs, start=True, stop=True)
                    nc.tensor.matmul(tots[:, c, 0:half], k.ones[:, :], rhs, start=True, stop=True).then_inc(counted, 1)

            @block.vector
            def _(dve):
                link = Chain(dve, chain)
                link(nc.vector.tensor_reduce(top[:, :], logits[:, :, :], AX.X, ALU.max))
                link(nc.vector.tensor_tensor(prob[:, :, :], logits[:, :, :], bc(top[:, :], E), ALU.subtract))
                dve.sem_inc(shifted, 1)
                dve.wait_ge(exped, 1)
                link(nc.vector.tensor_reduce(top[:, :], prob[:, :, :], AX.X, ALU.add))
                link(nc.vector.reciprocal(top[:, :], top[:, :]))
                link(nc.vector.tensor_tensor(prob[:, :, :], prob[:, :, :], bc(top[:, :], E), ALU.mult))
                link(nc.vector.tensor_reduce(top[:, :], prob[:, :, :], AX.X, ALU.max))
                link(nc.vector.tensor_tensor(hot[:, :, :], prob[:, :, :], bc(top[:, :], E), ALU.is_equal))
                link(nc.vector.tensor_scalar(order[:, :], k.iota[:, 0:E], -1.0, float(E), ALU.mult, ALU.add))
                link(nc.vector.tensor_tensor(prob[:, :, :], hot[:, :, :], bc(order[:, :], T, 1), ALU.mult))
                link(nc.vector.tensor_reduce(best[:, :], prob[:, :, :], AX.X, ALU.max))
                link(nc.vector.tensor_tensor(hot[:, :, :], prob[:, :, :], bc(best[:, :], E), ALU.is_equal))
                dve.sem_inc(hot_done, 1)
                dve.wait_ge(counted, 2)
                for c in range(2):
                    sl = slice(c * T // 2, (c + 1) * T // 2)
                    link(nc.vector.tensor_copy(rank[:, sl, :].rearrange("p t e -> p (t e)"), ranks[:, c, 0:half]))
                    link(nc.vector.tensor_copy(tot[:, sl, :].rearrange("p t e -> p (t e)"), tots[:, c, 0:half]))
                for e in range(E):
                    link(nc.vector.tensor_tensor_scan(run[:, :, e], tot[:, :, e], tot[:, :, e], 0.0, ALU.add, ALU.bypass))
                link(nc.vector.tensor_tensor(run[:, :, :], run[:, :, :], tot[:, :, :], ALU.subtract))
                link(nc.vector.tensor_tensor(rank[:, :, :], rank[:, :, :], run[:, :, :], ALU.add))
                link(nc.vector.tensor_tensor(rank[:, :, :], rank[:, :, :], hot[:, :, :], ALU.mult))
                link(nc.vector.tensor_reduce(place[:, :], rank[:, :, :], AX.X, ALU.add))
                link(nc.vector.tensor_scalar(kept[:, :], place[:, :], float(CAP), None, ALU.is_lt))
                link(nc.vector.tensor_tensor(scale[:, :], top[:, :], kept[:, :], ALU.mult))
                link(nc.vector.tensor_scalar(best[:, :], best[:, :], -float(SLOTS), float(E * SLOTS), ALU.mult, ALU.add))
                link(nc.vector.scalar_tensor_tensor(fetch[:, :], place[:, :], float(CAP - 1), best[:, :], ALU.min, ALU.add))
                link(nc.vector.tensor_scalar(kept[:, :], kept[:, :], -float(E * SLOTS), float(E * SLOTS), ALU.mult, ALU.add))
                link(nc.vector.tensor_tensor(place[:, :], place[:, :], best[:, :], ALU.add))
                link(nc.vector.tensor_tensor(send[:, :], place[:, :], kept[:, :], ALU.add))


def dispatch_tokens(nc, k, f, send, dest):
    fv = f[0:NPAD, :].rearrange("(g j p) d -> g p j d", j=GROUP, p=P)
    with Stage(nc) as s:
        rows = [s.sb(f"rows{h}", [P, GROUP, D], F32) for h in range(2)]
        idx = s.sb("idx", [P, 2, GROUP], I32)
        staged, go = s.sem("staged"), s.sem("go")
        loaded, sent = ([s.sem(f"{n}{h}") for h in range(2)] for n in ("loaded", "sent"))
        turns = GROUPS // 2
        with nc.Block() as block:
            @block.sync
            def _(sp):
                def turn(i, again):
                    for h in range(2):
                        if again:
                            hold(sp, go, sent[h], i * 16 * GROUP)
                        sp.dma_start(rows[h][:, :, :], fv[bass.ds(i * 2 + h, 1), :, :, :].rearrange("o p j d -> (o p) j d")).then_inc(loaded[h], 16)

                turn(0, False)
                with sp.Fori(1, turns) as i:
                    turn(i, True)

            @block.gpsimd
            def _(pool):
                pool.sem_inc(go, 1)

                def turn(i, again):
                    for h in range(2):
                        if again:
                            hold(pool, go, sent[h], i * 16 * GROUP)
                        nc.gpsimd.tensor_copy(idx[:, h, :], send[:, bass.ds((i * 2 + h) * GROUP, GROUP)]).then_inc(staged, 1)
                        hold(pool, go, staged, i * 2 + h + 1)
                        hold(pool, go, loaded[h], i * 16 + 16)
                        for j in range(GROUP):
                            pool.indirect_dma_start(out=dest, out_offset=bass.IndirectOffsetOnAxis(ap=idx[:, h, j:j + 1], axis=0),
                                                    in_=rows[h][:, j, :], in_offset=None,
                                                    bounds_check=EXPERTS * SLOTS - 1, oob_is_err=False).then_inc(sent[h], 16)

                turn(0, False)
                with pool.Fori(1, turns) as i:
                    turn(i, True)
                for h in range(2):
                    pool.wait_ge(sent[h], turns * 16 * GROUP)


def run_experts(nc, k, xbuf, w1, b1, w2, b2, ybuf, scatter):
    W, FC, BLOCKS = 512, HID // P, SLOTS // 512
    xv = xbuf.rearrange("(e b c p) d -> e b p c d", p=P, c=4, b=BLOCKS)
    yv = ybuf.rearrange("(g c p) d -> g p c d", p=P, c=4)
    one = lambda v, e: v[bass.ds(e, 1), :, :, :].rearrange("o p c d -> (o p) c d")
    with Stage(nc) as s:
        scatter.place(s)
        w1s = [s.sb(f"w1s{n}", [P, 2, HID], F32) for n in range(2)]
        w2s = [s.sb(f"w2s{n}", [P, FC, D], F32) for n in range(2)]
        b1s = [s.sb(f"b1s{n}", [P, FC], F32) for n in range(2)]
        b2s = [s.sb(f"b2s{n}", [1, D], F32) for n in range(2)]
        x = [s.sb(f"x{n}", [P, 4, D], F32) for n in range(2)]
        xt = [s.sb(f"xt{n}", [P, 2, W], F32) for n in range(2)]
        hid = [s.sb(f"hid{n}", [P, FC, W], F32) for n in range(2)]
        y = [s.sb(f"y{n}", [P, 4, D], F32) for n in range(2)]
        xt_ps = [s.ps(f"xt_ps{c}", [P, W]) for c in range(2)]
        hid_ps = [s.ps(f"hid_ps{n}", [P, W]) for n in range(4)]
        y_ps = [s.ps(f"y_ps{n}", [P, 512]) for n in range(2)]
        weights, x_loaded, y_stored = ([s.sem(f"{n}{h}") for h in range(2)] for n in ("weights", "x_loaded", "y_stored"))
        go, turned, xt_done, hid_mult, hid_done, y_mult, y_done, b1_ok = (s.sem(n) for n in (
            "go", "turned", "xt_done", "hid_mult", "hid_done", "y_mult", "y_done", "b1_ok"))
        NB = 2 * BLOCKS
        turns = EXPERTS // 2
        with nc.Block() as block:
            @block.sync
            def _(sp):
                def turn(i, again):
                    for n in range(2):
                        e = i * 2 + n
                        if again:
                            hold(sp, go, y_mult, (i * NB - NB + (n + 1) * BLOCKS) * 4)
                        pick = lambda v: v[bass.ds(e, 1)]
                        sp.dma_start(w1s[n][:, :, :], pick(w1).rearrange("o (c p) f -> (o p) c f", p=P)).then_inc(weights[n], 16)
                        sp.dma_start(w2s[n][:, :, :], pick(w2).rearrange("o (c p) d -> (o p) c d", p=P)).then_inc(weights[n], 16)
                        sp.dma_start(b1s[n][:, :], pick(b1).rearrange("o (c p) -> (o p) c", p=P), allow_slow_non_contiguous=True).then_inc(weights[n], 16)
                        sp.dma_start(b2s[n][:, :], pick(b2)).then_inc(weights[n], 16)
                        for b in range(BLOCKS):
                            m = n * BLOCKS + b
                            if again or m >= 2:
                                hold(sp, go, turned, (i * NB + m - 1) * 2)
                            sp.dma_start(x[m % 2][:, :, :], one(xv[:, b, :, :, :], e)).then_inc(x_loaded[m % 2], 16)
                            if again or m >= 2:
                                store(i * NB + m - 2, m % 2)

                def store(g, h):
                    hold(sp, go, y_done, g * 4 + 6)
                    sp.dma_start(yv[bass.ds(g, 1), :, :, :].rearrange("o p c d -> (o p) c d"), y[h][:, :, :]).then_inc(y_stored[h], 16)

                turn(0, False)
                with sp.Fori(1, turns) as i:
                    turn(i, True)
                for h in range(2):
                    store(turns * NB - 2 + h, h)
                for h in range(2):
                    sp.wait_ge(y_stored[h], 16 * (NB // 2) * turns)

            @block.tensor
            def _(pe):
                pe.wait_ge(go, 1)
                with pe.Fori(0, turns) as i:
                    for m in range(NB):
                        n = m // BLOCKS
                        pe.wait_ge(x_loaded[m % 2], i * (16 * NB // 2) + 16 * (m // 2 + 1))
                        pe.wait_ge(xt_done, (i * NB + m) * 2 + 2)
                        for c in range(2):
                            for r in range(4):
                                ins = nc.tensor.transpose(xt_ps[c][:, r * P:(r + 1) * P], x[m % 2][:, r, c * P:(c + 1) * P], k.ident[:, :])
                            ins.then_inc(turned, 1)
                        pe.wait_ge(xt_done, (i * NB + m) * 2 + 4)
                        pe.wait_ge(weights[n], i * 64 + 64)
                        for fc in range(FC):
                            pe.wait_ge(hid_done, (i * NB + m) * FC + fc + 1)
                            for c in range(2):
                                ins = nc.tensor.matmul(hid_ps[fc % 4][:, :], w1s[n][:, c, fc * P:(fc + 1) * P], xt[m % 2][:, c, :],
                                                       start=c == 0, stop=c == 1)
                            ins.then_inc(hid_mult, 1)
                        for r in range(4):
                            pe.wait_ge(y_done, (i * NB + m) * 4 + r + 1)
                            out = y_ps[r % 2][:, 0:D]
                            nc.tensor.matmul(out, k.ones[0:1, :], b2s[n][:, :], start=True, stop=False)
                            for fc in range(FC):
                                if r == 0:
                                    pe.wait_ge(hid_done, (i * NB + m) * FC + fc + 5)
                                ins = nc.tensor.matmul(out, hid[m % 2][:, fc, r * P:(r + 1) * P], w2s[n][:, fc, :], start=False, stop=fc == FC - 1)
                            ins.then_inc(y_mult, 1)

            @block.scalar
            def _(act):
                act.sem_inc(hid_done, 4)
                act.sem_inc(go, 1)

                with act.Fori(0, turns) as i:
                    for m in range(NB):
                        n = m // BLOCKS
                        hold(act, go, weights[n], i * 64 + 64)
                        for fc in range(FC):
                            act.wait_ge(hid_mult, (i * NB + m) * FC + fc + 1)
                            nc.scalar.activation(hid[m % 2][:, fc, :], hid_ps[fc % 4][:, :], ACT.Relu, bias=b1s[n][:, fc:fc + 1]).then_inc(hid_done, 1)

            @block.vector
            def _(dve):
                dve.sem_inc(xt_done, 2)
                dve.sem_inc(y_done, 2)
                dve.wait_ge(go, 1)

                def turn(i, again):
                    for m in range(NB):
                        for c in range(2):
                            dve.wait_ge(turned, (i * NB + m) * 2 + c + 1)
                            nc.vector.tensor_copy(xt[m % 2][:, c, :], xt_ps[c][:, :]).then_inc(xt_done, 1)
                        if again or m >= 2:
                            hold(dve, go, y_stored[m % 2], i * (16 * NB // 2) + 16 * (m // 2))
                        for r in range(4):
                            dve.wait_ge(y_mult, (i * NB + m) * 4 + r + 1)
                            nc.vector.tensor_copy(y[m % 2][:, r, :], y_ps[r % 2][:, 0:D]).then_inc(y_done, 1)

                turn(0, False)
                with dve.Fori(1, turns) as i:
                    turn(i, True)

            @block.gpsimd
            def _(pool):
                scatter_records(nc, pool, scatter)


def node_statistics(nc, k, sums, gain, offset, params, scatter):
    bias, gamma, beta = params
    turns = GROUPS // 2
    with Stage(nc) as s:
        scatter.place(s)
        mean, var, std, tmp = (s.sb(n, [P, D], F32) for n in ("mean", "var", "std", "tmp"))
        dev = [s.sb(f"dev{h}", [P, GROUP, D], F32) for h in range(2)]
        rows = [s.sb(f"row{n}", [P, D], F32) for n in range(3)]
        last = s.sb("last", [P, P], F32)
        sum_ps, sq_ps = s.ps("sum_ps", [P, 512]), s.ps("sq_ps", [P, 512])
        loaded, go, summed, dev_done, squared, used, chain, var_done, std_done, mask_done = (s.sem(n) for n in (
            "loaded", "go", "summed", "dev_done", "squared", "used", "chain", "var_done", "std_done", "mask_done"))
        with nc.Block() as block:
            @block.sync
            def _(sp):
                for r, v in zip(rows, params):
                    sp.dma_start(r[:, :], v.unsqueeze(0).to_broadcast([P, D])).then_inc(loaded, 16)

            @block.gpsimd
            def _(pool):
                nc.gpsimd.affine_select(out=last[:, :], in_=k.ones[:, :], compare_op=ALU.is_gt, fill=0.0,
                                        base=N - (TILES - 1) * P, pattern=[[0, P]], channel_multiplier=-1).then_inc(mask_done, 1)
                scatter_records(nc, pool, scatter)

            @block.tensor
            def _(pe):
                pe.wait_ge(go, 1)
                out = sum_ps[:, 0:D]
                nc.tensor.matmul(out, k.ones[:, :], sums[:, 0, :], start=True, stop=False)
                with pe.Fori(1, TILES - 1) as t:
                    nc.tensor.matmul(out, k.ones[:, :], sums[:, bass.ds(t, 1), :].rearrange("p o d -> p (o d)"), start=False, stop=False)
                nc.tensor.matmul(out, k.ones[:, :], sums[:, TILES - 1, :], start=False, stop=True).then_inc(summed, 1)
                pe.wait_ge(mask_done, 1)

                def turn(i, first, end):
                    for h in range(2):
                        pe.wait_ge(squared, i * 2 + h + 1)
                        for j in range(GROUP):
                            is_last = end and h == 1 and j == GROUP - 1
                            ins = nc.tensor.matmul(sq_ps[:, 0:D], (last if is_last else k.ones)[:, :], dev[h][:, j, :],
                                                   start=first and h == 0 and j == 0, stop=is_last)
                        ins.then_inc(used, 1)

                turn(0, True, False)
                with pe.Fori(1, turns - 1) as i:
                    turn(i, False, False)
                turn(turns - 1, False, True)

            @block.scalar
            def _(act):
                act.sem_inc(go, 1)
                with act.Fori(0, turns) as i:
                    for h in range(2):
                        act.wait_ge(dev_done, i * 2 + h + 1)
                        nc.scalar.activation(dev[h][:, :, :], dev[h][:, :, :], ACT.Square).then_inc(squared, 1)
                act.wait_ge(var_done, 1)
                nc.scalar.activation(std[:, :], var[:, :], ACT.Sqrt, bias=k.eps[:, :]).then_inc(std_done, 1)

            @block.vector
            def _(dve):
                link = Chain(dve, chain)
                dve.wait_ge(go, 1)
                dve.wait_ge(loaded, 48)
                dve.wait_ge(summed, 1)
                link(nc.vector.tensor_scalar(mean[:, :], sum_ps[:, 0:D], 1.0 / N, None, ALU.mult))

                def turn(i, again):
                    for h in range(2):
                        if again:
                            hold(dve, go, used, i * 2 + h - 1)
                        nc.vector.tensor_tensor(dev[h][:, :, :], sums[:, bass.ds((i * 2 + h) * GROUP, GROUP), :], bc(mean[:, :], GROUP, 1),
                                                ALU.subtract).then_inc(dev_done, 1)

                turn(0, False)
                with dve.Fori(1, turns) as i:
                    turn(i, True)
                dve.wait_ge(used, 2 * turns)
                link(nc.vector.tensor_scalar(var[:, :], sq_ps[:, 0:D], 1.0 / N, None, ALU.mult))
                dve.sem_inc(var_done, 1)
                dve.wait_ge(std_done, 1)
                link(nc.vector.reciprocal(std[:, :], std[:, :]))
                link(nc.vector.tensor_tensor(gain[:, :], std[:, :], rows[1][:, :], ALU.mult))
                link(nc.vector.tensor_tensor(mean[:, :], mean[:, :], rows[0][:, :], ALU.add))
                link(nc.vector.tensor_tensor(tmp[:, :], rows[0][:, :], mean[:, :], ALU.subtract))
                link(nc.vector.tensor_tensor(tmp[:, :], tmp[:, :], gain[:, :], ALU.mult))
                link(nc.vector.tensor_tensor(offset[:, :], tmp[:, :], rows[2][:, :], ALU.add))


def attention_table(nc, k, a, heads, mine, target, table):
    W = HEADS * GEXP
    with Stage(nc) as s:
        att = [s.sb(f"att{n}", [P, W], F32) for n in range(2)]
        prod = s.sb("prod", [P, TILES, W], F32)
        rounded, rest = s.sb("rounded", [P, TILES, HEADS], BF16), s.sb("rest", [P, TILES, HEADS], F32)
        loaded, chain, made, stored = (s.sem(n) for n in ("loaded", "chain", "made", "stored"))
        with nc.Block() as block:
            @block.sync
            def _(sp):
                for r, name in zip(att, ("L1_ffn_att_src", "L1_ffn_att_dst")):
                    sp.dma_start(r[:, :], a[name].rearrange("h e -> (h e)").unsqueeze(0).to_broadcast([P, W])).then_inc(loaded, 16)
                sp.wait_ge(made, 1)
                sp.dma_start(table.rearrange("(t p) w -> p t w", p=P), mine[:, :, :]).then_inc(stored, 16)
                sp.wait_ge(stored, 16)

            @block.vector
            def _(dve):
                link = Chain(dve, chain)
                dve.wait_ge(loaded, 32)
                link(nc.vector.tensor_copy(mine[:, :, 0:W], heads[:, :, :]))
                for r, dest in zip(att, (mine[:, :, W:W + HEADS], target[:, 0:TILES, :])):
                    link(nc.vector.tensor_tensor(prod[:, :, :], heads[:, :, :], bc(r[:, :], TILES, 1), ALU.mult))
                    link(nc.vector.tensor_reduce(dest, prod[:, :, :].rearrange("p t (h e) -> p t h e", h=HEADS), AX.X, ALU.add))
                link(nc.vector.memset(target[:, TILES, :], 0.0))
                left, first = mine[:, :, W:W + HEADS], W + HEADS
                for c in range(3):
                    part = mine[:, :, first + c * HEADS:first + (c + 1) * HEADS]
                    link(nc.vector.tensor_copy(rounded[:, :, :], left))
                    link(nc.vector.tensor_copy(part, rounded[:, :, :]))
                    if c < 2:
                        link(nc.vector.tensor_tensor(rest[:, :, :], left, part, ALU.subtract))
                        left = rest[:, :, :]
                dve.sem_inc(made, 1)


def attend_maxima(nc, k, q, table, fetched, top):
    turns = GPAIRS // LANES
    W, S = HEADS * GEXP, 3 * HEADS
    with Stage(nc) as s:
        idx = s.sb("idx", [P, LANES], I32)
        rows = s.sb("rows", [P, LANES, W + HEADS + S], F32)
        score = [s.sb(f"score{h}", [P, HALF, S], BF16) for h in range(2)]
        score_t = [s.sb(f"score_t{h}", [HALF * S, P], BF16) for h in range(2)]
        pick = s.sb("pick", [HALF * S, HALF, HEADS], BF16)
        far = s.sb("far", [P, P], BF16)
        away = s.sb("away", [P, LANES, P], BF16)
        top_p = s.sb("top_p", [P, LANES, HEADS], F32)
        score_ps = [s.ps(f"score_ps{h}", [HALF * S, 1024], BF16) for h in range(2)]
        all_ps = [s.ps(f"all_ps{n}", [P, HEADS, P]) for n in range(4)]
        gathered = [s.sem(f"gathered{u}") for u in range(LANES)]
        go, staged, taken, turned, copied, away_done, listed, chain, used, drained = (s.sem(n) for n in (
            "go", "staged", "taken", "turned", "copied", "away_done", "listed", "chain", "used", "drained"))
        with nc.Block() as block:
            @block.gpsimd
            def _(pool):
                pool.wait_ge(go, 2)
                with pool.Fori(0, turns) as i:
                    for h in range(2):
                        hold(pool, go, taken, i * 2 + h + 1)
                        nc.gpsimd.tensor_copy(idx[:, h * HALF:(h + 1) * HALF], q.row[:, bass.ds(i * LANES + h * HALF, HALF)]).then_inc(staged, 1)
                        hold(pool, go, staged, i * 2 + h + 1)
                        for u in range(h * HALF, (h + 1) * HALF):
                            pool.indirect_dma_start(out=rows[:, u, :], out_offset=None, in_=table,
                                                    in_offset=bass.IndirectOffsetOnAxis(ap=idx[:, u:u + 1], axis=0)).then_inc(gathered[u], 16)

            @block.scalar
            def _(act):
                act.sem_inc(taken, 2)
                act.sem_inc(copied, 2)
                act.wait_ge(go, 2)
                with act.Fori(0, turns) as i:
                    for h in range(2):
                        half = rows[:, h * HALF:(h + 1) * HALF, :]
                        for u in range(h * HALF, (h + 1) * HALF):
                            hold(act, go, gathered[u], i * 16 + 16)
                        nc.scalar.activation(fetched[:, bass.ds(i * LANES + h * HALF, HALF), :], half[:, :, 0:W + HEADS], ACT.Copy).then_inc(drained, 1)
                        act.wait_ge(drained, i * 2 + h + 1)
                        nc.scalar.activation(score[h][:, :, :], half[:, :, W + HEADS:], ACT.Copy).then_inc(taken, 1)
                        act.wait_ge(turned, i * 2 + h + 1)
                        hold(act, go, listed, (i * 2 + h + 1) * HALF)
                        nc.scalar.activation(score_t[h][:, :], score_ps[h][:, 0:P], ACT.Copy).then_inc(copied, 1)

            @block.tensor
            def _(pe):
                pe.sem_inc(listed, 2 * HALF)
                pe.wait_ge(go, 2)
                with pe.Fori(0, turns) as i:
                    for h in range(2):
                        pe.wait_ge(taken, i * 2 + h + 3)
                        pe.wait_ge(copied, i * 2 + h + 1)
                        nc.tensor.transpose(score_ps[h][:, 0:P], score[h][:, :, :].rearrange("p u s -> p (u s)"), k.ident_bf[:, :]).then_inc(turned, 1)
                        pe.wait_ge(copied, i * 2 + h + 3)
                        for v in range(HALF):
                            u = h * HALF + v
                            pe.wait_ge(used, i * LANES + u + 1)
                            if v == 0:
                                pe.wait_ge(away_done, i * 2 + h + 1)
                            for j in range(HEADS):
                                nc.tensor.matmul(all_ps[u % 4][:, j, :], pick[:, v, j:j + 1].to_broadcast([HALF * S, P]), score_t[h][:, :],
                                                 start=j == 0, stop=False)
                            nc.tensor.matmul(all_ps[u % 4][:, :, :], away[:, u, :], bc(far[:, :], HEADS, 1), start=False, stop=True).then_inc(listed, 1)

            @block.vector
            def _(dve):
                def mark(g, h):
                    nc.vector.tensor_tensor(away[:, h * HALF:(h + 1) * HALF, :], bc(k.iota[:, :], HALF, 1), bc(q.place[:, bass.ds(g * HALF, HALF)], P),
                                            ALU.not_equal).then_inc(away_done, 1)

                regs = [dve.alloc_register(f"tile{n}_{nc.next_id()}") for n in range(HALF)]

                def maxima(g, h):
                    tiles = load_tiles(nc, dve, q, g * HALF, regs)
                    for four in range(0, HALF, 4):
                        for u in range(four, four + 4):
                            dve.wait_ge(listed, (g + 2) * HALF + u + 1)
                            nc.vector.tensor_reduce(top_p[:, h * HALF + u, :], all_ps[u % 4][:, :, :], AX.X, ALU.max).then_inc(used, 1)
                        hold(dve, go, used, g * HALF + four + 8)
                        for u in range(four, four + 4):
                            top_t = top[:, bass.ds(tiles[u], 1), u % 2, :].rearrange("p o s -> p (o s)")
                            dve.wait_ge(chain, g * HALF + u + 1)
                            nc.vector.tensor_tensor(top_t, top_t, top_p[:, h * HALF + u, :], ALU.max).then_inc(chain, 1)

                dve.sem_inc(used, 4)
                dve.sem_inc(chain, 2)
                nc.vector.tensor_reduce(pick[:, :, :], k.ident[0:HALF * S, 0:HALF * S].rearrange("p (v c j) -> p v j c", v=HALF, c=3),
                                        AX.X, ALU.max).then_inc(go, 1)
                nc.vector.tensor_scalar(far[:, :], k.ident_bf[:, :], -1e30, None, ALU.mult).then_inc(go, 1)
                dve.wait_ge(go, 2)
                mark(0, 0)
                with dve.Fori(0, turns - 1) as i:
                    for h in range(2):
                        mark(i * 2 + h + 1, 1 - h)
                        maxima(i * 2 + h, h)
                last = turns * 2 - 1
                mark(last, 1)
                maxima(last - 1, 0)
                maxima(last, 1)


def attend_self(nc, k, mine, target, top, parts, sums):
    W, T = HEADS * GEXP, TILES
    with Stage(nc) as s:
        own, best = s.sb("own", [P, T, HEADS], F32), s.sb("best", [P, T, HEADS], F32)
        score, part = s.sb("score", [P, BUCKETS, 2 * HEADS], F32), s.sb("part", [P, BUCKETS, 2 * HEADS], F32)
        chain, shifted, exped = (s.sem(n) for n in ("chain", "shifted", "exped"))
        with nc.Block() as block:
            @block.vector
            def _(dve):
                link = Chain(dve, chain)
                link(nc.vector.memset(score[:, T, :], 0.0))
                link(nc.vector.memset(sums[:, T, 0, :], 0.0))
                link(nc.vector.memset(sums[:, :, 1, :], 0.0))
                link(nc.vector.tensor_copy(score[:, 0:T, 0:HEADS], target[:, 0:T, :]))
                link(nc.vector.tensor_tensor(best[:, :, :], top[:, 0:T, 0, :], top[:, 0:T, 1, :], ALU.max))
                link(nc.vector.tensor_tensor(best[:, :, :], best[:, :, :], target[:, 0:T, :], ALU.add))
                link(nc.vector.scalar_tensor_tensor(score[:, 0:T, HEADS:2 * HEADS], best[:, :, :], 0.2, best[:, :, :], ALU.mult, ALU.max))
                link(nc.vector.tensor_tensor(own[:, :, :], mine[:, :, W:W + HEADS], target[:, 0:T, :], ALU.add))
                link(nc.vector.scalar_tensor_tensor(own[:, :, :], own[:, :, :], 0.2, own[:, :, :], ALU.mult, ALU.max))
                link(nc.vector.tensor_tensor(own[:, :, :], own[:, :, :], score[:, 0:T, HEADS:2 * HEADS], ALU.subtract))
                dve.sem_inc(shifted, 1)
                dve.wait_ge(exped, 1)
                link(nc.vector.tensor_copy(sums[:, 0:T, 0, W:W + HEADS], own[:, :, :]))
                for c in range(3):
                    link(nc.vector.tensor_copy(parts[:, :, c, :], score[:, :, :]))
                    if c < 2:
                        link(nc.vector.tensor_copy(part[:, :, :], parts[:, :, c, :]))
                        link(nc.vector.tensor_tensor(score[:, :, :], score[:, :, :], part[:, :, :], ALU.subtract))
                for j in range(HEADS):
                    link(nc.vector.tensor_tensor(sums[:, 0:T, 0, j * GEXP:(j + 1) * GEXP], mine[:, :, j * GEXP:(j + 1) * GEXP],
                                                 bc(own[:, :, j], GEXP), ALU.mult))

            @block.scalar
            def _(act):
                act.wait_ge(shifted, 1)
                nc.scalar.activation(own[:, :, :], own[:, :, :], ACT.Exp).then_inc(exped, 1)


def attend_sums(nc, k, q, fetched, parts, sums):
    count, body = GPAIRS // HALF, 4
    W = HEADS * GEXP
    with Stage(nc) as s:
        hot = s.sb("hot", [P, body, HALF, P], F32)
        hot_bf = s.sb("hot_bf", [P, 2, HALF, P], BF16)
        hot_t = s.sb("hot_t", [P, 2, HALF, P], BF16)
        z = s.sb("z", [P, 2, HALF, HEADS], F32)
        val = s.sb("val", [P, 2, HALF, W + HEADS], F32)
        hot_ps = [s.ps(f"hot_ps{n}", [P, HALF, P], BF16) for n in range(2)]
        score_ps = [s.ps(f"score_ps{h}", [P, HALF, 64]) for h in range(2)]
        sum_ps = [s.ps(f"sum_ps{h}", [P, HALF, 64]) for h in range(2)]
        go, hot_done, widened, turned, copied, scored, chain, shifted, exped, valued, summed, added = (s.sem(n) for n in (
            "go", "hot_done", "widened", "turned", "copied", "scored", "chain", "shifted", "exped", "valued", "summed", "added"))
        PER = 4

        def groups(eng, step):
            loops = (count - 2) // body
            for h in range(body):
                step(h, h, 2)
            with eng.Fori(1, loops) as i:
                for h in range(body):
                    step(i * body + h, h, 2)
            for g in range(loops * body, count):
                step(g, g % body, min(2, count - 1 - g))

        with nc.Block() as block:
            @block.vector
            def _(dve):
                def front(g, h, again):
                    if again:
                        hold(dve, go, widened, g - 1)
                    for u in range(0, HALF, 2):
                        yield nc.vector.tensor_tensor(hot_bf[:, h % 2, u:u + 2, :], bc(k.iota[:, :], 2, 1), bc(q.place[:, bass.ds(g * HALF + u, 2)], P),
                                                      ALU.is_equal).then_inc(hot_done, 1)

                regs = [dve.alloc_register(f"tile{n}_{nc.next_id()}") for n in range(HALF)]

                def back(g, h):
                    tiles = load_tiles(nc, dve, q, g * HALF, regs)
                    for u in range(HALF):
                        sum_t = sums[:, bass.ds(tiles[u], 1), u % 2, :].rearrange("p o w -> p (o w)")
                        if u == 0:
                            hold(dve, go, summed, g + 1)
                        dve.wait_ge(added, (g + 1) * HALF + u + 1)
                        nc.vector.tensor_tensor(sum_t, sum_t, sum_ps[h % 2][:, u, 0:W + HEADS], ALU.add).then_inc(added, 1)

                def step(g, h, ahead):
                    edges = fetched[:, bass.ds(g * HALF, HALF), :]
                    hold(dve, go, scored, g + 1)
                    zh, got = z[:, h % 2, :, :], score_ps[h % 2]
                    z_steps = [
                        lambda: nc.vector.tensor_tensor(zh, edges[:, :, W:W + HEADS], got[:, :, 0:HEADS], ALU.add),
                        lambda: nc.vector.scalar_tensor_tensor(zh, zh, 0.2, zh, ALU.mult, ALU.max),
                        lambda: nc.vector.tensor_tensor(zh, zh, got[:, :, HEADS:2 * HEADS], ALU.subtract),
                        lambda: nc.vector.tensor_scalar(zh, zh, 0.0, None, ALU.min)]
                    pieces = front(g + 2, (h + 2) % body, True) if ahead == 2 else iter(())
                    for n, z_step in enumerate(z_steps):
                        if n:
                            hold(dve, go, chain, g * PER + n)
                        z_step().then_inc(chain, 1)
                        next(pieces, None)
                    hold(dve, go, chain, g * PER + 4)
                    dve.sem_inc(shifted, 1)
                    if not isinstance(g, int) or g >= 2:
                        back(g - 2, (h - 2) % body)
                    hold(dve, go, exped, g + 1)
                    v = val[:, h % 2, :, :]
                    for j in range(HEADS):
                        nc.vector.tensor_tensor(v[:, :, j * GEXP:(j + 1) * GEXP], edges[:, :, j * GEXP:(j + 1) * GEXP],
                                                bc(v[:, :, W + j], GEXP), ALU.mult).then_inc(valued, 1)

                dve.sem_inc(added, HALF + 2)
                dve.sem_inc(go, 1)
                for g in range(2):
                    for _ in front(g, g, False):
                        pass
                groups(dve, step)
                for g in (count - 2, count - 1):
                    back(g, g % body)

            @block.scalar
            def _(act):
                def copy(g, h):
                    act.wait_ge(turned, g + 1)
                    nc.scalar.activation(hot_t[:, h % 2, :, :], hot_ps[h % 2][:, :, :], ACT.Copy).then_inc(copied, 1)
                    act.wait_ge(hot_done, (g + 1) * HALF // 2)
                    nc.scalar.activation(hot[:, h, :, :], hot_bf[:, h % 2, :, :], ACT.Copy).then_inc(widened, 1)

                def step(g, h, ahead):
                    if not isinstance(g, int) or g >= 2:
                        hold(act, go, summed, g - 1)
                    act.wait_ge(shifted, g + 1)
                    nc.scalar.activation(val[:, h % 2, :, W:W + HEADS], z[:, h % 2, :, :], ACT.Exp).then_inc(exped, 1)
                    if ahead == 2:
                        copy(g + 2, (h + 2) % body)

                act.wait_ge(go, 1)
                copy(0, 0)
                copy(1, 1)
                groups(act, step)

            @block.tensor
            def _(pe):
                regs = [pe.alloc_register(f"tile{n}_{nc.next_id()}") for n in range(HALF)]

                def turn(g, h):
                    pe.wait_ge(hot_done, (g + 1) * HALF // 2)
                    for u in range(HALF):
                        ins = nc.tensor.transpose(hot_ps[h % 2][:, u, :], hot_bf[:, h % 2, u, :], k.ident_bf[:, :])
                    ins.then_inc(turned, 1)

                def spread_scores(g, h):
                    tiles = load_tiles(nc, pe, q, g * HALF, regs)
                    pe.wait_ge(copied, g + 1)
                    for u in range(HALF):
                        for c in range(3):
                            ins = nc.tensor.matmul(score_ps[h % 2][:, u, 0:2 * HEADS], hot_t[:, h % 2, u, :],
                                                   parts[:, bass.ds(tiles[u], 1), c, :].rearrange("p o w -> p (o w)"), start=c == 0, stop=c == 2)
                    ins.then_inc(scored, 1)

                def step(g, h, ahead):
                    if ahead:
                        spread_scores(g + 1, (h + 1) % body)
                    if ahead == 2:
                        turn(g + 2, (h + 2) % body)
                    pe.wait_ge(widened, g + 1)
                    pe.wait_ge(valued, g * HEADS + HEADS)
                    pe.wait_ge(added, g * HALF + 2)
                    for u in range(HALF):
                        ins = nc.tensor.matmul(sum_ps[h % 2][:, u, 0:W + HEADS], hot[:, h, u, :], val[:, h % 2, u, :], start=True, stop=True)
                    ins.then_inc(summed, 1)

                pe.wait_ge(go, 1)
                turn(0, 0)
                spread_scores(0, 0)
                turn(1, 1)
                groups(pe, step)


def attention_gates(nc, k, a, sums, gate):
    W, T, E = HEADS * GEXP, TILES, GEXP
    with Stage(nc) as s:
        v, sq = s.sb("v", [P, T, W], F32), s.sb("sq", [P, T, W], F32)
        rec = s.sb("rec", [P, T, HEADS], F32)
        row = [s.sb(f"row{n}", [P, W], F32) for n in range(3)]
        m1, m2, b, var = (s.sb(n, [P, T], F32) for n in ("m1", "m2", "b", "var"))
        sc, hot1, hot2, pick = (s.sb(n, [P, T, E], F32) for n in ("sc", "hot1", "hot2", "pick"))
        order = s.sb("order", [P, E], F32)
        loaded, chain, var_done, std_done, gap_done, exped = (s.sem(n) for n in (
            "loaded", "chain", "var_done", "std_done", "gap_done", "exped"))
        with nc.Block() as block:
            @block.sync
            def _(sp):
                for r, name in zip(row, ("L1_ffn_b_gat", "L1_ffn_ln_gamma", "L1_ffn_ln_beta")):
                    sp.dma_start(r[:, :], a[name].unsqueeze(0).to_broadcast([P, W])).then_inc(loaded, 16)

            @block.scalar
            def _(act):
                act.wait_ge(var_done, 1)
                nc.scalar.activation(var[:, :], var[:, :], ACT.Sqrt, bias=k.eps[:, :]).then_inc(std_done, 1)
                act.wait_ge(gap_done, 1)
                nc.scalar.activation(b[:, :], m2[:, :], ACT.Exp).then_inc(exped, 1)

            @block.vector
            def _(dve):
                link = Chain(dve, chain)
                dve.wait_ge(loaded, 48)
                total = sums[:, 0:T, 0, :]
                link(nc.vector.tensor_tensor(total, total, sums[:, 0:T, 1, :], ALU.add))
                link(nc.vector.tensor_scalar(rec[:, :, :], total[:, :, W:W + HEADS], 1e-16, None, ALU.add))
                link(nc.vector.reciprocal(rec[:, :, :], rec[:, :, :]))
                for j in range(HEADS):
                    link(nc.vector.tensor_tensor(v[:, :, j * E:(j + 1) * E], total[:, :, j * E:(j + 1) * E], bc(rec[:, :, j], E), ALU.mult))
                link(nc.vector.tensor_tensor(v[:, :, :], v[:, :, :], bc(row[0][:, :], T, 1), ALU.add))
                link(nc.vector.tensor_reduce(m1[:, :], v[:, :, :], AX.X, ALU.add))
                link(nc.vector.tensor_scalar(m1[:, :], m1[:, :], 1.0 / W, None, ALU.mult))
                link(nc.vector.tensor_tensor(v[:, :, :], v[:, :, :], bc(m1[:, :], W), ALU.subtract))
                link(nc.vector.tensor_tensor(sq[:, :, :], v[:, :, :], v[:, :, :], ALU.mult))
                link(nc.vector.tensor_reduce(var[:, :], sq[:, :, :], AX.X, ALU.add))
                link(nc.vector.tensor_scalar(var[:, :], var[:, :], 1.0 / W, None, ALU.mult))
                dve.sem_inc(var_done, 1)
                dve.wait_ge(std_done, 1)
                link(nc.vector.reciprocal(var[:, :], var[:, :]))
                link(nc.vector.tensor_tensor(v[:, :, :], v[:, :, :], bc(var[:, :], W), ALU.mult))
                link(nc.vector.tensor_tensor(v[:, :, :], v[:, :, :], bc(row[1][:, :], T, 1), ALU.mult))
                link(nc.vector.tensor_tensor(v[:, :, :], v[:, :, :], bc(row[2][:, :], T, 1), ALU.add))
                link(nc.vector.tensor_reduce(sc[:, :, :], v[:, :, :].rearrange("p t (h e) -> p t e h", h=HEADS), AX.X, ALU.add))
                link(nc.vector.tensor_scalar(sc[:, :, :], sc[:, :, :], 1.0 / HEADS, None, ALU.mult))
                link(nc.vector.tensor_scalar(order[:, :], k.iota[:, 0:E], -1.0, float(E), ALU.mult, ALU.add))
                for m, hot in ((m1, hot1), (m2, hot2)):
                    link(nc.vector.tensor_reduce(m[:, :], sc[:, :, :], AX.X, ALU.max))
                    link(nc.vector.tensor_tensor(pick[:, :, :], sc[:, :, :], bc(m[:, :], E), ALU.is_equal))
                    link(nc.vector.tensor_tensor(pick[:, :, :], pick[:, :, :], bc(order[:, :], T, 1), ALU.mult))
                    link(nc.vector.tensor_reduce(b[:, :], pick[:, :, :], AX.X, ALU.max))
                    link(nc.vector.tensor_tensor(hot[:, :, :], pick[:, :, :], bc(b[:, :], E), ALU.is_equal))
                    if m is m1:
                        link(nc.vector.scalar_tensor_tensor(sc[:, :, :], hot[:, :, :], -1e30, sc[:, :, :], ALU.mult, ALU.add))
                link(nc.vector.tensor_tensor(m2[:, :], m2[:, :], m1[:, :], ALU.subtract))
                dve.sem_inc(gap_done, 1)
                dve.wait_ge(exped, 1)
                link(nc.vector.tensor_scalar(m1[:, :], b[:, :], 1.0, None, ALU.add))
                link(nc.vector.reciprocal(m1[:, :], m1[:, :]))
                link(nc.vector.tensor_tensor(b[:, :], b[:, :], m1[:, :], ALU.mult))
                link(nc.vector.tensor_tensor(hot1[:, :, :], hot1[:, :, :], bc(m1[:, :], E), ALU.mult))
                link(nc.vector.tensor_tensor(hot2[:, :, :], hot2[:, :, :], bc(b[:, :], E), ALU.mult))
                link(nc.vector.tensor_tensor(gate[:, :, :], hot1[:, :, :], hot2[:, :, :], ALU.add))


def run_gated_experts(nc, k, a, x_old, f, gate, out):
    FC, W = GHID // P, GROUP * P // 2
    view = lambda v: v[0:NPAD, :].rearrange("(g j p) d -> g p j d", j=GROUP, p=P)
    at = lambda v, g: v[bass.ds(g, 1), :, :, :].rearrange("o p j d -> (o p) j d")
    xo, fv, ov = view(x_old), view(f), view(out)
    turns = GROUPS // 2
    with Stage(nc) as s:
        w1 = s.sb("w1", [P, GEXP, 2, GHID], F32)
        w2 = s.sb("w2", [P, GEXP, FC, D], F32)
        b1 = s.sb("b1", [P, GEXP, FC], F32)
        b2 = s.sb("b2", [P, GEXP, D], F32)
        x = [s.sb(f"x{h}", [P, GROUP, D], F32) for h in range(2)]
        fin = [s.sb(f"fin{h}", [P, GROUP, D], F32) for h in range(2)]
        ft = [s.sb(f"ft{h}", [P, 2, GROUP * P], F32) for h in range(2)]
        hid = [s.sb(f"hid{n}", [P, FC, GROUP * P], F32) for n in range(2)]
        ft_ps = [s.ps(f"ft_ps{n}", [P, 2, P]) for n in range(2)]
        hid_ps = [s.ps(f"hid_ps{n}", [P, 512]) for n in range(HB)]
        y_ps = [s.ps(f"y_ps{n}", [P, 512]) for n in range(YB)]
        go, weights, turned, copied, hid_mult, hid_done, y_mult, y_done, x_done, chain = (s.sem(n) for n in (
            "go", "weights", "turned", "copied", "hid_mult", "hid_done", "y_mult", "y_done", "x_done", "chain"))
        x_loaded, f_loaded, stored = ([s.sem(f"{n}{h}") for h in range(2)] for n in ("x_loaded", "f_loaded", "stored"))
        NH, NY, NT = GEXP * FC * 2, GEXP * GROUP, GROUP
        with nc.Block() as block:
            @block.sync
            def _(sp):
                sp.sem_inc(go, 1)
                for e in range(GEXP):
                    sp.dma_start(w1[:, e, :, :], a["L1_ffn_W1"][e, :, :].rearrange("(c p) f -> p c f", p=P)).then_inc(weights, 16)
                    sp.dma_start(w2[:, e, :, :], a["L1_ffn_W2"][e, :, :].rearrange("(c p) d -> p c d", p=P)).then_inc(weights, 16)
                    sp.dma_start(b1[:, e, :], a["L1_ffn_b1"][e, :].rearrange("(c p) -> p c", p=P), allow_slow_non_contiguous=True).then_inc(weights, 16)
                    sp.dma_start(b2[:, e, :], a["L1_ffn_b2"][e:e + 1, :].to_broadcast([P, D])).then_inc(weights, 16)

                def turn(i, again):
                    for h in range(2):
                        if again:
                            hold(sp, go, turned, (i * 2 + h - 1) * NT)
                        sp.dma_start(fin[h][:, :, :], at(fv, i * 2 + h)).then_inc(f_loaded[h], 16)
                        if again:
                            hold(sp, go, stored[h], i * 16)
                        sp.dma_start(x[h][:, :, :], at(xo, i * 2 + h)).then_inc(x_loaded[h], 16)

                turn(0, False)
                with sp.Fori(1, turns) as i:
                    turn(i, True)

            @block.gpsimd
            def _(pool):
                pool.wait_ge(go, 1)
                with pool.Fori(0, turns) as i:
                    for h in range(2):
                        hold(pool, go, x_done, i * 2 + h + 1)
                        pool.dma_start(at(ov, i * 2 + h), x[h][:, :, :]).then_inc(stored[h], 16)
                for h in range(2):
                    pool.wait_ge(stored[h], 16 * turns)

            @block.tensor
            def _(pe):
                pe.wait_ge(weights, 64 * GEXP)
                pe.wait_ge(go, 1)
                with pe.Fori(0, turns) as i:
                    for h in range(2):
                        nh, ny, nt = (i * 2 + h) * NH, (i * 2 + h) * NY, (i * 2 + h) * NT
                        pe.wait_ge(f_loaded[h], i * 16 + 16)
                        for j in range(GROUP):
                            pe.wait_ge(copied, nt + j + 1)
                            for c in range(2):
                                ins = nc.tensor.transpose(ft_ps[(h * GROUP + j) % 2][:, c, :], fin[h][:, j, c * P:(c + 1) * P], k.ident[:, :])
                            ins.then_inc(turned, 1)
                        pe.wait_ge(copied, nt + NT + 2)
                        for e in range(GEXP):
                            for c in range(FC):
                                for r in range(2):
                                    n = e * FC * 2 + c * 2 + r
                                    pe.wait_ge(hid_done, nh + n + 1)
                                    bank = hid_ps[(h * NH + n) % HB][:, 0:W]
                                    for d in range(2):
                                        ins = nc.tensor.matmul(bank, w1[:, e, d, c * P:(c + 1) * P], ft[h][:, d, r * W:(r + 1) * W], start=d == 0, stop=d == 1)
                                    ins.then_inc(hid_mult, 1)
                            for j in range(GROUP):
                                n = e * GROUP + j
                                pe.wait_ge(y_done, ny + n + 1)
                                if j == 0:
                                    pe.wait_ge(hid_done, nh + (e + 1) * FC * 2 + HB)
                                for c in range(FC):
                                    ins = nc.tensor.matmul(y_ps[(h * NY + n) % YB][:, 0:D], hid[e % 2][:, c, j * P:(j + 1) * P], w2[:, e, c, :],
                                                           start=c == 0, stop=c == FC - 1)
                                ins.then_inc(y_mult, 1)

            @block.scalar
            def _(act):
                act.sem_inc(hid_done, HB)
                act.wait_ge(weights, 64 * GEXP)
                act.wait_ge(go, 1)
                with act.Fori(0, turns) as i:
                    for h in range(2):
                        nh, ny = (i * 2 + h) * NH, (i * 2 + h) * NY
                        for e in range(GEXP):
                            for c in range(FC):
                                for r in range(2):
                                    n = e * FC * 2 + c * 2 + r
                                    act.wait_ge(hid_mult, nh + n + 1)
                                    nc.scalar.activation(hid[e % 2][:, c, r * W:(r + 1) * W], hid_ps[(h * NH + n) % HB][:, 0:W], ACT.Gelu,
                                                         bias=b1[:, e, c:c + 1]).then_inc(hid_done, 1)

            @block.vector
            def _(dve):
                dve.sem_inc(copied, 2)
                dve.sem_inc(y_done, YB)
                dve.wait_ge(weights, 64 * GEXP)
                dve.wait_ge(go, 1)
                with dve.Fori(0, turns) as i:
                    PER = 2 * GROUP * 2 * GEXP
                    link = Chain(dve, chain, i * PER, go)
                    for h in range(2):
                        ny, nt = (i * 2 + h) * NY, (i * 2 + h) * NT
                        for j in range(GROUP):
                            dve.wait_ge(turned, nt + j + 1)
                            nc.vector.tensor_copy(ft[h][:, :, j * P:(j + 1) * P], ft_ps[(h * GROUP + j) % 2][:, :, :]).then_inc(copied, 1)
                        hold(dve, go, x_loaded[h], i * 16 + 16)
                        for e in range(GEXP):
                            for j in range(GROUP):
                                g = gate[:, bass.ds((i * 2 + h) * GROUP + j, 1), e:e + 1].rearrange("p o e -> p (o e)")
                                link(nc.vector.scalar_tensor_tensor(x[h][:, j, :], b2[:, e, :], g, x[h][:, j, :], ALU.mult, ALU.add))
                            for j in range(GROUP):
                                n = e * GROUP + j
                                g = gate[:, bass.ds((i * 2 + h) * GROUP + j, 1), e:e + 1].rearrange("p o e -> p (o e)")
                                hold(dve, go, y_mult, ny + n + 1)
                                link(nc.vector.scalar_tensor_tensor(x[h][:, j, :], y_ps[(h * NY + n) % YB][:, 0:D], g, x[h][:, j, :], ALU.mult, ALU.add))
                                dve.sem_inc(y_done, 1)
                        dve.sem_inc(x_done, 1)
                    assert link.n == PER


HB, YB = 4, 2


def start_maxima(nc, k, mine, top):
    with Stage(nc) as s, nc.Block() as block:
        done = s.sem("done")

        @block.vector
        def _(dve):
            own = mine[:, :, HEADS * GEXP:HEADS * GEXP + HEADS]
            for n in range(2):
                nc.vector.tensor_copy(top[:, 0:TILES, n, :], own).then_inc(done, 1)
            nc.vector.memset(top[:, TILES, :, :], 0.0).then_inc(done, 1)


def pair_buffers(s, blocks):
    return Pairs(row=s.sb("row", [P, blocks * P], I32), place=s.sb("place", [P, blocks * P], F32),
                           weight=s.sb("weight", [P, blocks * P], F32), tile=s.sb("tile", [1, blocks * P], I32))


def program(nc, a, out, scratch):
    with ExitStack() as ctx:
        k = Kept()

        def const(name, shape, dt):
            return ctx.enter_context(nc.sbuf_tensor(name, shape, dt))

        k.iota_i = const("iota_i", [P, P], I32)
        k.iota = const("iota", [P, P], F32)
        k.ones = const("ones", [P, P], F32)
        k.ident = const("ident", [P, P], F32)
        k.ident_bf = const("ident_bf", [P, P], BF16)
        k.before = const("before", [P, P], F32)
        k.qcol_i = const("qcol_i", [P, EBLK], I32)
        k.qcol = const("qcol", [P, EBLK], F32)
        k.zero = const("zero", [P, D], F32)
        k.eps = const("eps", [P, 1], F32)
        constants(nc, k)
        f0 = scratch("f0", [NPAD + P, D], F32)
        layer_norm_in(nc, k, a["x"], f0)

        def plan(name, pairs, blocks, chunks):
            return Plan(pairs, blocks, chunks, scratch(f"tiles_{name}", [blocks * P], I32),
                        const(f"chunk_{name}", [P, blocks], I32), const(f"shift_{name}", [P, blocks], F32))

        plans = [plan("a", EPAIRS, EBLK, ECH), plan("e", EPAIRS, EBLK, ECH), plan("g", GPAIRS, GBLK, GCH)]
        sorted_e, sorted_g = scratch("sorted_e", [ECH * P, 3], F32), scratch("sorted_g", [GCH * P, 2], F32)
        xbuf, ybuf = scratch("xbuf", [EXPERTS * SLOTS, D], F32), scratch("ybuf", [EXPERTS * SLOTS, D], F32)
        rec_g_kept, pos_g_kept = scratch("rec_g_kept", [P, GCH, 2], F32), scratch("pos_g_kept", [P, GCH], I32)
        e_split, g_split = (0, 42, ECH // LANES), (0, 24, 45, 51, GCH // LANES)
        by_target = Fields(rows=[a["dst"], a["src"], a["w"]], fields=[(0, 0, 1), (1, 0, 1), (2, 0, 1)])
        by_source = Fields(rows=[sorted_e.rearrange("(c e) f -> c (e f)", e=P)], fields=[(0, 1, 3), (0, 0, 3), (0, 2, 3)])
        k.w0t = const("w0t", [P, 2, D], F32)
        k.b0 = const("b0", [1, D], F32)
        k.gate_w = const("gate_w", [P, 2, EXPERTS], F32)
        k.gate_b = const("gate_b", [1, EXPERTS], F32)
        k.w1g = const("w1g", [P, 2, D], F32)
        k.big = const("big", [P, 1], F32)
        k.small = const("small", [P, 1], F32)
        k.send = const("send", [P, TILES], I32)
        k.fetch = const("fetch", [P, TILES], I32)
        k.scale = const("scale", [P, TILES], F32)
        with Stage(nc) as kept:
            rec_e, pos_e = kept.sb("rec_e", [P, ECH, 3], F32), kept.sb("pos_e", [P, ECH], I32)
            scatter_e = lambda n: Scatter(rec_e, pos_e, sorted_e, 3, e_split[n], e_split[n + 1] - e_split[n])
            with Stage(nc) as s:
                rec_g, pos_g = s.sb("rec_g", [P, GCH, 2], F32), s.sb("pos_g", [P, GCH], I32)
                edge_ranks(nc, k, a, plans, rec_e, rec_g, pos_e, pos_g, xbuf, Scatter(rec_g, pos_g, sorted_g, 2, 0, g_split[1]))
                load_small(nc, k, [(rec_g_kept, rec_g[:, :, :]), (pos_g_kept, pos_g[:, :])])
            turn_weights(nc, k, [(a["L0_gnn_W"], k.w0t)])
            row = lambda v: v.unsqueeze(0)
            halves = lambda v: v.rearrange("(c p) o -> p c o", p=P)
            load_small(nc, k, [(k.b0[:, :], row(a["L0_gnn_b"])), (k.gate_w[:, :, :], halves(a["L0_ffn_gate_w"])),
                               (k.gate_b[:, :], row(a["L0_ffn_gate_b"])), (k.w1g[:, :, :], halves(a["L1_gnn_W"]))])
            x1, x2 = scratch("x1", [NPAD, D], F32), scratch("x2", [NPAD, D], F32)
            f1 = scratch("f1", [NPAD, D], F32)
            with Stage(nc) as s:
                agg = s.sb("agg", [P, BUCKETS, D], F32)
                with Stage(nc) as s2:
                    q = pair_buffers(s2, EBLK)
                    pair_arrays(nc, k, plans[0], q, by_target)
                    aggregate_edges(nc, k, f0, q, agg)
                with Stage(nc) as s2:
                    logits = s2.sb("logits", [P, TILES, EXPERTS], F32)
                    update_nodes(nc, k, Product(kind="product", sums=agg, w=k.w0t, bias=k.b0[:, :]), a["x"], x1, f1,
                                 k.gate_w, EXPERTS, k.gate_b[:, :], logits, scatter_e(0))
                    route_tokens(nc, k, logits, k.send, k.fetch, k.scale)
            dispatch_tokens(nc, k, f1, k.send, xbuf)
            run_experts(nc, k, xbuf, a["L0_ffn_w1"], a["L0_ffn_b1"], a["L0_ffn_w2"], a["L0_ffn_b2"], ybuf, scatter_e(1))
        rec_g, pos_g = const("rec_g", [P, GCH, 2], F32), const("pos_g", [P, GCH], I32)
        load_small(nc, k, [(rec_g[:, :, :], rec_g_kept), (pos_g[:, :], pos_g_kept)])
        scatter_g = lambda n: Scatter(rec_g, pos_g, sorted_g, 2, g_split[n], g_split[n + 1] - g_split[n])
        h1 = scratch("h1", [NPAD + P, D], F32)
        load_small(nc, k, [(h1[NPAD:NPAD + P, :], k.zero[:, :])])
        update_nodes(nc, k, Routed(kind="experts", table=ybuf, rows=k.fetch, scale=k.scale), x1, x2, None,
                     k.w1g, D, None, h1, scatter_g(1))
        W = HEADS * GEXP
        k.gat_w = const("gat_w", [P, 2, W], F32)
        k.gate = const("gate", [P, TILES, GEXP], F32)
        load_small(nc, k, [(k.gat_w[:, :, :], halves(a["L1_ffn_W_gat"]))])
        x3, f3 = scratch("x3", [NPAD, D], F32), scratch("f3", [NPAD, D], F32)
        with Stage(nc) as s0:
            heads = s0.sb("heads", [P, TILES, W], F32)
            with Stage(nc) as s:
                agg = s.sb("agg1", [P, BUCKETS, D], F32)
                with Stage(nc) as s2:
                    q = pair_buffers(s2, EBLK)
                    pair_arrays(nc, k, plans[1], q, by_source)
                    aggregate_edges(nc, k, h1, q, agg)
                with Stage(nc) as s2:
                    gain, offset = s2.sb("gain", [P, D], F32), s2.sb("offset", [P, D], F32)
                    node_statistics(nc, k, agg, gain, offset, (a["L1_gnn_bias"], a["L1_gnn_gamma"], a["L1_gnn_beta"]), scatter_g(2))
                    update_nodes(nc, k, Normed(kind="batch_norm", sums=agg, gain=gain, offset=offset), x2, x3, f3,
                                 k.gat_w, W, None, heads, scatter_g(3))
            with Stage(nc) as s:
                table = scratch("gat", [NPAD, W + 4 * HEADS], F32)
                mine, target = s.sb("mine", [P, TILES, W + 4 * HEADS], F32), s.sb("target", [P, BUCKETS, HEADS], F32)
                top, parts = s.sb("top", [P, BUCKETS, 2, HEADS], F32), s.sb("parts", [P, BUCKETS, 3, 2 * HEADS], BF16)
                sums = s.sb("sums", [P, BUCKETS, 2, W + HEADS], F32)
                attention_table(nc, k, a, heads, mine, target, table)
                with Stage(nc) as s2:
                    q = pair_buffers(s2, GBLK)
                    fetched = s2.sb("fetched", [P, GPAIRS, W + HEADS], F32)
                    pair_arrays(nc, k, plans[2], q, Fields(rows=[sorted_g.rearrange("(c e) f -> c (e f)", e=P)],
                                                                     fields=[(0, 1, 2), (0, 0, 2)]))
                    start_maxima(nc, k, mine, top)
                    attend_maxima(nc, k, q, table, fetched, top)
                    attend_self(nc, k, mine, target, top, parts, sums)
                    attend_sums(nc, k, q, fetched, parts, sums)
                attention_gates(nc, k, a, sums, k.gate)
        run_gated_experts(nc, k, a, x3, f3, k.gate, out)


def kernel(**inputs):
    import numpy as np
    import concourse.bacc as bacc
    from concourse.bass_utils import run_bass_kernel_spmd

    def rows(name, n_rows, fill):
        v = np.ascontiguousarray(inputs[name]).reshape(-1)
        full = np.full(n_rows * P, fill, v.dtype)
        full[:v.size] = v
        return full.reshape(n_rows, P)

    nc = bacc.Bacc("TRN2", target_bir_lowering=False, num_devices=1)
    arrays = {}
    x = np.ascontiguousarray(inputs["x"])
    arrays["x"] = np.concatenate([x, np.zeros((NPAD - N, D), x.dtype)])
    arrays["src"] = rows("src", EROWS, NPAD)
    arrays["dst"] = rows("dst", EROWS, NPAD)
    arrays["w"] = rows("edge_weight", EROWS, 0)
    ge = np.ascontiguousarray(inputs["L1_ffn_edge_index"])
    arrays["gsrc"], arrays["gdst"] = ge[0].reshape(GCH, P), ge[1].reshape(GCH, P)
    for name in inputs:
        if name.startswith("L") and name != "L1_ffn_edge_index":
            arrays[name] = np.ascontiguousarray(inputs[name])
    a = {n: nc.dram_tensor(f"in_{n}", v.shape, mybir.dt.from_np(v.dtype), kind="ExternalInput").ap() for n, v in arrays.items()}
    out = nc.dram_tensor("out_x", (NPAD, D), F32, kind="ExternalOutput").ap()

    def scratch(name, shape, dt):
        return nc.dram_tensor(name, shape, dt, kind="Internal").ap()

    program(nc, a, out, scratch)
    r = run_bass_kernel_spmd(nc, [{f"in_{n}": v for n, v in arrays.items()}], core_ids=[0])
    return np.ascontiguousarray(r.results[0]["out_x"])[:N]
```
